# Optimizing a Trainium2 kernel written in Bass

```python
import numpy as np
import jax
import jax.numpy as jnp

def _softmax(x, axis=-1):
    return jax.nn.softmax(x, axis=axis)

def _gelu(x):
    return jax.nn.gelu(x, approximate=True)

def _silu(x):
    return jax.nn.silu(x)

def _sigmoid(x):
    return jax.nn.sigmoid(x)

def _layernorm(x, axis=-1, eps=1e-05):
    m = jnp.mean(x, axis=axis, keepdims=True)
    v = jnp.var(x, axis=axis, keepdims=True)
    return (x - m) / jnp.sqrt(v + eps)

def _scatter_add(tgt, idx, src, axis=0):
    return tgt.at[idx].add(src)

def _segment_sum(src, seg, n):
    return jax.ops.segment_sum(src, seg, n)
kernel_name = 'mk_seq_preln_d1_jaxref_r4_4c0f5b'

def setup_inputs(seed: int=0):
    np.random.seed(seed)
    _w = jnp.asarray

    def _L0_attn_setup():
        import jax, jax.numpy as jnp
        import numpy as np
        B, N, E, H = (2, 512, 256, 16)
        D = E // H
        EPS = 1e-05
        SCALE = D ** (-0.5)
        STD = 0.02
        key = jax.random.key(seed)
        ks = jax.random.split(key, 10)
        rn = lambda k, shape: jax.random.normal(k, shape, dtype=jnp.float32)
        x = rn(ks[0], (B, N, E))
        Wq = rn(ks[1], (E, E)) * STD
        Wk = rn(ks[2], (E, E)) * STD
        Wv = rn(ks[3], (E, E)) * STD
        Wo = rn(ks[4], (E, E)) * STD
        Wf1 = rn(ks[5], (E, D)) * STD
        Wf2 = rn(ks[6], (D, E)) * STD
        Wg1 = rn(ks[7], (E, D)) * STD
        Wg2 = rn(ks[8], (D, E)) * STD
        norm_weight = jnp.ones((E,), dtype=jnp.float32)
        return dict(x=x, Wq=Wq, Wk=Wk, Wv=Wv, Wo=Wo, Wf1=Wf1, Wf2=Wf2, Wg1=Wg1, Wg2=Wg2, norm_weight=norm_weight)
    _L0_attn_in = _L0_attn_setup()

    def _L0_ffn_setup():
        import jax, jax.numpy as jnp
        import numpy as np
        H = 8
        KD = 128
        TOPK = 8
        NUM_KEYS = 64
        N_EXPERTS = NUM_KEYS * NUM_KEYS
        N_DIM = 256
        BN_EPS = 1e-05

        def gelu_new(x):
            c = jnp.sqrt(jnp.asarray(2.0 / jnp.pi, x.dtype))
            return 0.5 * x * (1.0 + jnp.tanh(c * (x + 0.044715 * x * x * x)))
        key = jax.random.key(seed)
        ks = jax.random.split(key, 5)
        b, s = (2, 256)
        x = jax.random.normal(ks[0], (b, s, N_DIM), dtype=jnp.float32)
        w_q = jax.random.normal(ks[1], (N_DIM, 2 * H * KD), dtype=jnp.float32) * 0.02
        bn_gamma = jnp.ones((2 * H * KD,), dtype=jnp.float32)
        bn_beta = jnp.zeros((2 * H * KD,), dtype=jnp.float32)
        keys = jax.random.normal(ks[2], (H, NUM_KEYS, 2, KD), dtype=jnp.float32) * 0.02
        down_embed = jax.random.normal(ks[3], (N_EXPERTS, N_DIM), dtype=jnp.float32) * 0.02
        up_embed = jax.random.normal(ks[4], (N_EXPERTS, N_DIM), dtype=jnp.float32) * 0.02
        return {'x': x, 'w_q': w_q, 'bn_gamma': bn_gamma, 'bn_beta': bn_beta, 'keys': keys, 'down_embed': down_embed, 'up_embed': up_embed}
    _L0_ffn_in = _L0_ffn_setup()
    _d = {'L0_attn_x': _L0_attn_in['x'], 'L0_attn_Wq': _L0_attn_in['Wq'], 'L0_attn_Wk': _L0_attn_in['Wk'], 'L0_attn_Wv': _L0_attn_in['Wv'], 'L0_attn_Wo': _L0_attn_in['Wo'], 'L0_attn_Wf1': _L0_attn_in['Wf1'], 'L0_attn_Wf2': _L0_attn_in['Wf2'], 'L0_attn_Wg1': _L0_attn_in['Wg1'], 'L0_attn_Wg2': _L0_attn_in['Wg2'], 'L0_attn_norm_weight': _L0_attn_in['norm_weight'], 'L0_ffn_w_q': _L0_ffn_in['w_q'], 'L0_ffn_bn_gamma': _L0_ffn_in['bn_gamma'], 'L0_ffn_bn_beta': _L0_ffn_in['bn_beta'], 'L0_ffn_keys': _L0_ffn_in['keys'], 'L0_ffn_down_embed': _L0_ffn_in['down_embed'], 'L0_ffn_up_embed': _L0_ffn_in['up_embed']}
    _x0 = _d['L0_attn_x']
    _d['L0_attn_x'] = jax.random.normal(jax.random.fold_in(jax.random.key(seed), 1), (2, 4096, 256), dtype=_x0.dtype)
    del _x0
    return _d

def reference(L0_attn_x, L0_attn_Wq, L0_attn_Wk, L0_attn_Wv, L0_attn_Wo, L0_attn_Wf1, L0_attn_Wf2, L0_attn_Wg1, L0_attn_Wg2, L0_attn_norm_weight, L0_ffn_w_q, L0_ffn_bn_gamma, L0_ffn_bn_beta, L0_ffn_keys, L0_ffn_down_embed, L0_ffn_up_embed):

    def _L0_attn_ref(x, Wq, Wk, Wv, Wo, Wf1, Wf2, Wg1, Wg2, norm_weight):
        import jax, jax.numpy as jnp
        import numpy as np
        B, N, E, H = (2, 512, 256, 16)
        D = E // H
        EPS = 1e-05
        SCALE = D ** (-0.5)
        STD = 0.02
        b, n, e = x.shape
        q = jax.nn.silu(x @ Wq).reshape(b, n, H, D)
        k = jax.nn.silu(x @ Wk).reshape(b, n, H, D)
        v = (x @ Wv).reshape(b, n, H, D)
        f = jax.nn.sigmoid(x @ Wf1 @ Wf2).reshape(b, n, H, D)

        def step(S, qkvf):
            qt, kt, vt, ft = qkvf
            S = ft[..., :, None] * S + kt[..., :, None] * vt[..., None, :]
            ot = jnp.einsum('bhk,bhkv->bhv', qt, S)
            return (S, ot)
        S0 = jnp.zeros((b, H, D, D), x.dtype)
        xs = (jnp.moveaxis(q, 1, 0) * SCALE, jnp.moveaxis(k, 1, 0), jnp.moveaxis(v, 1, 0), jnp.moveaxis(f, 1, 0))
        _, o = jax.lax.scan(step, S0, xs)
        o = jnp.moveaxis(o, 0, 1).reshape(b, n, e)
        g = jax.nn.sigmoid(x @ Wg1 @ Wg2)
        og = (o * g).reshape(b, n, H, D)
        og = og * jax.lax.rsqrt(jnp.mean(og * og, axis=-1, keepdims=True) + EPS)
        o = og.reshape(b, n, e) * norm_weight
        return o @ Wo

    def _L0_ffn_ref(x, w_q, bn_gamma, bn_beta, keys, down_embed, up_embed):
        import jax, jax.numpy as jnp
        import numpy as np
        H = 8
        KD = 128
        TOPK = 8
        NUM_KEYS = 64
        N_EXPERTS = NUM_KEYS * NUM_KEYS
        N_DIM = 256
        BN_EPS = 1e-05

        def gelu_new(x):
            c = jnp.sqrt(jnp.asarray(2.0 / jnp.pi, x.dtype))
            return 0.5 * x * (1.0 + jnp.tanh(c * (x + 0.044715 * x * x * x)))
        b, n, d = x.shape
        q = jnp.einsum('bnd,de->bne', x, w_q)
        mean = jnp.mean(q, axis=(0, 1))
        var = jnp.var(q, axis=(0, 1))
        q = (q - mean) * jax.lax.rsqrt(var + BN_EPS) * bn_gamma + bn_beta
        q = q.reshape(b, n, 2, H, KD).transpose(2, 0, 1, 3, 4)
        sim = jnp.einsum('pbnhd,hkpd->pbnhk', q, keys)
        sx, ix = jax.lax.top_k(sim[0], TOPK)
        sy, iy = jax.lax.top_k(sim[1], TOPK)
        all_scores = (sx[..., :, None] + sy[..., None, :]).reshape(b, n, H, TOPK * TOPK)
        all_indices = (ix[..., :, None] * NUM_KEYS + iy[..., None, :]).reshape(b, n, H, TOPK * TOPK)
        scores, pk = jax.lax.top_k(all_scores, TOPK)
        indices = jnp.take_along_axis(all_indices, pk, axis=-1)
        wd = down_embed[indices]
        wu = up_embed[indices]
        h = jnp.einsum('bnd,bnhkd->bnhk', x, wd)
        h = gelu_new(h)
        h = jax.nn.softmax(scores, axis=-1) * h
        out = jnp.einsum('bnhk,bnhkd->bnd', h, wu)
        return out
    x = L0_attn_x
    x = x + _L0_attn_ref(_layernorm(x, axis=-1), L0_attn_Wq, L0_attn_Wk, L0_attn_Wv, L0_attn_Wo, L0_attn_Wf1, L0_attn_Wf2, L0_attn_Wg1, L0_attn_Wg2, L0_attn_norm_weight)
    x = x + _L0_ffn_ref(_layernorm(x, axis=-1), L0_ffn_w_q, L0_ffn_bn_gamma, L0_ffn_bn_beta, L0_ffn_keys, L0_ffn_down_embed, L0_ffn_up_embed)
    return x

_drawn_inputs = setup_inputs


def setup_inputs(seed=0):
    import zlib

    import numpy as np

    out = dict(_drawn_inputs(seed))
    spreads = {'L0_attn_norm_weight': (1.0, 0.2),
     'L0_ffn_bn_gamma': (1.0, 0.6),
     'L0_ffn_bn_beta': (0.0, 0.8)}
    factors = {'L0_attn_Wf1': 8.0,
     'L0_attn_Wf2': 8.0,
     'L0_attn_Wg1': 8.0,
     'L0_attn_Wg2': 8.0,
     'L0_ffn_w_q': 8.0,
     'L0_ffn_keys': 8.0,
     'L0_ffn_down_embed': 8.0,
     'L0_ffn_up_embed': 8.0}
    for name, (base, spread) in spreads.items():
        noise = np.random.default_rng([zlib.crc32(name.encode()), seed]).standard_normal(out[name].shape)
        drawn = base * np.exp(spread * noise) if base else spread * noise
        out[name] = jnp.asarray(drawn.astype(out[name].dtype))
    for name, factor in factors.items():
        out[name] = (out[name] * factor).astype(out[name].dtype)
    return out
```

```python
import concourse.bass as bass
from concourse import mybir
from contextlib import ExitStack

BATCH, SEQ, E = 2, 4096, 256
HEADS, D = 16, 16
P = 128
TOKENS = BATCH * SEQ
EG = E // P
TILE = 512
SUB = TILE // P
STEPS = SEQ // TILE
LN_EPS = 1e-5
FH, KD, TOPK, KEYS = 8, 128, 8, 64
QG = 2 * FH
QC = QG * KD
SIMS = QG * KEYS
EHI, ELO = 128, 32
CAND = 20
PSCALE = 16384.0
SUBTILES = TOKENS // P

f32 = mybir.dt.float32
f16 = mybir.dt.float16
bf16 = mybir.dt.bfloat16
u32 = mybir.dt.uint32
ALU = mybir.AluOpType
ACT = mybir.ActivationFunctionType
AX = mybir.AxisListType

PP_STEPS = 13
UNITS = EG * D
NS = 8
NPROD = 4
LAG = 3
REDUCE_FROM = 6


def inner(ap, n):
    if len(ap.shape) == 2:
        return ap.rearrange("p (a o) -> p a o", o=1).broadcast_to([ap.shape[0], ap.shape[1], n])
    return ap.rearrange("p a (b o) -> p a b o", o=1).broadcast_to([*ap.shape, n])


def attention(nc, x, wq, wk, wv, wo, wf1, wf2, wg1, wg2, norm_w, c_ident, c_sel, c_red, c_bm, x1_dram, x2t_dram, cacc):
    x_v = x.rearrange("b (ts p) e -> b p ts e", p=P)
    x1_v = x1_dram.rearrange("(b ts p) e -> b p ts e", b=BATCH, p=P)
    x2t_v = x2t_dram.rearrange("c p t -> p c t")
    with ExitStack() as ctx:
        def sb(name, shape, dt=f32):
            return ctx.enter_context(nc.sbuf_tensor(name, shape, dt))

        def ps(name, shape):
            return ctx.enter_context(nc.psum_tensor(name, shape, f32))

        def sem(name):
            return ctx.enter_context(nc.semaphore(name))

        ident = sb("ident", [P, P])
        sel_f = sb("sel_f", [P, D * P])
        sel = sb("sel", [P, D, P], bf16)
        red = sb("red", [P, D, P])
        bm = sb("bm", [P, P])
        w_q = sb("w_q", [P, EG, E])
        w_k = sb("w_k", [P, EG, E])
        w_v = sb("w_v", [P, EG, E])
        w_o = sb("w_o", [P, EG, E])
        w_low = sb("w_low", [P, EG, 48])
        w_up = sb("w_up", [48, E])
        nw = sb("nw", [P, EG])
        eps = sb("eps", [P, 1])
        mhalf = sb("mhalf", [P, SUB])
        x_in = [sb(f"x_in{b}", [P, SUB, E]) for b in range(BATCH)]
        st = sb("st", [P, SUB, 6])
        mv = sb("mv", [P, SUB, 2])
        veps = sb("veps", [P, SUB])
        rstd = sb("rstd", [P, SUB])
        xn = sb("xn", [P, SUB, E])
        xt = sb("xt", [P, EG, TILE])
        low = sb("low", [48, TILE])
        q_s = [sb(f"q_s{b}", [P, EG, TILE]) for b in range(BATCH)]
        k_s = [sb(f"k_s{b}", [P, EG, TILE]) for b in range(BATCH)]
        f_s = [sb(f"f_s{b}", [P, EG, TILE]) for b in range(BATCH)]
        g_s = [sb(f"g_s{b}", [P, EG, TILE]) for b in range(BATCH)]
        v_f = sb("v_f", [P, EG, TILE])
        v_r = sb("v_r", [P, EG, TILE])
        v_p = [sb(f"v_p{b}", [P, 3, EG, TILE], bf16) for b in range(BATCH)]
        kv = sb("kv", [P, 2, TILE])
        state = sb("state", [P, NS, TILE])
        prod = sb("prod", [P, NPROD, TILE])
        carry = [sb(f"carry{b}", [P, UNITS]) for b in range(BATCH)]
        og = sb("og", [P, EG * TILE])
        sq = sb("sq", [P, EG * TILE])
        x1 = sb("x1", [P, SUB, E])
        st2 = sb("st2", [P, SUB, 6])
        mv2 = sb("mv2", [P, SUB, 2])
        veps2 = sb("veps2", [P, SUB])
        rstd2 = sb("rstd2", [P, SUB])
        x2 = sb("x2", [P, SUB, E + 1])
        x2t = sb("x2t", [P, EG, TILE])

        pp = [ps(f"pp{i}", [P, TILE]) for i in range(2)]
        vb = [ps(f"vb{i}", [P, TILE]) for i in range(2)]
        o_ps = ps("o_ps", [P, EG, TILE])
        pm = ps("pm", [P, EG, TILE])

        s_wload = sem("s_wload")
        s_const = sem("s_const")
        s_xload = [sem(f"s_xload{b}") for b in range(BATCH)]
        s_var = sem("s_var")
        s_rstd = sem("s_rstd")
        s_xn = sem("s_xn")
        s_ppfull = sem("s_ppfull")
        s_ppfree = sem("s_ppfree")
        s_vsplit = sem("s_vsplit")
        s_vb = sem("s_vb")
        s_kv = sem("s_kv")
        s_scan = sem("s_scan")
        s_carry = sem("s_carry")
        s_prod = sem("s_prod")
        s_red = sem("s_red")
        s_og = sem("s_og")
        s_sq = sem("s_sq")
        s_ms = sem("s_ms")
        s_rms = sem("s_rms")
        s_ogn = sem("s_ogn")
        s_attn = sem("s_attn")
        s_x1 = sem("s_x1")
        s_var2 = sem("s_var2")
        s_rstd2 = sem("s_rstd2")
        s_x2 = sem("s_x2")
        s_x2tp = sem("s_x2tp")
        s_x2t = sem("s_x2t")
        s_cov = sem("s_cov")
        s_cacc = sem("s_cacc")
        s_x1st = sem("s_x1st")
        s_x2st = sem("s_x2st")
        s_step = sem("s_step")
        s_lns = sem("s_lns")

        CARRIES = UNITS // 4
        WLOADS = 13

        def passes(eng, body):
            body(0, True, False)
            with eng.Fori(1, STEPS - 1) as it:
                body(it, False, False)
            body(STEPS - 1, False, True)

        block = ctx.enter_context(nc.Block())

        @block.sync
        def _(sp):
            for dst, src in ((ident[:], c_ident), (sel_f[:], c_sel), (red[:].rearrange("p a b -> p (a b)"), c_red),
                             (bm[:], c_bm)):
                sp.dma_start(dst, src).then_inc(s_wload, 16)
            for dst, src in ((w_q, wq), (w_k, wk), (w_v, wv), (w_o, wo)):
                sp.dma_start(dst[:], src.rearrange("(c p) n -> p c n", p=P)).then_inc(s_wload, 16)
            sp.dma_start(nw[:], norm_w.rearrange("(c p) -> p c", p=P), allow_slow_non_contiguous=True).then_inc(s_wload, 16)
            sp.wait_ge(s_const, 1)
            sp.dma_start(w_low[:, :, 0:16], wf1.rearrange("(c p) n -> p c n", p=P)).then_inc(s_wload, 16)
            sp.dma_start(w_low[:, :, 32:48], wg1.rearrange("(c p) n -> p c n", p=P)).then_inc(s_wload, 16)
            sp.dma_start(w_up[0:16, :], wf2).then_inc(s_wload, 16)
            sp.dma_start(w_up[32:48, :], wg2).then_inc(s_wload, 16)

            def load(it, b, fresh):
                at = it * SUB if isinstance(it, int) else sp.snap(it * SUB)
                if not fresh:
                    sp.wait_ge(s_x1, 2 * it - 1 + b)
                sp.dma_start(x_in[b][:], x_v[b, :, bass.ds(at, SUB), :]).then_inc(s_xload[b], 16)

            def store(n, it, b):
                sp.wait_ge(s_x2t, n + 1)
                sp.dma_start(x2t_v[:, :, bass.ds(it * TILE + b * SEQ, TILE)], x2t[:]).then_inc(s_x2st, 16)
                sp.dma_start(x1_v[b, :, bass.ts(it, SUB), :], x1[:]).then_inc(s_x1st, 16)

            load(0, 0, True)
            load(0, 1, True)

            def body(it, first, last):
                n = it * 2
                if not first:
                    store(n - 1, it - 1, 1)
                    load(it, 1, False)
                store(n, it, 0)
                if not last:
                    load(it + 1, 0, False)

            passes(sp, body)
            store(2 * STEPS - 1, STEPS - 1, 1)
            sp.wait_ge(s_x1st, 32 * STEPS)
            sp.wait_ge(s_x2st, 32 * STEPS)

        @block.gpsimd
        def _(pool):
            nc.gpsimd.memset(w_low[:], 0.0).then_inc(s_const, 1)
            nc.gpsimd.memset(mhalf[:], -0.5)
            nc.gpsimd.memset(eps[:], LN_EPS)
            for b in range(BATCH):
                nc.gpsimd.memset(carry[b][:], 0.0)
            nc.gpsimd.memset(cacc[:], 0.0)
            nc.gpsimd.memset(x2[:, :, E:E + 1], 1.0)
            pool.drain().then_inc(s_const, 1)

            def head_rstd(n):
                pool.wait_ge(s_var, n + 1)
                nc.gpsimd.tensor_tensor(rstd[:], veps[:], mhalf[:], ALU.pow).then_inc(s_rstd, 1)

            def tail_rstd(n):
                pool.wait_ge(s_var2, n + 1)
                nc.gpsimd.tensor_tensor(rstd2[:], veps2[:], mhalf[:], ALU.pow).then_inc(s_rstd2, 1)

            def heavy(n, b, tail, head):
                for u in range(UNITS):
                    pool.wait_ge(s_scan, n * UNITS + u + 1)
                    if u >= NPROD or not (isinstance(n, int) and n == 0):
                        pool.wait_ge(s_red, n * UNITS + u - NPROD + 1)
                    nc.gpsimd.tensor_tensor(prod[:, u % NPROD, :], state[:, u % NS, :], q_s[b][:, u // D, :],
                                            ALU.mult).then_inc(s_prod, 1)
                    if tail and u == 9:
                        tail_rstd(n - 1)
                    if head and u == 14:
                        head_rstd(n + 1)

            head_rstd(0)

            def body(it, first, last):
                heavy(it * 2, 0, not first, True)
                heavy(it * 2 + 1, 1, True, not last)

            passes(pool, body)
            tail_rstd(2 * STEPS - 1)

        @block.scalar
        def _(act):
            def evac(n, b, step, out, func):
                act.wait_ge(s_ppfull, n * PP_STEPS + step + 1)
                nc.scalar.activation(out, pp[(b * PP_STEPS + step) % 2][0:out.shape[0], :], func).then_inc(s_ppfree, 1)

            def head(n, b, lo, hi):
                for step in range(lo, hi):
                    if step < 2:
                        evac(n, b, step, xt[:, step, :], ACT.Copy)
                    elif step < 4:
                        if step == 2 and not (isinstance(n, int) and n == 0):
                            act.wait_ge(s_vsplit, n)
                        evac(n, b, step, v_f[:, step - 2, :], ACT.Copy)
                    elif step == 4:
                        evac(n, b, step, low[:], ACT.Copy)
                    elif step < 7:
                        evac(n, b, step, q_s[b][:, step - 5, :], ACT.Silu)
                    elif step < 9:
                        evac(n, b, step, k_s[b][:, step - 7, :], ACT.Silu)
                    elif step < 11:
                        evac(n, b, step, f_s[b][:, step - 9, :], ACT.Sigmoid)
                    else:
                        evac(n, b, step, g_s[b][:, step - 11, :], ACT.Sigmoid)

            def tail_rms(n):
                act.wait_ge(s_og, n + 1)
                nc.scalar.activation(sq[:], og[:], ACT.Square).then_inc(s_sq, 1)
                act.wait_ge(s_ms, n + 1)
                nc.scalar.activation(sq[:], pm[:].rearrange("p c t -> p (c t)"), ACT.Ln, bias=eps[:, 0:1]).then_inc(s_lns, 1)
                act.wait_ge(s_lns, n + 1)
                nc.scalar.activation(sq[:], sq[:], ACT.Exp, scale=-0.5).then_inc(s_rms, 1)

            def tail_x2t(n):
                act.wait_ge(s_x2tp, n + 1)
                if not (isinstance(n, int) and n == 0):
                    act.wait_ge(s_x2st, n * 16)
                nc.scalar.activation(x2t[:], pm[:], ACT.Copy).then_inc(s_x2t, 1)

            act.wait_ge(s_const, 2)
            head(0, 0, 0, PP_STEPS)

            def body(it, first, last):
                n = it * 2
                if not first:
                    tail_rms(n - 1)
                    tail_x2t(n - 1)
                head(n + 1, 1, 0, PP_STEPS)
                tail_rms(n)
                tail_x2t(n)
                if not last:
                    head(n + 2, 0, 0, PP_STEPS)

            passes(act, body)
            tail_rms(2 * STEPS - 1)
            tail_x2t(2 * STEPS - 1)

        @block.vector
        def _(dve):
            dve.wait_ge(s_const, 2)
            dve.wait_ge(s_wload, 16 * WLOADS)
            nc.vector.tensor_copy(sel[:].rearrange("p a b -> p (a b)"), sel_f[:])
            for c in range(EG):
                nc.vector.tensor_scalar(w_o[:, c, :], w_o[:, c, :], nw[:, c:c + 1], None, ALU.mult)
            dve.drain().then_inc(s_step, 1)

            def head_stats(n, b, it):
                dve.wait_ge(s_xload[b], it * 16 + 16)
                for s in range(SUB):
                    nc.vector.bn_stats(st[:, s, :], x_in[b][:, s, :])
                dve.drain()
                for s in range(SUB):
                    nc.vector.bn_aggr(mv[:, s, :], st[:, s, :])
                dve.drain()
                nc.vector.tensor_scalar(veps[:], mv[:, :, 1], LN_EPS, None, ALU.add).then_inc(s_var, 1)

            def head_norm(n, b):
                dve.wait_ge(s_rstd, n + 1)
                if not (isinstance(n, int) and n == 0):
                    dve.wait_ge(s_ppfull, (n - 1) * PP_STEPS + 2)
                for s in range(SUB):
                    i = nc.vector.tensor_scalar(xn[:, s, :], x_in[b][:, s, :], mv[:, s, 0:1], rstd[:, s:s + 1],
                                                ALU.subtract, ALU.mult)
                i.then_inc(s_xn, 1)

            def head_split(n, b):
                dve.wait_ge(s_ppfree, n * PP_STEPS + 4)
                nc.vector.tensor_copy(v_p[b][:, 0], v_f[:])
                dve.drain()
                nc.vector.tensor_tensor(v_r[:], v_f[:], v_p[b][:, 0], ALU.subtract)
                dve.drain()
                nc.vector.tensor_copy(v_p[b][:, 1], v_r[:])
                dve.drain()
                nc.vector.tensor_tensor(v_p[b][:, 2], v_r[:], v_p[b][:, 1], ALU.subtract).then_inc(s_vsplit, 1)

            def tail_gate(n, b):
                dve.wait_ge(s_red, n * UNITS + UNITS)
                nc.vector.tensor_tensor(og[:], o_ps[:].rearrange("p c t -> p (c t)"),
                                        g_s[b][:].rearrange("p c t -> p (c t)"), ALU.mult).then_inc(s_og, 1)

            def tail_ogn(n):
                dve.wait_ge(s_rms, n + 1)
                nc.vector.tensor_tensor(og[:], og[:], sq[:], ALU.mult).then_inc(s_ogn, 1)

            def tail_x1(n, b):
                dve.wait_ge(s_attn, n + 1)
                if not (isinstance(n, int) and n == 0):
                    dve.wait_ge(s_x1st, n * 16)
                nc.vector.tensor_tensor(x1[:].rearrange("p s e -> p (s e)"), pm[:].rearrange("p c t -> p (c t)"),
                                        x_in[b][:].rearrange("p s e -> p (s e)"), ALU.add).then_inc(s_x1, 1)
                dve.drain()
                for s in range(SUB):
                    nc.vector.bn_stats(st2[:, s, :], x1[:, s, :])
                dve.drain()
                for s in range(SUB):
                    nc.vector.bn_aggr(mv2[:, s, :], st2[:, s, :])
                dve.drain()
                nc.vector.tensor_scalar(veps2[:], mv2[:, :, 1], LN_EPS, None, ALU.add).then_inc(s_var2, 1)

            def tail_norm(n):
                dve.wait_ge(s_rstd2, n + 1)
                for s in range(SUB):
                    i = nc.vector.tensor_scalar(x2[:, s, 0:E], x1[:, s, :], mv2[:, s, 0:1], rstd2[:, s:s + 1],
                                                ALU.subtract, ALU.mult)
                i.then_inc(s_x2, 1)

            def tail_cacc(n):
                dve.wait_ge(s_cov, n + 1)
                nc.vector.tensor_tensor(cacc[:], pm[:, :, 0:E + 1], cacc[:], ALU.add).then_inc(s_cacc, 1)

            def kv_mult(n, b, u):
                dve.wait_ge(s_vb, n * UNITS + u + 1)
                if u >= 2 or not (isinstance(n, int) and n == 0):
                    dve.wait_ge(s_scan, n * UNITS + u - 1)
                nc.vector.tensor_tensor(kv[:, u % 2, :], vb[u % 2][:], k_s[b][:, u // D, :], ALU.mult).then_inc(s_kv, 1)

            def scan(n, b, u):
                dve.wait_ge(s_kv, n * UNITS + u + 1)
                if u >= NS or not (isinstance(n, int) and n == 0):
                    dve.wait_ge(s_prod, n * UNITS + u - NS + 1)
                    dve.wait_ge(s_carry, n * CARRIES + (u - NS) // 4 + 1)
                nc.vector.tensor_tensor_scan(state[:, u % NS, :], f_s[b][:, u // D, :], kv[:, u % 2, :],
                                             carry[b][:, u:u + 1], ALU.mult, ALU.add).then_inc(s_scan, 1)

            def save_carry(n, b, j):
                dve.wait_ge(s_scan, n * UNITS + 4 * j + 4)
                u = 4 * j
                nc.vector.tensor_copy(carry[b][:, u:u + 4], state[:, u % NS:u % NS + 4, TILE - 1]).then_inc(s_carry, 1)

            def heavy(n, b, it, tail, head, next_it):
                dve.wait_ge(s_ppfree, n * PP_STEPS + PP_STEPS)
                kv_mult(n, b, 0)
                for u in range(UNITS):
                    if u + 1 < UNITS:
                        kv_mult(n, b, u + 1)
                    scan(n, b, u)
                    if u % 4 == 0 and u:
                        save_carry(n, b, u // 4 - 1)
                    if tail and u == 3:
                        tail_gate(n - 1, 1 - b)
                    if tail and u == 6:
                        tail_ogn(n - 1)
                    if tail and u == 8:
                        tail_x1(n - 1, 1 - b)
                    if tail and u == 11:
                        tail_norm(n - 1)
                    if head and u == 13:
                        head_stats(n + 1, 1 - b, next_it)
                    if head and u == 16:
                        head_norm(n + 1, 1 - b)
                    if tail and u == 17:
                        tail_cacc(n - 1)
                    if head and u == 23:
                        head_split(n + 1, 1 - b)
                save_carry(n, b, CARRIES - 1)

            head_stats(0, 0, 0)
            head_norm(0, 0)
            head_split(0, 0)

            def body(it, first, last):
                heavy(it * 2, 0, it, not first, True, it)
                heavy(it * 2 + 1, 1, it, True, not last, it + 1)

            passes(dve, body)
            n = 2 * STEPS - 1
            tail_gate(n, 1)
            tail_ogn(n)
            tail_x1(n, 1)
            tail_norm(n)
            tail_cacc(n)

        @block.tensor
        def _(pe):
            pe.wait_ge(s_wload, 16 * WLOADS)
            pe.wait_ge(s_step, 1)

            def pp_bank(n, b, step):
                if step >= 2 or not (isinstance(n, int) and n == 0):
                    pe.wait_ge(s_ppfree, n * PP_STEPS + step - 1)
                return pp[(b * PP_STEPS + step) % 2]

            def head(n, b, step):
                bank = pp_bank(n, b, step)
                if step < 2:
                    pe.wait_ge(s_xn, n + 1)
                    for s in range(SUB):
                        i = nc.tensor.transpose(bank[:, s * P:(s + 1) * P], xn[:, s, step * P:(step + 1) * P], ident[:])
                elif step == 4:
                    for c in range(EG):
                        i = nc.tensor.matmul(bank[0:48, :], w_low[:, c, :], xt[:, c, :], start=c == 0, stop=c == EG - 1)
                elif step < 9:
                    if step == 2:
                        pe.wait_ge(s_ppfree, n * PP_STEPS + 2)
                    w = w_v if step < 4 else w_q if step < 7 else w_k
                    g = step - (2 if step < 4 else 5 if step < 7 else 7)
                    for c in range(EG):
                        i = nc.tensor.matmul(bank[:], w[:, c, g * P:(g + 1) * P], xt[:, c, :], start=c == 0, stop=c == EG - 1)
                else:
                    g = (step - 9) % EG
                    r = 0 if step < 11 else 32
                    i = nc.tensor.matmul(bank[:], w_up[r:r + 16, g * P:(g + 1) * P], low[r:r + 16, :], start=True, stop=True)
                i.then_inc(s_ppfull, 1)

            def tail_ms(n):
                pe.wait_ge(s_sq, n + 1)
                if not (isinstance(n, int) and n == 0):
                    pe.wait_ge(s_cacc, n)
                for g in range(EG):
                    i = nc.tensor.matmul(pm[:, g, :], bm[:], sq[:, g * TILE:(g + 1) * TILE], start=True, stop=True)
                i.then_inc(s_ms, 1)

            def tail_wo(n):
                pe.wait_ge(s_ogn, n + 1)
                pmv = pm[:].rearrange("p c (s e) -> p (c s) e", e=E)
                for s in range(SUB):
                    for g in range(EG):
                        i = nc.tensor.matmul(pmv[:, s, :], og[:, g * TILE + s * P:g * TILE + (s + 1) * P], w_o[:, g, :],
                                             start=g == 0, stop=g == EG - 1)
                i.then_inc(s_attn, 1)

            def tail_x2t(n):
                pe.wait_ge(s_x2, n + 1)
                for c in range(EG):
                    for s in range(SUB):
                        i = nc.tensor.transpose(pm[:, c, s * P:(s + 1) * P], x2[:, s, c * P:(c + 1) * P], ident[:])
                i.then_inc(s_x2tp, 1)

            def tail_cov(n):
                pe.wait_ge(s_x2t, n + 1)
                for c in range(EG):
                    for s in range(SUB):
                        i = nc.tensor.matmul(pm[:, c, 0:E + 1], x2[:, s, c * P:(c + 1) * P], x2[:, s, :],
                                             start=s == 0, stop=s == SUB - 1)
                i.then_inc(s_cov, 1)

            def spread(n, b, u):
                if u >= 2 or not (isinstance(n, int) and n == 0):
                    pe.wait_ge(s_kv, n * UNITS + u - 1)
                for part in range(3):
                    i = nc.tensor.matmul(vb[u % 2][:], sel[:, u % D, :], v_p[b][:, part, u // D, :],
                                         start=part == 0, stop=part == 2)
                i.then_inc(s_vb, 1)

            def reduce(n, u):
                pe.wait_ge(s_prod, n * UNITS + u + 1)
                if u == 0 and not (isinstance(n, int) and n == 0):
                    pe.wait_ge(s_og, n)
                nc.tensor.matmul(o_ps[:, u // D, :], red[:, u % D, :], prod[:, u % NPROD, :],
                                 start=u % D == 0, stop=u % D == D - 1).then_inc(s_red, 1)

            def heavy(n, b, tail, head_next):
                pe.wait_ge(s_vsplit, n + 1)
                for u in range(UNITS):
                    spread(n, b, u)
                    if u == REDUCE_FROM:
                        for v in range(REDUCE_FROM - LAG):
                            reduce(n, v)
                    if u >= REDUCE_FROM:
                        reduce(n, u - LAG)
                    if tail and u == 5:
                        tail_ms(n - 1)
                    if tail and u == 8:
                        tail_wo(n - 1)
                    if tail and u == 13:
                        tail_x2t(n - 1)
                    if tail and u == 15:
                        tail_cov(n - 1)
                    if head_next and u >= 18 and u < 18 + PP_STEPS:
                        head(n + 1, 1 - b, u - 18)
                for v in range(UNITS - LAG, UNITS):
                    reduce(n, v)

            for step in range(PP_STEPS):
                head(0, 0, step)

            def body(it, first, last):
                heavy(it * 2, 0, not first, True)
                heavy(it * 2 + 1, 1, True, not last)

            passes(pe, body)
            n = 2 * STEPS - 1
            tail_ms(n)
            tail_wo(n)
            tail_x2t(n)
            tail_cov(n)


def fold(nc, fw_q, gamma, beta, keys, down, up, c_ident, c_iota, c_iotac, cacc, m_w, m_c, ones3, ident, down_t, up_s,
         iota, iotac):
    with ExitStack() as ctx:
        def sb(name, shape, dt=f32):
            return ctx.enter_context(nc.sbuf_tensor(name, shape, dt))

        def ps(name, shape):
            return ctx.enter_context(nc.psum_tensor(name, shape, f32))

        def sem(name):
            return ctx.enter_context(nc.semaphore(name))

        fq = sb("fq", [P, EG, QC])
        kn = sb("kn", [KEYS, FH, 2, KD])
        kt = sb("kt", [P, QG, KEYS])
        kts = sb("kts", [P, QG, KEYS])
        wt = sb("wt", [P, QG, E])
        yw = sb("yw", [P, QG, E])
        gam = sb("gam", [P, QG])
        bet = sb("bet", [P, QG])
        dn = sb("dn", [P, ELO, E])
        mcol = sb("mcol", [P, EG])
        mrow = sb("mrow", [1, E])
        cc = sb("cc", [P, EG, E])
        var = sb("var", [P, QG])
        mean = sb("mean", [P, QG])
        mh = sb("mh", [P, QG])
        s_bn = sb("s_bn", [P, QG])
        cst = sb("cst", [P, QG])
        cst3 = sb("cst3", [P, QG, 3])
        cf = sb("cf", [3, SIMS])
        cr = sb("cr", [3, SIMS])
        c1 = sb("c1", [3, SIMS], bf16)
        c2 = sb("c2", [3, SIMS], bf16)
        c3 = sb("c3", [3, SIMS], bf16)
        io_f = sb("io_f", [P, EHI * 16])
        ioc_f = sb("ioc_f", [P, CAND * TOPK])

        bank = [ps(f"fb{i}", [P, 512]) for i in range(4)]

        s_ld = sem("f_ld")
        s_pe = sem("f_pe")
        s_ev = sem("f_ev")
        s_v = sem("f_v")
        s_pw = sem("f_pw")
        s_dn = sem("f_dn")
        s_de = sem("f_de")
        s_id = sem("f_id")
        block = ctx.enter_context(nc.Block())

        @block.sync
        def _(sp):
            sp.dma_start(ident[:], c_ident).then_inc(s_id, 16)
            sp.dma_start(fq[:], fw_q.rearrange("(c p) n -> p c n", p=P)).then_inc(s_ld, 16)
            sp.dma_start(kn[:], keys.rearrange("h k p d -> k h p d")).then_inc(s_ld, 16)
            sp.dma_start(gam[:], gamma.rearrange("(g p) -> p g", p=P), allow_slow_non_contiguous=True).then_inc(s_ld, 16)
            sp.dma_start(bet[:], beta.rearrange("(g p) -> p g", p=P), allow_slow_non_contiguous=True).then_inc(s_ld, 16)
            sp.dma_start(io_f[:], c_iota).then_inc(s_ld, 16)
            sp.dma_start(ioc_f[:], c_iotac).then_inc(s_ld, 16)
            sp.dma_start(dn[:], down.rearrange("(p l) c -> p l c", l=ELO)).then_inc(s_dn, 16)
            sp.dma_start(up_s[:], up.rearrange("(p l) c -> p l c", l=ELO)).then_inc(s_ld, 16)

        LOADS = 7
        NKEYT = QG // 8
        NWT = QG // 2

        @block.gpsimd
        def _(pool):
            nc.gpsimd.memset(mh[:], -0.5).then_inc(s_pw, 1)
            pool.wait_ge(s_pw, 1)
            pool.wait_ge(s_v, 3)
            nc.gpsimd.tensor_tensor(s_bn[:], var[:], mh[:], ALU.pow).then_inc(s_pw, 1)

        @block.scalar
        def _(act):
            for j in range(2 * ELO // 4):
                act.wait_ge(s_de, j + 1)
                c, l4 = j % EG, j // EG
                nc.scalar.activation(down_t[:, c, l4 * 4:l4 * 4 + 4, :].rearrange("p a b -> p (a b)"),
                                     bank[2 + j % 2][:], ACT.Copy).then_inc(s_dn, 1)

        @block.tensor
        def _(pe):
            step = [0]

            def take(i):
                i.then_inc(s_pe, 1)
                step[0] += 1

            def free():
                if step[0] >= 2:
                    pe.wait_ge(s_ev, step[0] - 1)
                return bank[step[0] % 2]

            pe.wait_ge(s_id, 16)
            pe.wait_ge(s_ld, 16 * LOADS)
            for j in range(NKEYT):
                b = free()
                for i in range(8):
                    g = j * 8 + i
                    last = nc.tensor.transpose(b[:, i * KEYS:(i + 1) * KEYS], kn[:, g % FH, g // FH, :], ident[0:KEYS, 0:KEYS])
                take(last)
            for j in range(NWT):
                b = free()
                for i in range(4):
                    g, c = j * 2 + i // 2, i % 2
                    last = nc.tensor.transpose(b[:, i * P:(i + 1) * P], fq[:, c, g * KD:(g + 1) * KD], ident[:])
                take(last)
            pe.wait_ge(s_dn, 16)
            for j in range(2 * ELO // 4):
                c, l4 = j % EG, j // EG
                if j >= 2:
                    pe.wait_ge(s_dn, 16 + j - 1)
                for i in range(4):
                    last = nc.tensor.transpose(bank[2 + j % 2][:, i * P:(i + 1) * P], dn[:, l4 * 4 + i, c * P:(c + 1) * P], ident[:])
                last.then_inc(s_de, 1)
            pe.wait_ge(s_v, 1)
            b = free()
            for c in range(EG):
                last = nc.tensor.transpose(b[0:1, c * P:(c + 1) * P], mcol[:, c:c + 1], ident[:])
            take(last)
            pe.wait_ge(s_ev, step[0])
            b = free()
            for c in range(EG):
                last = nc.tensor.matmul(b[:, c * E:(c + 1) * E], mrow[0:1, c * P:(c + 1) * P], mrow[0:1, :], start=True, stop=True)
            take(last)
            pe.wait_ge(s_v, 2)
            for j in range(NWT):
                b = free()
                for i in range(2):
                    g = j * 2 + i
                    for c in range(EG):
                        last = nc.tensor.matmul(b[:, i * E:(i + 1) * E], fq[:, c, g * KD:(g + 1) * KD], cc[:, c, :],
                                                start=c == 0, stop=c == EG - 1)
                take(last)
            b = free()
            for g in range(QG):
                for c in range(EG):
                    last = nc.tensor.matmul(b[:, g:g + 1], fq[:, c, g * KD:(g + 1) * KD], mcol[:, c:c + 1],
                                            start=c == 0, stop=c == EG - 1)
            take(last)
            pe.wait_ge(s_v, 4)
            for j in range(4):
                b = free()
                c, half = j % EG, j // EG
                for i in range(8):
                    g = half * 8 + i
                    last = nc.tensor.matmul(b[:, i * KEYS:(i + 1) * KEYS], wt[:, g, c * P:(c + 1) * P], kts[:, g, :],
                                            start=True, stop=True)
                take(last)
            for half in range(2):
                b = free()
                for i in range(8):
                    g = half * 8 + i
                    last = nc.tensor.matmul(b[0:3, i * KEYS:(i + 1) * KEYS], cst3[:, g, :], kt[:, g, :], start=True, stop=True)
                take(last)

        @block.vector
        def _(dve):
            step = [0]

            def full():
                dve.wait_ge(s_pe, step[0] + 1)
                step[0] += 1
                return bank[(step[0] - 1) % 2]

            nc.vector.tensor_scalar(mcol[:], cacc[:, :, E], 1.0 / TOKENS, None, ALU.mult).then_inc(s_v, 1)
            for j in range(NKEYT):
                nc.vector.tensor_copy(kt[:, j * 8:j * 8 + 8, :].rearrange("p a b -> p (a b)"), full()[:]).then_inc(s_ev, 1)
            for j in range(NWT):
                nc.vector.tensor_copy(wt[:, j * 2:j * 2 + 2, :].rearrange("p a b -> p (a b)"), full()[:]).then_inc(s_ev, 1)
            nc.vector.tensor_copy(mrow[0:1, :], full()[0:1, 0:E]).then_inc(s_ev, 1)
            b = full()
            nc.vector.scalar_tensor_tensor(cc[:], cacc[:, :, 0:E], 1.0 / TOKENS,
                                           b[:, 0:EG * E].rearrange("p (c e) -> p c e", e=E),
                                           ALU.mult, ALU.subtract).then_inc(s_ev, 1)
            dve.drain().then_inc(s_v, 1)
            for j in range(NWT):
                nc.vector.tensor_tensor(yw[:, j * 2:j * 2 + 2, :].rearrange("p a b -> p (a b)"), full()[:],
                                        wt[:, j * 2:j * 2 + 2, :].rearrange("p a b -> p (a b)"), ALU.mult).then_inc(s_ev, 1)
            dve.drain()
            nc.vector.tensor_reduce(var[:], yw[:], AX.X, ALU.add)
            dve.drain()
            nc.vector.tensor_scalar(var[:], var[:], 0.0, LN_EPS, ALU.max, ALU.add).then_inc(s_v, 1)
            nc.vector.tensor_copy(mean[:], full()[:, 0:QG]).then_inc(s_ev, 1)
            dve.wait_ge(s_pw, 2)
            nc.vector.tensor_tensor(s_bn[:], s_bn[:], gam[:], ALU.mult)
            dve.drain()
            nc.vector.tensor_tensor(mean[:], mean[:], s_bn[:], ALU.mult)
            nc.vector.tensor_tensor(kts[:], kt[:], inner(s_bn[:], KEYS), ALU.mult)
            dve.drain()
            nc.vector.tensor_tensor(cst[:], bet[:], mean[:], ALU.subtract)
            dve.drain()
            nc.vector.tensor_copy(cst3[:], inner(cst[:], 3))
            dve.drain().then_inc(s_v, 1)
            for j in range(4):
                c, half = j % EG, j // EG
                nc.vector.tensor_copy(m_w[:, c, half * 512:(half + 1) * 512], full()[:]).then_inc(s_ev, 1)
            for half in range(2):
                nc.vector.tensor_copy(cf[:, half * 512:(half + 1) * 512], full()[0:3, :]).then_inc(s_ev, 1)
            dve.drain()
            nc.vector.tensor_copy(c1[:], cf[:])
            dve.drain()
            nc.vector.tensor_tensor(cr[:], cf[:], c1[:], ALU.subtract)
            dve.drain()
            nc.vector.tensor_copy(c2[:], cr[:])
            dve.drain()
            nc.vector.tensor_tensor(c3[:], cr[:], c2[:], ALU.subtract)
            nc.vector.tensor_scalar(m_c[:], c1[:], ident[0:3, 0:1], None, ALU.mult)
            dve.drain()
            nc.vector.scalar_tensor_tensor(m_c[:], c2[:], ident[0:3, 1:2], m_c[:], ALU.mult, ALU.add)
            dve.drain()
            nc.vector.scalar_tensor_tensor(m_c[:], c3[:], ident[0:3, 2:3], m_c[:], ALU.mult, ALU.add)
            nc.vector.memset(ones3[:], 1.0)
            nc.vector.tensor_copy(iota[:].rearrange("p a b -> p (a b)"), io_f[:])
            nc.vector.tensor_copy(iotac[:].rearrange("p a b -> p (a b)"), ioc_f[:])


def experts(nc, x1_dram, x2t_dram, out, m_w, m_c, ones3, ident, down_t, up_s, iota, iotac):
    x1_v = x1_dram.rearrange("(m p) e -> p m e", p=P)
    x2t_v = x2t_dram.rearrange("c p t -> p c t")
    with ExitStack() as ctx:
        def sb(name, shape, dt=f32):
            return ctx.enter_context(nc.sbuf_tensor(name, shape, dt))

        def ps(name, shape):
            return ctx.enter_context(nc.psum_tensor(name, shape, f32))

        def sem(name):
            return ctx.enter_context(nc.semaphore(name))

        xt = [sb(f"ext{i}", [P, EG, P]) for i in range(2)]
        x1 = [sb(f"ex1{i}", [P, E]) for i in range(2)]
        y = [sb(f"ey{i}", [P, E]) for i in range(2)]
        held = sb("held", [P, 1])
        s8 = sb("s8", [P, QG, TOPK])
        i8 = sb("i8", [P, QG, TOPK], u32)
        ix = sb("ix", [P, FH, TOPK])
        iy = sb("iy", [P, FH, TOPK])
        cand = sb("cand", [P, FH, CAND])
        code = sb("code", [P, FH, CAND])
        top = sb("top", [P, FH, TOPK])
        pos = sb("pos", [P, FH, TOPK], u32)
        posh = sb("posh", [P, FH, TOPK], f16)
        oh = sb("oh", [P, FH, CAND, TOPK], f16)
        ohc = sb("ohc", [P, FH, CAND, TOPK])
        ex = sb("ex", [P, FH, TOPK])
        rs = sb("rs", [P, FH])
        pf = sb("pf", [P, FH * TOPK])
        ph = sb("ph", [P, FH * TOPK], f16)
        ecode = sb("ecode", [P, FH * TOPK])
        ecu = sb("ecu", [P, FH * TOPK], u32)
        ehu = sb("ehu", [P, FH * TOPK], u32)
        elu = sb("elu", [P, FH * TOPK], u32)
        rt = sb("rt", [P, 3, P])
        rtt = sb("rtt", [P, 3, P], f16)
        uh = sb("uh", [P, EHI, P], f16)
        vl = sb("vl", [P, ELO, P], f16)
        gh = sb("gh", [P, ELO, P])

        ps_s = ps("ps_s", [P, SIMS])
        ps_h = [ps(f"ps_h{i}", [P, 512]) for i in range(2)]
        ps_a = [ps(f"ps_a{i}", [P, 16, ELO]) for i in range(2)]
        ps_t = ps("ps_t", [P, 512])
        ps_o = ps("ps_o", [P, 512])

        s_xt = [sem(f"e_xt{i}") for i in range(2)]
        s_x1 = [sem(f"e_x1{i}") for i in range(2)]
        s_st = [sem(f"e_st{i}") for i in range(2)]
        s_sim = sem("e_sim")
        s_simu = sem("e_simu")
        s_top = sem("e_top")
        s_exp = sem("e_exp")
        s_oh = sem("e_oh")
        s_ohc = sem("e_ohc")
        s_rt = sem("e_rt")
        s_tr = sem("e_tr")
        s_rtt = sem("e_rtt")
        s_uv = sem("e_uv")
        s_a = sem("e_a")
        s_g = sem("e_g")
        s_h = sem("e_h")
        s_gh = sem("e_gh")
        s_o = sem("e_o")
        s_y = sem("e_y")
        HG = ELO // 4
        AG = P // 16

        def passes(eng, body):
            body(0, True, False)
            with eng.Fori(1, SUBTILES // 2 - 1) as it:
                body(it, False, False)
            body(SUBTILES // 2 - 1, False, True)

        block = ctx.enter_context(nc.Block())

        @block.sync
        def _(sp):
            def load_xt(m, it, i, fresh):
                if not fresh:
                    sp.wait_ge(s_h, (m - 1) * HG)
                sp.dma_start(xt[i][:], x2t_v[:, :, bass.ts(m, P)]).then_inc(s_xt[i], 16)

            def load_x1(m, it, i, fresh):
                if not fresh:
                    sp.wait_ge(s_y, m - 1)
                sp.dma_start(x1[i][:], x1_v[:, bass.ds(m, 1), :].rearrange("p m e -> p (m e)")).then_inc(s_x1[i], 16)

            def store(m, it, i):
                sp.wait_ge(s_y, m + 1)
                sp.dma_start(out[bass.ts(m, P), :], y[i][:]).then_inc(s_st[i], 16)

            load_xt(0, 0, 0, True)
            load_xt(1, 0, 1, True)
            load_x1(0, 0, 0, True)
            load_x1(1, 0, 1, True)

            def body(it, first, last):
                for i in range(2):
                    m = it * 2 + i
                    if not last:
                        load_xt(m + 2, it + 1, i, False)
                    store(m, it, i)
                    if not last:
                        load_x1(m + 2, it + 1, i, False)

            passes(sp, body)
            for i in range(2):
                sp.wait_ge(s_st[i], 16 * (SUBTILES // 2))

        @block.gpsimd
        def _(pool):
            def decode(m):
                pool.wait_ge(s_oh, m + 1)
                nc.gpsimd.tensor_tensor(ohc[:], oh[:], inner(code[:], TOPK), ALU.mult).then_inc(s_ohc, 1)

            decode(0)
            with pool.Fori(1, SUBTILES) as m:
                decode(m)

        @block.scalar
        def _(act):
            def softmax_exp(m):
                act.wait_ge(s_top, m + 1)
                nc.scalar.activation(ex[:], ex[:], ACT.Exp).then_inc(s_exp, 1)

            def turn(m):
                act.wait_ge(s_tr, m + 1)
                nc.scalar.activation(rtt[:].rearrange("p a b -> p (a b)"), ps_t[:, 0:3 * P], ACT.Copy).then_inc(s_rtt, 1)

            softmax_exp(0)
            turn(0)

            def body(it, first, last):
                for i in range(2):
                    m = it * 2 + i
                    if not (first and i == 0):
                        act.wait_ge(s_o, m)
                    for j in range(HG):
                        act.wait_ge(s_h, m * HG + j + 1)
                        nc.scalar.activation(gh[:, 4 * j:4 * j + 4, :].rearrange("p a b -> p (a b)"), ps_h[j % 2][:],
                                             ACT.Gelu_apprx_tanh).then_inc(s_gh, 1)
                    if not (last and i == 1):
                        softmax_exp(m + 1)
                        turn(m + 1)

            passes(act, body)

        @block.tensor
        def _(pe):
            def sims(m, it, i, fresh):
                pe.wait_ge(s_xt[i], it * 16 + 16)
                if not fresh:
                    pe.wait_ge(s_simu, m)
                for half in range(2):
                    cols = slice(half * 512, (half + 1) * 512)
                    nc.tensor.matmul(ps_s[:, cols], ones3[:], m_c[:, cols], start=True, stop=False)
                    for c in range(EG):
                        last = nc.tensor.matmul(ps_s[:, cols], xt[i][:, c, :], m_w[:, c, cols], start=False, stop=c == EG - 1)
                last.then_inc(s_sim, 1)

            def turn(m):
                pe.wait_ge(s_rt, m + 1)
                for j in range(3):
                    last = nc.tensor.transpose(ps_t[:, j * P:(j + 1) * P], rt[:, j, :], ident[:])
                last.then_inc(s_tr, 1)

            def hidden(m, i):
                for j in range(HG):
                    if not (isinstance(m, int) and m * HG + j < 2):
                        pe.wait_ge(s_gh, m * HG + j - 1)
                    for k in range(4):
                        for c in range(EG):
                            last = nc.tensor.matmul(ps_h[j % 2][:, k * P:(k + 1) * P], down_t[:, c, 4 * j + k, :],
                                                    xt[i][:, c, :], start=c == 0, stop=c == EG - 1)
                    last.then_inc(s_h, 1)

            def weights(m):
                pe.wait_ge(s_uv, m + 1)
                for j in range(AG):
                    if not (isinstance(m, int) and m * AG + j < 2):
                        pe.wait_ge(s_g, m * AG + j - 1)
                    for t in range(16):
                        last = nc.tensor.matmul(ps_a[j % 2][:, t, :], uh[:, :, j * 16 + t], vl[:, :, j * 16 + t],
                                                start=True, stop=True)
                    last.then_inc(s_a, 1)

            def combine(m, fresh):
                pe.wait_ge(s_g, m * AG + AG)
                if not fresh:
                    pe.wait_ge(s_y, m)
                for l in range(ELO):
                    last = nc.tensor.matmul(ps_o[:, 0:E], gh[:, l, :], up_s[:, l, :], start=l == 0, stop=l == ELO - 1)
                last.then_inc(s_o, 1)

            sims(0, 0, 0, True)
            turn(0)

            def body(it, first, last):
                for i in range(2):
                    m = it * 2 + i
                    hidden(m, i)
                    if not (last and i == 1):
                        sims(m + 1, it + i, 1 - i, False)
                    weights(m)
                    combine(m, first and i == 0)
                    if not (last and i == 1):
                        turn(m + 1)

            passes(pe, body)

        @block.vector
        def _(dve):
            def route(m):
                dve.wait_ge(s_sim, m + 1)
                nc.vector.memset(held[:], 0.0)
                for g in range(QG):
                    nc.vector.max(s8[:, g, :], ps_s[:, g * KEYS:(g + 1) * KEYS])
                dve.drain()
                for g in range(QG):
                    last = nc.vector.max_index(i8[:, g, :], s8[:, g, :], ps_s[:, g * KEYS:(g + 1) * KEYS])
                last.then_inc(s_simu, 1)

                def pairs(dst, a, b):
                    nc.vector.tensor_tensor(dst[:, :, 0:8], inner(a[:, :, 0], 8), b[:, :, 0:8], ALU.add)
                    nc.vector.tensor_tensor(dst[:, :, 8:12], inner(a[:, :, 1], 4), b[:, :, 0:4], ALU.add)
                    for r in (2, 3):
                        nc.vector.tensor_tensor(dst[:, :, 8 + 2 * r:10 + 2 * r], inner(a[:, :, r], 2), b[:, :, 0:2], ALU.add)
                    nc.vector.tensor_tensor(dst[:, :, 16:20], a[:, :, 4:8], inner(b[:, :, 0], 4), ALU.add)

                pairs(cand, s8[:, 0:FH, :], s8[:, FH:QG, :])
                dve.drain()
                for h in range(FH):
                    nc.vector.max(top[:, h, :], cand[:, h, :])
                nc.vector.tensor_scalar(ix[:], i8[:, 0:FH, :], float(KEYS), None, ALU.mult)
                nc.vector.tensor_copy(iy[:], i8[:, FH:QG, :])
                dve.drain()
                for h in range(FH):
                    nc.vector.max_index(pos[:, h, :], top[:, h, :], cand[:, h, :])
                nc.vector.tensor_tensor(ex[:], top[:], inner(top[:, :, 0], TOPK), ALU.subtract).then_inc(s_top, 1)
                pairs(code, ix[:], iy[:])
                dve.drain()
                nc.vector.tensor_copy(posh[:], pos[:])
                dve.drain()
                nc.vector.tensor_tensor(oh[:], posh[:].rearrange("p h (o k) -> p h o k", o=1).broadcast_to([P, FH, CAND, TOPK]),
                                        iotac[:].rearrange("p (o c) k -> p o c k", o=1).broadcast_to([P, FH, CAND, TOPK]),
                                        ALU.is_equal).then_inc(s_oh, 1)
                dve.wait_ge(s_exp, m + 1)
                nc.vector.tensor_reduce(rs[:], ex[:], AX.X, ALU.add)
                dve.drain()
                nc.vector.reciprocal(rs[:], rs[:])
                dve.drain()
                nc.vector.scalar_tensor_tensor(pf[:].rearrange("p (h k) -> p h k", k=TOPK), ex[:], PSCALE, inner(rs[:], TOPK),
                                               ALU.mult, ALU.mult)
                dve.drain()
                nc.vector.tensor_copy(ph[:], pf[:])
                dve.drain()
                nc.vector.tensor_copy(rt[:, 2, 0:64], ph[:])
                nc.vector.tensor_tensor(rt[:, 2, 64:128], pf[:], ph[:], ALU.subtract)
                dve.wait_ge(s_ohc, m + 1)
                nc.vector.tensor_reduce(ecode[:].rearrange("p (h k) -> p h k", k=TOPK), ohc[:].rearrange("p h c k -> p h k c"),
                                        AX.X, ALU.add)
                dve.drain()
                nc.vector.tensor_copy(ecu[:], ecode[:])
                dve.drain()
                nc.vector.tensor_scalar(ehu[:], ecu[:], 5, None, ALU.logical_shift_right)
                nc.vector.tensor_scalar(elu[:], ecu[:], ELO - 1, None, ALU.bitwise_and)
                dve.drain()
                for part in range(2):
                    nc.vector.tensor_copy(rt[:, 0, part * 64:(part + 1) * 64], ehu[:])
                    last = nc.vector.tensor_copy(rt[:, 1, part * 64:(part + 1) * 64], elu[:])
                dve.drain().then_inc(s_rt, 1)

            def onehots(m, fresh):
                dve.wait_ge(s_rtt, m + 1)
                if not fresh:
                    dve.wait_ge(s_a, m * AG)

                def same(dst, row, n):
                    nc.vector.tensor_tensor(
                        dst.rearrange("p e (a b) -> p e a b", b=16),
                        rtt[:, row:row + 1, :].rearrange("p o (a b) -> p o a b", b=16).broadcast_to([P, n, P // 16, 16]),
                        iota[:, 0:n, :].rearrange("p e (o b) -> p e o b", o=1).broadcast_to([P, n, P // 16, 16]),
                        ALU.is_equal)

                same(vl[:], 1, ELO)
                same(uh[:], 0, EHI)
                dve.drain()
                nc.vector.tensor_tensor(vl[:], vl[:], rtt[:, 2:3, :].broadcast_to([P, ELO, P]), ALU.mult).then_inc(s_uv, 1)

            def gate(m):
                dve.wait_ge(s_gh, m * HG + HG)
                ghv = gh[:].rearrange("p l t -> p t l")
                for j in range(AG):
                    dve.wait_ge(s_a, m * AG + j + 1)
                    nc.vector.tensor_tensor(ghv[:, j * 16:(j + 1) * 16, :], ps_a[j % 2][:], ghv[:, j * 16:(j + 1) * 16, :],
                                            ALU.mult).then_inc(s_g, 1)

            def finish(m, it, i, fresh):
                dve.wait_ge(s_o, m + 1)
                dve.wait_ge(s_x1[i], it * 16 + 16)
                if not fresh:
                    dve.wait_ge(s_st[i], it * 16)
                nc.vector.scalar_tensor_tensor(y[i][:], ps_o[:, 0:E], 1.0 / PSCALE, x1[i][:], ALU.mult, ALU.add).then_inc(s_y, 1)

            route(0)

            def body(it, first, last):
                for i in range(2):
                    m = it * 2 + i
                    onehots(m, first and i == 0)
                    gate(m)
                    if not (last and i == 1):
                        route(m + 1)
                    finish(m, it, i, first)

            passes(dve, body)


def build(nc, x, wq, wk, wv, wo, wf1, wf2, wg1, wg2, norm_w, fw_q, gamma, beta, keys, down, up,
          c_ident, c_sel, c_red, c_bm, c_iota, c_iotac, out):
    x1_dram = nc.dram_tensor("x1_dram", (TOKENS, E), f32, kind="Internal").ap()
    x2t_dram = nc.dram_tensor("x2t_dram", (EG, P, TOKENS), f32, kind="Internal").ap()
    with ExitStack() as ctx:
        cacc = ctx.enter_context(nc.sbuf_tensor("cacc", [P, EG, E + 1], f32))
        attention(nc, x, wq, wk, wv, wo, wf1, wf2, wg1, wg2, norm_w, c_ident, c_sel, c_red, c_bm, x1_dram, x2t_dram, cacc)

        def sb(name, shape, dt=f32):
            return ctx.enter_context(nc.sbuf_tensor(name, shape, dt))

        m_w = sb("m_w", [P, EG, SIMS])
        m_c = sb("m_c", [3, SIMS], bf16)
        ones3 = sb("ones3", [3, P], bf16)
        ident = sb("ident2", [P, P])
        down_t = sb("down_t", [P, EG, ELO, EHI])
        up_s = sb("up_s", [P, ELO, E])
        iota = sb("iota", [P, EHI, 16], f16)
        iotac = sb("iotac", [P, CAND, TOPK], f16)
        fold(nc, fw_q, gamma, beta, keys, down, up, c_ident, c_iota, c_iotac, cacc, m_w, m_c, ones3, ident, down_t, up_s,
             iota, iotac)
        experts(nc, x1_dram, x2t_dram, out.rearrange("b t e -> (b t) e"), m_w, m_c, ones3, ident, down_t, up_s, iota, iotac)


INPUTS = ["L0_attn_x", "L0_attn_Wq", "L0_attn_Wk", "L0_attn_Wv", "L0_attn_Wo", "L0_attn_Wf1", "L0_attn_Wf2", "L0_attn_Wg1",
          "L0_attn_Wg2", "L0_attn_norm_weight", "L0_ffn_w_q", "L0_ffn_bn_gamma", "L0_ffn_bn_beta", "L0_ffn_keys",
          "L0_ffn_down_embed", "L0_ffn_up_embed"]


def constants():
    import numpy as np

    k, m = np.arange(P)[:, None, None], np.arange(P)[None, None, :]
    dv = np.arange(D)[None, :, None]
    sel = k == m // D * D + dv
    red = (k // D == m // D) & (m % D == dv)
    bm = np.arange(P)[:, None] // D == np.arange(P)[None, :] // D
    f = np.float32
    return {
        "c_ident": np.eye(P, dtype=f),
        "c_sel": sel.reshape(P, -1).astype(f),
        "c_red": red.reshape(P, -1).astype(f) * f(D ** -0.5),
        "c_bm": bm.astype(f) * f(1.0 / D),
        "c_iota": np.tile(np.repeat(np.arange(EHI), 16), (P, 1)).astype(f),
        "c_iotac": np.tile(np.repeat(np.arange(CAND), TOPK), (P, 1)).astype(f),
    }


def kernel(**inputs):
    import numpy as np
    import concourse.bacc as bacc
    from concourse.bass_utils import run_bass_kernel_spmd

    nc = bacc.Bacc("TRN2", target_bir_lowering=False, num_devices=1)
    arrays = {f"in_{n}": np.ascontiguousarray(inputs[n]) for n in INPUTS} | constants()
    args = [nc.dram_tensor(n, a.shape, mybir.dt.from_np(a.dtype), kind="ExternalInput").ap() for n, a in arrays.items()]
    args.append(nc.dram_tensor("out_x", (BATCH, SEQ, E), f32, kind="ExternalOutput").ap())
    build(nc, *args)
    r = run_bass_kernel_spmd(nc, [arrays], core_ids=[0])
    return r.results[0]["out_x"]
```

```python
import concourse.bass as bass
from concourse import mybir
from contextlib import ExitStack

BATCH, SEQ, E = 2, 4096, 256
HEADS, D = 16, 16
P = 128
TOKENS = BATCH * SEQ
EG = E // P
TILE = 512
SUB = TILE // P
STEPS = SEQ // TILE
LN_EPS = 1e-5
FH, KD, TOPK, KEYS = 8, 128, 8, 64
QG = 2 * FH
QC = QG * KD
SIMS = QG * KEYS
EHI, ELO = 128, 32
CAND = 20
EXP_AT = 6
TURN_AT = 4
XSCALE = 1024.0
PSCALE = 16384.0
GSCALE = 2.0 ** -24
SIM_STEPS = 14
ROUNDER = 1.5 * 2.0 ** 23
SMALLEST = 2.0 ** -100
SUBTILES = TOKENS // P

f32 = mybir.dt.float32
f16 = mybir.dt.float16
bf16 = mybir.dt.bfloat16
u32 = mybir.dt.uint32
ALU = mybir.AluOpType
ACT = mybir.ActivationFunctionType
AX = mybir.AxisListType

PP_STEPS = 13
QUAD = 32
UNITS = EG * D
NS = 8
NPROD = 4
LAG = 3


def inner(ap, n):
    if len(ap.shape) == 2:
        return ap.rearrange("p (a o) -> p a o", o=1).broadcast_to([ap.shape[0], ap.shape[1], n])
    return ap.rearrange("p a (b o) -> p a b o", o=1).broadcast_to([*ap.shape, n])


def pairs(eng, dst, a, b):
    eng.tensor_tensor(dst[:, :, 0:8], inner(a[:, :, 0], 8), b[:, :, 0:8], ALU.add)
    eng.tensor_tensor(dst[:, :, 8:12], inner(a[:, :, 1], 4), b[:, :, 0:4], ALU.add)
    for r in (2, 3):
        eng.tensor_tensor(dst[:, :, 8 + 2 * r:10 + 2 * r], inner(a[:, :, r], 2), b[:, :, 0:2], ALU.add)
    eng.tensor_tensor(dst[:, :, 16:20], a[:, :, 4:8], inner(b[:, :, 0], 4), ALU.add)


def attention(nc, x, wq, wk, wv, wo, wf1, wf2, wg1, wg2, norm_w, c_ident, c_sel, c_red, c_bm, x1_dram, x2t_dram, cacc):
    x_v = x.rearrange("b (ts p) e -> b p ts e", p=P)
    x1_v = x1_dram.rearrange("(b ts p) e -> b p ts e", b=BATCH, p=P)
    x2t_v = x2t_dram.rearrange("m p k t -> p m k t")
    with ExitStack() as ctx:
        def sb(name, shape, dt=f32):
            return ctx.enter_context(nc.sbuf_tensor(name, shape, dt))

        def ps(name, shape):
            return ctx.enter_context(nc.psum_tensor(name, shape, f32))

        def sem(name):
            return ctx.enter_context(nc.semaphore(name))

        ident = sb("ident", [P, P])
        sel_f = sb("sel_f", [3 * QUAD, 4 * P])
        sel = sb("sel", [3 * QUAD, 4, P], bf16)
        red = sb("red", [P, D, P])
        bm = sb("bm", [P, P])
        w_q = sb("w_q", [P, EG, E])
        w_k = sb("w_k", [P, EG, E])
        w_v = sb("w_v", [P, EG, E])
        w_o = sb("w_o", [P, EG, E])
        w_low = sb("w_low", [P, EG, 48])
        w_up = sb("w_up", [48, E])
        nw = sb("nw", [P, EG])
        eps = sb("eps", [P, 1])
        mhalf = sb("mhalf", [P, SUB])
        x_in = sb("x_in", [P, SUB, E])
        x_res = sb("x_res", [P, SUB, E])
        st = sb("st", [P, SUB, 6])
        mv = sb("mv", [P, SUB, 2])
        veps = sb("veps", [P, SUB])
        rstd = sb("rstd", [P, SUB])
        xn = sb("xn", [P, SUB, E])
        xt = sb("xt", [P, EG, TILE])
        low = sb("low", [48, TILE])
        q_s = [sb(f"q_s{b}", [P, EG, TILE]) for b in range(BATCH)]
        k_s = [sb(f"k_s{b}", [P, EG, TILE]) for b in range(BATCH)]
        f_s = [sb(f"f_s{b}", [P, EG, TILE]) for b in range(BATCH)]
        g_s = [sb(f"g_s{b}", [P, EG, TILE]) for b in range(BATCH)]
        v_f = sb("v_f", [P, EG, TILE])
        v_r = sb("v_r", [P, EG, TILE])
        v_p = sb("v_p", [P, 3, EG, TILE], bf16)
        v_s = [sb(f"v_s{b}", [3 * QUAD, 4, EG, TILE], bf16) for b in range(BATCH)]
        kv = sb("kv", [P, 2, TILE])
        state = sb("state", [P, NS, TILE])
        prod = sb("prod", [P, NPROD, TILE])
        carry = [sb(f"carry{b}", [P, UNITS]) for b in range(BATCH)]
        og = sb("og", [P, EG * TILE])
        sq = sb("sq", [P, EG * TILE])
        x1 = sb("x1", [P, SUB, E])
        st2 = sb("st2", [P, SUB, 6])
        mv2 = sb("mv2", [P, SUB, 2])
        veps2 = sb("veps2", [P, SUB])
        rstd2 = sb("rstd2", [P, SUB])
        x2 = sb("x2", [P, SUB, E + 1])
        x2t = sb("x2t", [P, SUB, 2 * EG, P], f16)

        pp = [ps(f"pp{i}", [P, TILE]) for i in range(2)]
        vb = [ps(f"vb{i}", [P, TILE]) for i in range(2)]
        o_ps = ps("o_ps", [P, EG, TILE])
        pm = ps("pm", [P, EG, TILE])

        s_wload = sem("s_wload")
        s_const = sem("s_const")
        s_xin = sem("s_xin")
        s_xres = sem("s_xres")
        s_var = sem("s_var")
        s_rstd = sem("s_rstd")
        s_xn = sem("s_xn")
        s_ppfull = sem("s_ppfull")
        s_ppfree = sem("s_ppfree")
        s_vsplit = sem("s_vsplit")
        s_vs = sem("s_vs")
        s_vb = sem("s_vb")
        s_kv = sem("s_kv")
        s_scan = sem("s_scan")
        s_carry = sem("s_carry")
        s_prod = sem("s_prod")
        s_red = sem("s_red")
        s_og = sem("s_og")
        s_sq = sem("s_sq")
        s_ms = sem("s_ms")
        s_rms = sem("s_rms")
        s_ogn = sem("s_ogn")
        s_attn = sem("s_attn")
        s_x1 = sem("s_x1")
        s_var2 = sem("s_var2")
        s_rstd2 = sem("s_rstd2")
        s_x2 = sem("s_x2")
        s_x2tp = sem("s_x2tp")
        s_x2h = sem("s_x2h")
        s_x2t = sem("s_x2t")
        s_cov = sem("s_cov")
        s_cacc = sem("s_cacc")
        s_x1st = sem("s_x1st")
        s_x2st = sem("s_x2st")
        s_step = sem("s_step")
        s_lns = sem("s_lns")

        CARRIES = UNITS // 4
        STACKED = 12 * 16

        def none_before(n):
            return isinstance(n, int) and n == 0
        WLOADS = 13

        def passes(eng, body):
            body(0, True, False)
            with eng.Fori(1, STEPS - 1) as it:
                body(it, False, False)
            body(STEPS - 1, False, True)

        block = ctx.enter_context(nc.Block())

        @block.sync
        def _(sp):
            for dst, src in ((ident[:], c_ident), (sel_f[:], c_sel), (red[:].rearrange("p a b -> p (a b)"), c_red),
                             (bm[:], c_bm)):
                sp.dma_start(dst, src).then_inc(s_wload, 16)
            for dst, src in ((w_q, wq), (w_k, wk), (w_v, wv), (w_o, wo)):
                sp.dma_start(dst[:], src.rearrange("(c p) n -> p c n", p=P)).then_inc(s_wload, 16)
            sp.dma_start(nw[:], norm_w.rearrange("(c p) -> p c", p=P), allow_slow_non_contiguous=True).then_inc(s_wload, 16)
            sp.wait_ge(s_const, 1)
            sp.dma_start(w_low[:, :, 0:16], wf1.rearrange("(c p) n -> p c n", p=P)).then_inc(s_wload, 16)
            sp.dma_start(w_low[:, :, 32:48], wg1.rearrange("(c p) n -> p c n", p=P)).then_inc(s_wload, 16)
            sp.dma_start(w_up[0:16, :], wf2).then_inc(s_wload, 16)
            sp.dma_start(w_up[32:48, :], wg2).then_inc(s_wload, 16)

            def load_in(n, it, b):
                if not none_before(n):
                    sp.wait_ge(s_xn, n)
                sp.dma_start(x_in[:], x_v[b, :, bass.ds(it * SUB, SUB), :]).then_inc(s_xin, 16)

            def load_res(n, it, b):
                if not none_before(n):
                    sp.wait_ge(s_x1, n)
                sp.dma_start(x_res[:], x_v[b, :, bass.ds(it * SUB, SUB), :]).then_inc(s_xres, 16)

            def store(n, it, b):
                sp.wait_ge(s_x2t, n + 1)
                sp.dma_start(x2t_v[:, bass.ds(it * SUB + b * (SEQ // P), SUB), :, :], x2t[:]).then_inc(s_x2st, 16)
                sp.dma_start(x1_v[b, :, bass.ts(it, SUB), :], x1[:]).then_inc(s_x1st, 16)

            def stack(n, b):
                if not (isinstance(n, int) and n < 2):
                    sp.wait_ge(s_vb, (n - 1) * UNITS)
                sp.wait_ge(s_vsplit, n + 1)
                for q in range(4):
                    for part in range(3):
                        sp.dma_start(v_s[b][part * QUAD:(part + 1) * QUAD, q], v_p[q * QUAD:(q + 1) * QUAD, part]).then_inc(s_vs, 16)

            load_in(0, 0, 0)
            load_in(1, 0, 1)
            stack(0, 0)

            def body(it, first, last):
                n = it * 2
                if not last:
                    load_in(n + 2, it + 1, 0)
                load_res(n, it, 0)
                stack(n + 1, 1)
                if not first:
                    store(n - 1, it - 1, 1)
                if not last:
                    load_in(n + 3, it + 1, 1)
                load_res(n + 1, it, 1)
                if not last:
                    stack(n + 2, 0)
                store(n, it, 0)

            passes(sp, body)
            store(2 * STEPS - 1, STEPS - 1, 1)
            sp.wait_ge(s_x1st, 32 * STEPS)
            sp.wait_ge(s_x2st, 32 * STEPS)

        @block.gpsimd
        def _(pool):
            nc.gpsimd.memset(w_low[:], 0.0).then_inc(s_const, 1)
            nc.gpsimd.memset(mhalf[:], -0.5)
            nc.gpsimd.memset(eps[:], LN_EPS)
            for b in range(BATCH):
                nc.gpsimd.memset(carry[b][:], 0.0)
            nc.gpsimd.memset(cacc[:], 0.0)
            nc.gpsimd.memset(x2[:, :, E:E + 1], 1.0)
            pool.drain().then_inc(s_const, 1)

            def head_rstd(n):
                pool.wait_ge(s_var, n + 1)
                nc.gpsimd.tensor_tensor(rstd[:], veps[:], mhalf[:], ALU.pow).then_inc(s_rstd, 1)

            def tail_rstd(n):
                pool.wait_ge(s_var2, n + 1)
                nc.gpsimd.tensor_tensor(rstd2[:], veps2[:], mhalf[:], ALU.pow).then_inc(s_rstd2, 1)

            def heavy(n, b, tail, head):
                for u in range(UNITS):
                    pool.wait_ge(s_scan, n * UNITS + u + 1)
                    if u >= NPROD or not none_before(n):
                        pool.wait_ge(s_red, n * UNITS + u - NPROD + 1)
                    nc.gpsimd.tensor_tensor(prod[:, u % NPROD, :], state[:, u % NS, :], q_s[b][:, u // D, :],
                                            ALU.mult).then_inc(s_prod, 1)
                    if head and u == 1:
                        head_rstd(n + 1)
                    if tail and u == 14:
                        tail_rstd(n - 1)

            head_rstd(0)

            def body(it, first, last):
                heavy(it * 2, 0, not first, True)
                heavy(it * 2 + 1, 1, True, not last)

            passes(pool, body)
            tail_rstd(2 * STEPS - 1)

        @block.scalar
        def _(act):
            def evac(n, b, step, out, func):
                act.wait_ge(s_ppfull, n * PP_STEPS + step + 1)
                nc.scalar.activation(out, pp[(b * PP_STEPS + step) % 2][0:out.shape[0], :], func).then_inc(s_ppfree, 1)

            def turned(n, b):
                for c in range(EG):
                    evac(n, b, c, xt[:, c, :], ACT.Copy)

            def values(n, b):
                if not none_before(n):
                    act.wait_ge(s_vsplit, n)
                for g in range(EG):
                    evac(n, b, 2 + g, v_f[:, g, :], ACT.Copy)
                evac(n, b, 4, low[:], ACT.Copy)

            def query(n, b, g):
                evac(n, b, 5 + g, q_s[b][:, g, :], ACT.Silu)

            def keys_gates(n, b):
                for g in range(EG):
                    evac(n, b, 7 + g, k_s[b][:, g, :], ACT.Silu)
                for g in range(EG):
                    evac(n, b, 9 + g, f_s[b][:, g, :], ACT.Sigmoid)
                for g in range(EG):
                    evac(n, b, 11 + g, g_s[b][:, g, :], ACT.Sigmoid)

            def tail_sq(n, g):
                act.wait_ge(s_og, n * EG + g + 1)
                ts = slice(g * TILE, (g + 1) * TILE)
                nc.scalar.activation(sq[:, ts], og[:, ts], ACT.Square).then_inc(s_sq, 1)

            def tail_rms(n):
                act.wait_ge(s_ms, n + 1)
                nc.scalar.activation(sq[:], pm[:].rearrange("p c t -> p (c t)"), ACT.Ln, bias=eps[:, 0:1]).then_inc(s_lns, 1)
                act.wait_ge(s_lns, n + 1)
                nc.scalar.activation(sq[:], sq[:], ACT.Exp, scale=-0.5).then_inc(s_rms, 1)

            def tail_x2t(n):
                act.wait_ge(s_x2tp, n + 1)
                if not none_before(n):
                    act.wait_ge(s_x2st, n * 16)
                for c in range(EG):
                    i = nc.scalar.activation(x2t[:, :, c, :], pm[:, c, :].rearrange("p (s t) -> p s t", t=P), ACT.Copy,
                                             scale=XSCALE)
                i.then_inc(s_x2h, 1)

            def during(n, b, tail, head):
                if tail:
                    tail_sq(n - 1, 1)
                if head:
                    turned(n + 1, 1 - b)
                if tail:
                    tail_rms(n - 1)
                if head:
                    values(n + 1, 1 - b)
                    query(n + 1, 1 - b, 0)
                tail_sq(n, 0)
                if tail:
                    tail_x2t(n - 1)
                if head:
                    query(n + 1, 1 - b, 1)
                    keys_gates(n + 1, 1 - b)

            act.wait_ge(s_const, 2)
            turned(0, 0)
            values(0, 0)
            query(0, 0, 0)
            query(0, 0, 1)
            keys_gates(0, 0)

            def body(it, first, last):
                n = it * 2
                during(n, 0, not first, True)
                during(n + 1, 1, True, not last)

            passes(act, body)
            tail_sq(2 * STEPS - 1, 1)
            tail_rms(2 * STEPS - 1)
            tail_x2t(2 * STEPS - 1)

        @block.vector
        def _(dve):
            dve.wait_ge(s_const, 2)
            dve.wait_ge(s_wload, 16 * WLOADS)
            nc.vector.tensor_copy(sel[:].rearrange("p a b -> p (a b)"), sel_f[:])
            for c in range(EG):
                nc.vector.tensor_scalar(w_o[:, c, :], w_o[:, c, :], nw[:, c:c + 1], None, ALU.mult)
            dve.drain().then_inc(s_step, 1)

            def head_stats(n):
                dve.wait_ge(s_xin, n * 16 + 16)
                for s in range(SUB):
                    nc.vector.bn_stats(st[:, s, :], x_in[:, s, :])
                dve.drain()
                for s in range(SUB):
                    nc.vector.bn_aggr(mv[:, s, :], st[:, s, :])
                dve.drain()
                nc.vector.tensor_scalar(veps[:], mv[:, :, 1], LN_EPS, None, ALU.add).then_inc(s_var, 1)

            def head_norm(n):
                dve.wait_ge(s_rstd, n + 1)
                if not none_before(n):
                    dve.wait_ge(s_ppfull, (n - 1) * PP_STEPS + 2)
                for s in range(SUB):
                    i = nc.vector.tensor_scalar(xn[:, s, :], x_in[:, s, :], mv[:, s, 0:1], rstd[:, s:s + 1],
                                                ALU.subtract, ALU.mult)
                i.then_inc(s_xn, 1)

            def head_split(n):
                if not none_before(n):
                    dve.wait_ge(s_vs, n * STACKED)
                dve.wait_ge(s_ppfree, n * PP_STEPS + 4)
                nc.vector.tensor_copy(v_p[:, 0], v_f[:])
                dve.drain()
                nc.vector.tensor_tensor(v_r[:], v_f[:], v_p[:, 0], ALU.subtract)

            def head_split_rest(n):
                dve.drain()
                nc.vector.tensor_copy(v_p[:, 1], v_r[:])
                dve.drain()
                nc.vector.tensor_tensor(v_p[:, 2], v_r[:], v_p[:, 1], ALU.subtract).then_inc(s_vsplit, 1)

            def tail_gate(n, b, g):
                dve.wait_ge(s_red, n * UNITS + (g + 1) * D)
                dve.wait_ge(s_ppfree, n * PP_STEPS + PP_STEPS)
                nc.vector.tensor_tensor(og[:, g * TILE:(g + 1) * TILE], o_ps[:, g, :], g_s[b][:, g, :], ALU.mult).then_inc(s_og, 1)

            def tail_ogn(n):
                dve.wait_ge(s_rms, n + 1)
                nc.vector.tensor_tensor(og[:], og[:], sq[:], ALU.mult).then_inc(s_ogn, 1)

            def tail_x1(n):
                dve.wait_ge(s_attn, n + 1)
                dve.wait_ge(s_xres, n * 16 + 16)
                if not none_before(n):
                    dve.wait_ge(s_x1st, n * 16)
                nc.vector.tensor_tensor(x1[:].rearrange("p s e -> p (s e)"), pm[:].rearrange("p c t -> p (c t)"),
                                        x_res[:].rearrange("p s e -> p (s e)"), ALU.add).then_inc(s_x1, 1)

            def tail_stats(n):
                dve.drain()
                for s in range(SUB):
                    nc.vector.bn_stats(st2[:, s, :], x1[:, s, :])
                dve.drain()
                for s in range(SUB):
                    nc.vector.bn_aggr(mv2[:, s, :], st2[:, s, :])
                dve.drain()
                nc.vector.tensor_scalar(veps2[:], mv2[:, :, 1], LN_EPS, None, ALU.add).then_inc(s_var2, 1)

            def tail_norm(n):
                dve.wait_ge(s_rstd2, n + 1)
                for s in range(SUB):
                    i = nc.vector.tensor_scalar(x2[:, s, 0:E], x1[:, s, :], mv2[:, s, 0:1], rstd2[:, s:s + 1],
                                                ALU.subtract, ALU.mult)
                i.then_inc(s_x2, 1)

            def tail_low(n):
                dve.wait_ge(s_x2h, n + 1)
                for c in range(EG):
                    i = nc.vector.scalar_tensor_tensor(x2t[:, :, EG + c, :], pm[:, c, :].rearrange("p (s t) -> p s t", t=P), XSCALE,
                                                       x2t[:, :, c, :], ALU.mult, ALU.subtract)
                i.then_inc(s_x2t, 1)

            def tail_cacc(n):
                dve.wait_ge(s_cov, n + 1)
                nc.vector.tensor_tensor(cacc[:], pm[:, :, 0:E + 1], cacc[:], ALU.add).then_inc(s_cacc, 1)

            def kv_mult(n, b, u):
                dve.wait_ge(s_vb, n * UNITS + u + 1)
                if u >= 2 or not none_before(n):
                    dve.wait_ge(s_scan, n * UNITS + u - 1)
                nc.vector.tensor_tensor(kv[:, u % 2, :], vb[u % 2][:], k_s[b][:, u // D, :], ALU.mult).then_inc(s_kv, 1)

            def scan(n, b, u):
                dve.wait_ge(s_kv, n * UNITS + u + 1)
                if u >= NS or not none_before(n):
                    dve.wait_ge(s_prod, n * UNITS + u - NS + 1)
                    dve.wait_ge(s_carry, n * CARRIES + (u - NS) // 4 + 1)
                nc.vector.tensor_tensor_scan(state[:, u % NS, :], f_s[b][:, u // D, :], kv[:, u % 2, :],
                                             carry[b][:, u:u + 1], ALU.mult, ALU.add).then_inc(s_scan, 1)

            def save_carry(n, b, j):
                dve.wait_ge(s_scan, n * UNITS + 4 * j + 4)
                u = 4 * j
                nc.vector.tensor_copy(carry[b][:, u:u + 4], state[:, u % NS:u % NS + 4, TILE - 1]).then_inc(s_carry, 1)

            def heavy(n, b, tail, head):
                dve.wait_ge(s_ppfree, n * PP_STEPS + 11)
                kv_mult(n, b, 0)
                for u in range(UNITS):
                    if u + 1 < UNITS:
                        kv_mult(n, b, u + 1)
                    scan(n, b, u)
                    if u % 4 == 0 and u:
                        save_carry(n, b, u // 4 - 1)
                    if head and u == 0:
                        head_stats(n + 1)
                    if tail and u == 2:
                        tail_gate(n - 1, 1 - b, 1)
                    if head and u == 3:
                        head_norm(n + 1)
                    if tail and u == 7:
                        tail_ogn(n - 1)
                    if tail and u == 12:
                        tail_x1(n - 1)
                    if tail and u == 13:
                        tail_stats(n - 1)
                    if tail and u == 15:
                        tail_norm(n - 1)
                    if head and u == 16:
                        head_split(n + 1)
                    if head and u == 17:
                        head_split_rest(n + 1)
                    if u == 19:
                        tail_gate(n, b, 0)
                    if tail and u == 20:
                        tail_low(n - 1)
                    if tail and u == 27:
                        tail_cacc(n - 1)
                save_carry(n, b, CARRIES - 1)

            head_stats(0)
            head_norm(0)
            head_split(0)
            head_split_rest(0)

            def body(it, first, last):
                heavy(it * 2, 0, not first, True)
                heavy(it * 2 + 1, 1, True, not last)

            passes(dve, body)
            n = 2 * STEPS - 1
            tail_gate(n, 1, 1)
            tail_ogn(n)
            tail_x1(n)
            tail_stats(n)
            tail_norm(n)
            tail_low(n)
            tail_cacc(n)

        @block.tensor
        def _(pe):
            pe.wait_ge(s_wload, 16 * WLOADS)
            pe.wait_ge(s_step, 1)

            def pp_bank(n, b, step):
                if step >= 2 or not none_before(n):
                    pe.wait_ge(s_ppfree, n * PP_STEPS + step - 1)
                return pp[(b * PP_STEPS + step) % 2]

            def head(n, b, step, halves=(0, 1)):
                bank = pp_bank(n, b, step) if 0 in halves else pp[(b * PP_STEPS + step) % 2]
                if step < 2:
                    pe.wait_ge(s_xn, n + 1)
                    for s in range(SUB):
                        i = nc.tensor.transpose(bank[:, s * P:(s + 1) * P], xn[:, s, step * P:(step + 1) * P], ident[:])
                elif step < 9:
                    if step == 2:
                        pe.wait_ge(s_ppfree, n * PP_STEPS + 2)
                    w = w_v if step < 4 else w_low if step == 4 else w_q if step < 7 else w_k
                    g = step - (2 if step < 4 else 4 if step == 4 else 5 if step < 7 else 7)
                    cols = slice(0, 48) if step == 4 else slice(g * P, (g + 1) * P)
                    for c in halves:
                        i = nc.tensor.matmul(bank[0:cols.stop - cols.start, :], w[:, c, cols], xt[:, c, :], start=c == 0,
                                             stop=c == EG - 1)
                else:
                    if step == 9:
                        pe.wait_ge(s_ppfree, n * PP_STEPS + 5)
                    g = (step - 9) % EG
                    r = 0 if step < 11 else 32
                    i = nc.tensor.matmul(bank[:], w_up[r:r + 16, g * P:(g + 1) * P], low[r:r + 16, :], start=True, stop=True)
                if 1 in halves:
                    i.then_inc(s_ppfull, 1)

            def tail_ms(n, g):
                pe.wait_ge(s_sq, n * EG + g + 1)
                if g == 0 and not none_before(n):
                    pe.wait_ge(s_cacc, n)
                i = nc.tensor.matmul(pm[:, g, :], bm[:], sq[:, g * TILE:(g + 1) * TILE], start=True, stop=True)
                if g == EG - 1:
                    i.then_inc(s_ms, 1)

            def tail_wo(n, s):
                if s == 0:
                    pe.wait_ge(s_ogn, n + 1)
                pmv = pm[:].rearrange("p c (s e) -> p (c s) e", e=E)
                for g in range(EG):
                    i = nc.tensor.matmul(pmv[:, s, :], og[:, g * TILE + s * P:g * TILE + (s + 1) * P], w_o[:, g, :],
                                         start=g == 0, stop=g == EG - 1)
                if s == SUB - 1:
                    i.then_inc(s_attn, 1)

            def tail_x2t(n):
                pe.wait_ge(s_x2, n + 1)
                for c in range(EG):
                    for s in range(SUB):
                        i = nc.tensor.transpose(pm[:, c, s * P:(s + 1) * P], x2[:, s, c * P:(c + 1) * P], ident[:])
                i.then_inc(s_x2tp, 1)

            def tail_cov(n, c, half):
                if c == 0 and half == 0:
                    pe.wait_ge(s_x2t, n + 1)
                for s in (2 * half, 2 * half + 1):
                    i = nc.tensor.matmul(pm[:, c, 0:E + 1], x2[:, s, c * P:(c + 1) * P], x2[:, s, :],
                                         start=s == 0, stop=s == SUB - 1)
                if c == EG - 1 and half == 1:
                    i.then_inc(s_cov, 1)

            def spread(n, b, u):
                if u >= 2 or not none_before(n):
                    pe.wait_ge(s_kv, n * UNITS + u - 1)
                nc.tensor.matmul(vb[u % 2][:], sel[:, u % 4, :], v_s[b][:, u % D // 4, u // D, :], start=True,
                                 stop=True).then_inc(s_vb, 1)

            def reduce(n, u):
                pe.wait_ge(s_prod, n * UNITS + u + 1)
                if u % D == 0 and not (u == 0 and none_before(n)):
                    if not none_before(n):
                        pe.wait_ge(s_og, n * EG - 1 + u // D)
                nc.tensor.matmul(o_ps[:, u // D, :], red[:, u % D, :], prod[:, u % NPROD, :],
                                 start=u % D == 0, stop=u % D == D - 1).then_inc(s_red, 1)

            def heavy(n, b, tail, head_next):
                pe.wait_ge(s_vs, n * STACKED + STACKED)
                for u in range(UNITS):
                    spread(n, b, u)
                    if u >= LAG:
                        reduce(n, u - LAG)
                    if tail:
                        if u in (5, 6):
                            tail_ms(n - 1, u - 5)
                        if 8 <= u < 8 + SUB:
                            tail_wo(n - 1, u - 8)
                        if u == 17:
                            tail_x2t(n - 1)
                        if 22 <= u < 26:
                            tail_cov(n - 1, (u - 22) // 2, (u - 22) % 2)
                    if head_next:
                        if u in (4, 5):
                            head(n + 1, 1 - b, u - 4)
                        if u in (7, 8):
                            head(n + 1, 1 - b, 2, (u - 7,))
                        if 12 <= u < 24:
                            head(n + 1, 1 - b, 3 + (u - 12) // 2, ((u - 12) % 2,))
                        if 24 <= u < 28:
                            head(n + 1, 1 - b, 9 + u - 24)
                for v in range(UNITS - LAG, UNITS):
                    reduce(n, v)

            for step in range(PP_STEPS):
                head(0, 0, step)

            def body(it, first, last):
                heavy(it * 2, 0, not first, True)
                heavy(it * 2 + 1, 1, True, not last)

            passes(pe, body)
            n = 2 * STEPS - 1
            for g in range(EG):
                tail_ms(n, g)
            for s in range(SUB):
                tail_wo(n, s)
            tail_x2t(n)
            for c in range(EG):
                for half in range(2):
                    tail_cov(n, c, half)


def fold(nc, fw_q, gamma, beta, keys, down, up, c_ident, c_iota, c_iotac, cacc, res):
    m_w, m_c, ones3, ident, down_t, up_s, iota, iotac, scl = res
    with ExitStack() as ctx:
        def sb(name, shape, dt=f32):
            return ctx.enter_context(nc.sbuf_tensor(name, shape, dt))

        def ps(name, shape):
            return ctx.enter_context(nc.psum_tensor(name, shape, f32))

        def sem(name):
            return ctx.enter_context(nc.semaphore(name))

        fq = sb("fq", [P, EG, QC])
        kn = sb("kn", [KEYS, FH, 2, KD])
        kt = sb("kt", [P, QG, KEYS])
        kts = sb("kts", [P, QG, KEYS])
        wt = sb("wt", [P, QG, E])
        yw = sb("yw", [P, 2, 2, E])
        gam = sb("gam", [P, QG])
        bet = sb("bet", [P, QG])
        stage = sb("stage", [P, ELO, E])
        mcol = sb("mcol", [P, EG])
        mrow = sb("mrow", [1, E])
        cc = sb("cc", [P, EG, E])
        var = sb("var", [P, QG])
        mean = sb("mean", [P, QG])
        mh = sb("mh", [P, QG])
        s_bn = sb("s_bn", [P, QG])
        cst = sb("cst", [P, QG])
        cst3 = sb("cst3", [P, QG, 3])
        mf = sb("mf", [P, EG, SIMS])
        cf = sb("cf", [3, SIMS])
        cr = sb("cr", [3, SIMS])
        c1 = sb("c1", [3, SIMS], bf16)
        c2 = sb("c2", [3, SIMS], bf16)
        c3 = sb("c3", [3, SIMS], bf16)
        io_f = sb("io_f", [P, EHI * 16])
        ioc_f = sb("ioc_f", [P, CAND * TOPK])
        mx = sb("mx", [P, 4])
        mx1 = sb("mx1", [1, 4])
        e1 = sb("e1", [1, 4], u32)
        onesr = sb("onesr", [1, P])

        bank = [ps(f"fb{i}", [P, 512]) for i in range(4)]
        ps_mx = ps("ps_mx", [P, 512])

        s_ld = sem("f_ld")
        s_pe = sem("f_pe")
        s_ev = sem("f_ev")
        s_v = sem("f_v")
        s_pw = sem("f_pw")
        s_dn = sem("f_dn")
        s_up = sem("f_up")
        s_de = sem("f_de")
        s_dh = sem("f_dh")
        s_dl = sem("f_dl")
        s_id = sem("f_id")
        s_mx = sem("f_mx")
        s_mt = sem("f_mt")
        s_sc = sem("f_sc")
        s_bc = sem("f_bc")
        s_ds = sem("f_ds")
        s_sb = sem("f_sb")
        s_uh = sem("f_uh")
        s_us = sem("f_us")
        s_mh = sem("f_mh")
        s_ms = sem("f_ms")
        block = ctx.enter_context(nc.Block())

        LOADS = 6
        NKEYT = QG // 8
        NWT = QG // 2
        NDT = EG * ELO // 4

        @block.sync
        def _(sp):
            sp.dma_start(stage[:], down.rearrange("(p l) c -> p l c", l=ELO)).then_inc(s_dn, 16)
            sp.dma_start(ident[:], c_ident).then_inc(s_id, 16)
            sp.dma_start(fq[:], fw_q.rearrange("(c p) n -> p c n", p=P)).then_inc(s_ld, 16)
            sp.dma_start(kn[:], keys.rearrange("h k p d -> k h p d")).then_inc(s_ld, 16)
            sp.dma_start(gam[:], gamma.rearrange("(g p) -> p g", p=P), allow_slow_non_contiguous=True).then_inc(s_ld, 16)
            sp.dma_start(bet[:], beta.rearrange("(g p) -> p g", p=P), allow_slow_non_contiguous=True).then_inc(s_ld, 16)
            sp.dma_start(io_f[:], c_iota).then_inc(s_ld, 16)
            sp.dma_start(ioc_f[:], c_iotac).then_inc(s_ld, 16)
            sp.wait_ge(s_de, NDT)
            sp.dma_start(stage[:], up.rearrange("(p l) c -> p l c", l=ELO)).then_inc(s_up, 16)

        @block.gpsimd
        def _(pool):
            nc.gpsimd.memset(mh[:], -0.5).then_inc(s_pw, 1)
            pool.wait_ge(s_pw, 1)
            pool.wait_ge(s_v, 3)
            nc.gpsimd.tensor_tensor(s_bn[:], var[:], mh[:], ALU.pow).then_inc(s_pw, 1)

        @block.scalar
        def _(act):
            for j in range(NDT):
                act.wait_ge(s_de, j + 1)
                c, l4 = j % EG, j // EG
                nc.scalar.activation(down_t[:, 0, c, l4 * 4:l4 * 4 + 4, :].rearrange("p a b -> p (a b)"),
                                     bank[2 + j % 2][:], ACT.Copy).then_inc(s_dh, 1)
            act.wait_ge(s_us, 1)
            nc.scalar.activation(up_s[:, 0], stage[:], ACT.Copy).then_inc(s_uh, 1)
            act.wait_ge(s_ms, 1)
            nc.scalar.activation(m_w[:, 0], mf[:], ACT.Copy).then_inc(s_mh, 1)

        @block.tensor
        def _(pe):
            step = [0]

            def take(i):
                i.then_inc(s_pe, 1)
                step[0] += 1

            def free():
                if step[0] >= 2:
                    pe.wait_ge(s_ev, step[0] - 1)
                return bank[step[0] % 2]

            def largest(k):
                pe.wait_ge(s_mx, k + 1)
                nc.tensor.transpose(ps_mx[0:1, 0:P], mx[:, 2:3], ident[:]).then_inc(s_mt, 1)
                pe.wait_ge(s_sc, k + 1)
                nc.tensor.matmul(ps_mx[:, 256:258], onesr[:], mx1[:, 2:4], start=True, stop=True).then_inc(s_bc, 1)

            pe.wait_ge(s_id, 16)
            largest(0)
            pe.wait_ge(s_ld, 16 * LOADS)
            for j in range(NKEYT):
                b = free()
                for i in range(8):
                    g = j * 8 + i
                    last = nc.tensor.transpose(b[:, i * KEYS:(i + 1) * KEYS], kn[:, g % FH, g // FH, :], ident[0:KEYS, 0:KEYS])
                take(last)
            for j in range(NWT):
                b = free()
                for i in range(4):
                    g, c = j * 2 + i // 2, i % 2
                    last = nc.tensor.transpose(b[:, i * P:(i + 1) * P], fq[:, c, g * KD:(g + 1) * KD], ident[:])
                take(last)
            pe.wait_ge(s_ds, 1)
            for j in range(NDT):
                c, l4 = j % EG, j // EG
                if j >= 2:
                    pe.wait_ge(s_dl, j - 1)
                for i in range(4):
                    last = nc.tensor.transpose(bank[2 + j % 2][:, i * P:(i + 1) * P], stage[:, l4 * 4 + i, c * P:(c + 1) * P], ident[:])
                last.then_inc(s_de, 1)
            pe.wait_ge(s_v, 1)
            b = free()
            for c in range(EG):
                last = nc.tensor.transpose(b[0:1, c * P:(c + 1) * P], mcol[:, c:c + 1], ident[:])
            take(last)
            pe.wait_ge(s_ev, step[0])
            b = free()
            for c in range(EG):
                last = nc.tensor.matmul(b[:, c * E:(c + 1) * E], mrow[0:1, c * P:(c + 1) * P], mrow[0:1, :], start=True, stop=True)
            take(last)
            pe.wait_ge(s_v, 2)
            for j in range(NWT):
                b = free()
                for i in range(2):
                    g = j * 2 + i
                    for c in range(EG):
                        last = nc.tensor.matmul(b[:, i * E:(i + 1) * E], fq[:, c, g * KD:(g + 1) * KD], cc[:, c, :],
                                                start=c == 0, stop=c == EG - 1)
                take(last)
            b = free()
            for g in range(QG):
                for c in range(EG):
                    last = nc.tensor.matmul(b[:, g:g + 1], fq[:, c, g * KD:(g + 1) * KD], mcol[:, c:c + 1],
                                            start=c == 0, stop=c == EG - 1)
            take(last)
            pe.wait_ge(s_v, 4)
            for j in range(4):
                b = free()
                c, half = j % EG, j // EG
                for i in range(8):
                    g = half * 8 + i
                    last = nc.tensor.matmul(b[:, i * KEYS:(i + 1) * KEYS], wt[:, g, c * P:(c + 1) * P], kts[:, g, :],
                                            start=True, stop=True)
                take(last)
            for half in range(2):
                b = free()
                for i in range(8):
                    g = half * 8 + i
                    last = nc.tensor.matmul(b[0:3, i * KEYS:(i + 1) * KEYS], cst3[:, g, :], kt[:, g, :], start=True, stop=True)
                take(last)
            largest(1)
            largest(2)

        @block.vector
        def _(dve):
            step = [0]

            def full():
                dve.wait_ge(s_pe, step[0] + 1)
                step[0] += 1
                return bank[(step[0] - 1) % 2]

            def scale(k, matrix):
                nc.vector.tensor_reduce(mx[:, 0:1], matrix, AX.X, ALU.max)
                nc.vector.tensor_reduce(mx[:, 1:2], matrix, AX.X, ALU.min)
                dve.drain()
                nc.vector.scalar_tensor_tensor(mx[:, 2:3], mx[:, 1:2], -1.0, mx[:, 0:1], ALU.mult, ALU.max).then_inc(s_mx, 1)
                dve.wait_ge(s_mt, k + 1)
                nc.vector.tensor_reduce(mx1[0:1, 0:1], ps_mx[0:1, 0:P], AX.X, ALU.max)
                dve.drain()
                nc.vector.tensor_scalar(mx1[0:1, 1:2], mx1[0:1, 0:1], SMALLEST, None, ALU.max)
                dve.drain()
                nc.vector.tensor_scalar(e1[0:1, 0:1], mx1[0:1, 1:2].bitcast(u32), 0x7F800000, None, ALU.bitwise_and)
                dve.drain()
                nc.vector.tensor_scalar(mx1[0:1, 2:3].bitcast(u32), e1[0:1, 0:1], -1.0, float((2 * 127 + 13) << 23), ALU.mult, ALU.add)
                nc.vector.tensor_scalar(mx1[0:1, 3:4].bitcast(u32), e1[0:1, 0:1], float(13 << 23), None, ALU.subtract)
                dve.drain().then_inc(s_sc, 1)
                dve.wait_ge(s_bc, k + 1)
                nc.vector.tensor_copy(scl[:, 2 * k:2 * k + 2], ps_mx[:, 256:258])
                dve.drain()

            nc.vector.memset(onesr[:], 1.0)
            dve.wait_ge(s_dn, 16)
            scale(0, stage[:].rearrange("p a b -> p (a b)"))
            nc.vector.tensor_scalar(stage[:], stage[:], scl[:, 0:1], None, ALU.mult).then_inc(s_ds, 1)
            nc.vector.tensor_scalar(mcol[:], cacc[:, :, E], 1.0 / TOKENS, None, ALU.mult).then_inc(s_v, 1)
            for j in range(NKEYT):
                nc.vector.tensor_copy(kt[:, j * 8:j * 8 + 8, :].rearrange("p a b -> p (a b)"), full()[:]).then_inc(s_ev, 1)
            for j in range(NWT):
                nc.vector.tensor_copy(wt[:, j * 2:j * 2 + 2, :].rearrange("p a b -> p (a b)"), full()[:]).then_inc(s_ev, 1)
            for j in range(NDT):
                dve.wait_ge(s_dh, j + 1)
                c, l4 = j % EG, j // EG
                nc.vector.tensor_tensor(down_t[:, 1, c, l4 * 4:l4 * 4 + 4, :].rearrange("p a b -> p (a b)"), bank[2 + j % 2][:],
                                        down_t[:, 0, c, l4 * 4:l4 * 4 + 4, :].rearrange("p a b -> p (a b)"),
                                        ALU.subtract).then_inc(s_dl, 1)
            nc.vector.tensor_copy(mrow[0:1, :], full()[0:1, 0:E]).then_inc(s_ev, 1)
            b = full()
            nc.vector.scalar_tensor_tensor(cc[:], cacc[:, :, 0:E], 1.0 / TOKENS,
                                           b[:, 0:EG * E].rearrange("p (c e) -> p c e", e=E),
                                           ALU.mult, ALU.subtract).then_inc(s_ev, 1)
            dve.drain().then_inc(s_v, 1)
            for j in range(NWT):
                nc.vector.tensor_tensor(yw[:, j % 2].rearrange("p a b -> p (a b)"), full()[:],
                                        wt[:, j * 2:j * 2 + 2, :].rearrange("p a b -> p (a b)"), ALU.mult).then_inc(s_ev, 1)
                dve.drain()
                nc.vector.tensor_reduce(var[:, j * 2:j * 2 + 2], yw[:, j % 2], AX.X, ALU.add)
            dve.drain()
            nc.vector.tensor_scalar(var[:], var[:], 0.0, LN_EPS, ALU.max, ALU.add).then_inc(s_v, 1)
            nc.vector.tensor_copy(mean[:], full()[:, 0:QG]).then_inc(s_ev, 1)
            dve.wait_ge(s_pw, 2)
            nc.vector.tensor_tensor(s_bn[:], s_bn[:], gam[:], ALU.mult)
            dve.drain()
            nc.vector.tensor_tensor(mean[:], mean[:], s_bn[:], ALU.mult)
            nc.vector.tensor_tensor(kts[:], kt[:], inner(s_bn[:], KEYS), ALU.mult)
            dve.drain()
            nc.vector.tensor_tensor(cst[:], bet[:], mean[:], ALU.subtract)
            dve.drain()
            nc.vector.tensor_copy(cst3[:], inner(cst[:], 3))
            dve.drain().then_inc(s_v, 1)
            for j in range(4):
                c, half = j % EG, j // EG
                nc.vector.tensor_copy(mf[:, c, half * 512:(half + 1) * 512], full()[:]).then_inc(s_ev, 1)
            for half in range(2):
                nc.vector.tensor_copy(cf[:, half * 512:(half + 1) * 512], full()[0:3, :]).then_inc(s_ev, 1)
            dve.drain()
            scale(1, mf[:].rearrange("p a b -> p (a b)"))
            nc.vector.tensor_scalar(mf[:], mf[:], scl[:, 2:3], None, ALU.mult).then_inc(s_ms, 1)
            nc.vector.tensor_scalar(cf[:], cf[:], scl[0:3, 2:3], XSCALE, ALU.mult, ALU.mult)
            dve.drain()
            nc.vector.tensor_copy(c1[:], cf[:])
            dve.drain()
            nc.vector.tensor_tensor(cr[:], cf[:], c1[:], ALU.subtract)
            dve.drain()
            nc.vector.tensor_copy(c2[:], cr[:])
            dve.drain()
            nc.vector.tensor_tensor(c3[:], cr[:], c2[:], ALU.subtract)
            nc.vector.tensor_scalar(m_c[:], c1[:], ident[0:3, 0:1], None, ALU.mult)
            dve.drain()
            nc.vector.scalar_tensor_tensor(m_c[:], c2[:], ident[0:3, 1:2], m_c[:], ALU.mult, ALU.add)
            dve.drain()
            nc.vector.scalar_tensor_tensor(m_c[:], c3[:], ident[0:3, 2:3], m_c[:], ALU.mult, ALU.add)
            nc.vector.memset(ones3[:], 1.0)
            nc.vector.tensor_copy(iota[:].rearrange("p a b -> p (a b)"), io_f[:])
            nc.vector.tensor_copy(iotac[:].rearrange("p a b -> p (a b)"), ioc_f[:])
            dve.wait_ge(s_up, 16)
            scale(2, stage[:].rearrange("p a b -> p (a b)"))
            nc.vector.tensor_scalar(stage[:], stage[:], scl[:, 4:5], None, ALU.mult).then_inc(s_us, 1)
            dve.wait_ge(s_mh, 1)
            nc.vector.tensor_tensor(m_w[:, 1], mf[:], m_w[:, 0], ALU.subtract)
            dve.wait_ge(s_uh, 1)
            nc.vector.tensor_tensor(up_s[:, 1], stage[:], up_s[:, 0], ALU.subtract)
            nc.vector.tensor_scalar(scl[:, 6:7], scl[:, 1:2], 1.0 / XSCALE, None, ALU.mult)
            nc.vector.tensor_scalar(scl[:, 7:8], scl[:, 3:4], 1.0 / XSCALE, None, ALU.mult)
            nc.vector.tensor_scalar(scl[:, 8:9], scl[:, 0:1], GSCALE, None, ALU.mult)
            nc.vector.scalar_tensor_tensor(scl[:, 9:10], scl[:, 1:2], 1.0 / (GSCALE * PSCALE), scl[:, 5:6], ALU.mult, ALU.mult)


def experts(nc, x1_dram, x2t_dram, out, res):
    m_w, m_c, ones3, ident, down_t, up_s, iota, iotac, scl = res
    x1_v = x1_dram.rearrange("(m p) e -> p m e", p=P)
    x2t_v = x2t_dram.rearrange("m p k t -> p m k t")
    with ExitStack() as ctx:
        def sb(name, shape, dt=f32):
            return ctx.enter_context(nc.sbuf_tensor(name, shape, dt))

        def ps(name, shape):
            return ctx.enter_context(nc.psum_tensor(name, shape, f32))

        def sem(name):
            return ctx.enter_context(nc.semaphore(name))

        xt = [sb(f"ext{i}", [P, 2, EG, P], f16) for i in range(2)]
        x1 = [sb(f"ex1{i}", [P, E]) for i in range(2)]
        y = [sb(f"ey{i}", [P, E]) for i in range(2)]
        held = sb("held", [P, 1])
        s8 = sb("s8", [P, QG, TOPK])
        i8 = sb("i8", [P, QG, TOPK], u32)
        ix = sb("ix", [P, FH, TOPK])
        iy = sb("iy", [P, FH, TOPK])
        cand = sb("cand", [P, FH, CAND])
        code = sb("code", [P, FH, CAND])
        top = sb("top", [P, FH, TOPK])
        pos = sb("pos", [P, FH, TOPK], u32)
        posh = sb("posh", [P, FH, TOPK], f16)
        oh = sb("oh", [P, FH, CAND, TOPK], f16)
        ohc = sb("ohc", [P, FH, CAND, TOPK])
        ex = sb("ex", [P, FH, TOPK])
        rs = sb("rs", [P, FH])
        held_p = sb("held_p", [P, 1])
        by_elo = sb("by_elo", [P, FH * TOPK])
        pf = sb("pf", [P, FH * TOPK])
        ph = sb("ph", [P, FH * TOPK], f16)
        ecode = sb("ecode", [P, FH * TOPK])
        eh = sb("eh", [P, FH * TOPK])
        el = sb("el", [P, FH * TOPK])
        rt = sb("rt", [P, 3, P])
        rtt = sb("rtt", [P, 3, P], f16)
        uh = sb("uh", [P, EHI, P], f16)
        vl = sb("vl", [P, ELO, P], f16)
        gh = [sb(f"gh{i}", [P, ELO, P]) for i in range(2)]
        gp = sb("gp", [P, 2, ELO, P], f16)

        ps_s = ps("ps_s", [P, SIMS])
        ps_h = [ps(f"ps_h{i}", [P, 512]) for i in range(2)]
        ps_a = [ps(f"ps_a{i}", [P, 16, ELO]) for i in range(2)]
        ps_t = ps("ps_t", [P, 512])
        ps_o = ps("ps_o", [P, 512])

        s_xt = [sem(f"e_xt{i}") for i in range(2)]
        s_x1 = [sem(f"e_x1{i}") for i in range(2)]
        s_st = [sem(f"e_st{i}") for i in range(2)]
        s_sim = sem("e_sim")
        s_simu = sem("e_simu")
        s_top = sem("e_top")
        s_exp = sem("e_exp")
        s_oh = sem("e_oh")
        s_ohc = sem("e_ohc")
        s_rt = sem("e_rt")
        s_tr = sem("e_tr")
        s_rtt = sem("e_rtt")
        s_v1 = sem("e_v1")
        s_vp = sem("e_vp")
        s_u1 = sem("e_u1")
        s_rs = sem("e_rs")
        s_ec = sem("e_ec")
        s_a = sem("e_a")
        s_g = sem("e_g")
        s_h = sem("e_h")
        s_gh = sem("e_gh")
        s_gp = sem("e_gp")
        s_gl = sem("e_gl")
        s_o = sem("e_o")
        s_y = sem("e_y")
        HG = ELO // 4
        AG = P // 16

        def passes(eng, body):
            body(0, True, False)
            with eng.Fori(1, SUBTILES // 2 - 1) as it:
                body(it, False, False)
            body(SUBTILES // 2 - 1, False, True)

        block = ctx.enter_context(nc.Block())

        @block.sync
        def _(sp):
            def load_xt(m, it, i, fresh):
                if not fresh:
                    sp.wait_ge(s_h, (m - 1) * HG)
                sp.dma_start(xt[i][:].rearrange("p a c t -> p (a c t)"), x2t_v[:, bass.ds(m, 1), :, :].rearrange("p m k t -> p (m k t)")).then_inc(s_xt[i], 16)

            def load_x1(m, it, i, fresh):
                if not fresh:
                    sp.wait_ge(s_y, m - 1)
                sp.dma_start(x1[i][:], x1_v[:, bass.ds(m, 1), :].rearrange("p m e -> p (m e)")).then_inc(s_x1[i], 16)

            def store(m, it, i):
                sp.wait_ge(s_y, m + 1)
                sp.dma_start(out[bass.ts(m, P), :], y[i][:]).then_inc(s_st[i], 16)

            load_xt(0, 0, 0, True)
            load_xt(1, 0, 1, True)
            load_x1(0, 0, 0, True)
            load_x1(1, 0, 1, True)

            def body(it, first, last):
                for i in range(2):
                    m = it * 2 + i
                    if not last:
                        load_xt(m + 2, it + 1, i, False)
                    if i == 1 or not first:
                        store(m - 1, it - 1 + i, 1 - i)
                        if i == 0 or not last:
                            load_x1(m + 1, it + i, 1 - i, False)

            passes(sp, body)
            store(SUBTILES - 1, SUBTILES // 2 - 1, 1)
            for i in range(2):
                sp.wait_ge(s_st[i], 16 * (SUBTILES // 2))

        @block.gpsimd
        def _(pool):
            def decode(m):
                pool.wait_ge(s_simu, m + 1)
                nc.gpsimd.tensor_tensor(held_p[:], by_elo[:, 0:1], by_elo[:, 0:1], ALU.mult)
                nc.gpsimd.tensor_scalar(ix[:], i8[:, 0:FH, :], float(KEYS), None, ALU.mult)
                nc.gpsimd.tensor_copy(iy[:], i8[:, FH:QG, :])
                pool.drain()
                pairs(nc.gpsimd, code, ix[:], iy[:])
                pool.drain()
                pool.wait_ge(s_oh, m + 1)
                nc.gpsimd.tensor_tensor(ohc[:], oh[:], inner(code[:], TOPK), ALU.mult).then_inc(s_ohc, 1)

            def parts(m, fresh):
                pool.wait_ge(s_rs, m + 1)
                nc.gpsimd.tensor_tensor(pf[:].rearrange("p (h k) -> p h k", k=TOPK), ex[:], inner(rs[:], TOPK), ALU.mult)
                pool.drain()
                nc.gpsimd.tensor_scalar(pf[:], pf[:], PSCALE, None, ALU.mult)
                pool.drain()
                nc.gpsimd.tensor_copy(ph[:], pf[:])
                pool.drain()
                if not fresh:
                    pool.wait_ge(s_tr, m)
                nc.gpsimd.tensor_tensor(rt[:, 2, 64:128], pf[:], ph[:], ALU.subtract)
                nc.gpsimd.tensor_copy(rt[:, 2, 0:64], ph[:])
                pool.wait_ge(s_ec, m + 1)
                nc.gpsimd.tensor_tensor(eh[:], ecode[:], by_elo[:], ALU.mult)
                pool.drain()
                nc.gpsimd.tensor_scalar(eh[:], eh[:], -(ELO - 1) / (2.0 * ELO), None, ALU.add)
                pool.drain()
                nc.gpsimd.tensor_scalar(eh[:], eh[:], ROUNDER, None, ALU.add)
                pool.drain()
                nc.gpsimd.tensor_scalar(eh[:], eh[:], -ROUNDER, None, ALU.add)
                pool.drain()
                nc.gpsimd.tensor_scalar(el[:], eh[:], float(ELO), None, ALU.mult)
                pool.drain()
                for part in range(2):
                    nc.gpsimd.tensor_copy(rt[:, 0, part * 64:(part + 1) * 64], eh[:])
                    nc.gpsimd.tensor_tensor(rt[:, 1, part * 64:(part + 1) * 64], ecode[:], el[:], ALU.subtract)
                pool.drain().then_inc(s_rt, 1)

            def weigh(m):
                pool.wait_ge(s_v1, m + 1)
                nc.gpsimd.tensor_tensor(vl[:], vl[:], rtt[:, 2:3, :].broadcast_to([P, ELO, P]), ALU.mult).then_inc(s_vp, 1)

            def low(m, i):
                for j in range(AG):
                    pool.wait_ge(s_gp, m * AG + j + 1)
                    ts = slice(j * 16, (j + 1) * 16)
                    nc.gpsimd.tensor_tensor(gp[:, 1, :, ts], gh[i][:, :, ts], gp[:, 0, :, ts], ALU.subtract).then_inc(s_gl, 1)

            nc.gpsimd.memset(by_elo[:], 1.0 / ELO)
            pool.drain()
            decode(0)
            parts(0, True)
            weigh(0)
            decode(1)
            parts(1, False)

            def body(it, first, last):
                for i in range(2):
                    m = it * 2 + i
                    low(m, i)
                    if not (last and i == 1):
                        weigh(m + 1)
                    if not last:
                        decode(m + 2)
                        parts(m + 2, False)

            passes(pool, body)

        @block.scalar
        def _(act):
            def softmax_exp(m):
                act.wait_ge(s_top, m + 1)
                nc.scalar.activation(ex[:], ex[:], ACT.Exp, scale=scl[:, 7:8]).then_inc(s_exp, 1)

            def turn(m):
                act.wait_ge(s_tr, m + 1)
                nc.scalar.activation(rtt[:].rearrange("p a b -> p (a b)"), ps_t[:, 0:3 * P], ACT.Copy).then_inc(s_rtt, 1)

            def gelu(m, i, fresh, lo, hi):
                if lo == 0 and not fresh:
                    act.wait_ge(s_gl, (m - 1) * AG)
                for j in range(lo, hi):
                    act.wait_ge(s_h, m * HG + j + 1)
                    nc.scalar.activation(gh[i][:, 4 * j:4 * j + 4, :].rearrange("p a b -> p (a b)"), ps_h[j % 2][:],
                                         ACT.Gelu_apprx_tanh, scale=scl[:, 6:7]).then_inc(s_gh, 1)

            def high(m, i, fresh, lo, hi):
                if lo == 0 and not fresh:
                    act.wait_ge(s_o, m)
                for j in range(lo, hi):
                    act.wait_ge(s_g, m * AG + j + 1)
                    ts = slice(j * 16, (j + 1) * 16)
                    nc.scalar.activation(gp[:, 0, :, ts], gh[i][:, :, ts], ACT.Copy).then_inc(s_gp, 1)

            gelu(0, 0, True, 0, HG)
            softmax_exp(0)
            turn(0)
            softmax_exp(1)

            def body(it, first, last):
                for i in range(2):
                    m = it * 2 + i
                    high(m, i, first and i == 0, 0, 1)
                    if not (last and i == 1):
                        turn(m + 1)
                    high(m, i, first and i == 0, 1, AG)
                    if not (last and i == 1):
                        gelu(m + 1, 1 - i, first and i == 0, 0, EXP_AT)
                    if not last:
                        softmax_exp(m + 2)
                    if not (last and i == 1):
                        gelu(m + 1, 1 - i, first and i == 0, EXP_AT, HG)

            passes(act, body)

        @block.tensor
        def _(pe):
            def sims(m, it, i, fresh, lo, hi):
                if lo == 0:
                    pe.wait_ge(s_xt[i], it * 16 + 16)
                    if not fresh:
                        pe.wait_ge(s_simu, m)
                for step in range(lo, hi):
                    half, k = step // 7, step % 7
                    cols = slice(half * 512, (half + 1) * 512)
                    if k == 0:
                        last = nc.tensor.matmul(ps_s[:, cols], ones3[:], m_c[:, cols], start=True, stop=False)
                    else:
                        c, (xpart, wpart) = (k - 1) // 3, ((0, 0), (0, 1), (1, 0))[(k - 1) % 3]
                        last = nc.tensor.matmul(ps_s[:, cols], xt[i][:, xpart, c, :], m_w[:, wpart, c, cols], start=False,
                                                stop=k == 6)
                if hi == SIM_STEPS:
                    last.then_inc(s_sim, 1)

            def turn(m):
                pe.wait_ge(s_rt, m + 1)
                for j in range(3):
                    last = nc.tensor.transpose(ps_t[:, j * P:(j + 1) * P], rt[:, j, :], ident[:])
                last.then_inc(s_tr, 1)

            def hidden(m, i):
                for j in range(HG):
                    if not (isinstance(m, int) and m * HG + j < 2):
                        pe.wait_ge(s_gh, m * HG + j - 1)
                    for k in range(4):
                        out_k, l = ps_h[j % 2][:, k * P:(k + 1) * P], 4 * j + k
                        for c in range(EG):
                            nc.tensor.matmul(out_k, down_t[:, 0, c, l, :], xt[i][:, 0, c, :], start=c == 0, stop=False)
                            nc.tensor.matmul(out_k, down_t[:, 0, c, l, :], xt[i][:, 1, c, :], start=False, stop=False)
                            last = nc.tensor.matmul(out_k, down_t[:, 1, c, l, :], xt[i][:, 0, c, :], start=False,
                                                    stop=c == EG - 1)
                    last.then_inc(s_h, 1)

            def weights(m, lo, hi):
                if lo == 0:
                    pe.wait_ge(s_u1, m + 1)
                    pe.wait_ge(s_vp, m + 1)
                for j in range(lo, hi):
                    if not (isinstance(m, int) and m * AG + j < 2):
                        pe.wait_ge(s_g, m * AG + j - 1)
                    for t in range(16):
                        last = nc.tensor.matmul(ps_a[j % 2][:, t, :], uh[:, :, j * 16 + t], vl[:, :, j * 16 + t],
                                                start=True, stop=True)
                    last.then_inc(s_a, 1)

            def combine(m, fresh):
                pe.wait_ge(s_gl, m * AG + AG)
                if not fresh:
                    pe.wait_ge(s_y, m)
                for l in range(ELO):
                    nc.tensor.matmul(ps_o[:, 0:E], gp[:, 0, l, :], up_s[:, 0, l, :], start=l == 0, stop=False)
                    nc.tensor.matmul(ps_o[:, 0:E], gp[:, 0, l, :], up_s[:, 1, l, :], start=False, stop=False)
                    last = nc.tensor.matmul(ps_o[:, 0:E], gp[:, 1, l, :], up_s[:, 0, l, :], start=False, stop=l == ELO - 1)
                last.then_inc(s_o, 1)

            sims(0, 0, 0, True, 0, SIM_STEPS)
            hidden(0, 0)
            sims(1, 0, 1, False, 0, SIM_STEPS)
            turn(0)

            def body(it, first, last):
                for i in range(2):
                    m = it * 2 + i
                    for j in range(AG):
                        weights(m, j, j + 1)
                        if not last and j > 0:
                            sims(m + 2, it + 1, i, False, 2 * j - 2, 2 * j)
                        if j == TURN_AT and not (last and i == 1):
                            turn(m + 1)
                    if not (last and i == 1):
                        hidden(m + 1, 1 - i)
                    combine(m, first and i == 0)

            passes(pe, body)

        @block.vector
        def _(dve):
            def route(m, fresh):
                if not fresh:
                    dve.wait_ge(s_rt, m)
                dve.wait_ge(s_sim, m + 1)
                nc.vector.memset(held[:], 0.0)
                for g in range(QG):
                    nc.vector.max(s8[:, g, :], ps_s[:, g * KEYS:(g + 1) * KEYS])
                dve.drain()
                pairs(nc.vector, cand, s8[:, 0:FH, :], s8[:, FH:QG, :])
                for g in range(QG):
                    last = nc.vector.max_index(i8[:, g, :], s8[:, g, :], ps_s[:, g * KEYS:(g + 1) * KEYS])
                last.then_inc(s_simu, 1)
                dve.drain()
                for h in range(FH):
                    nc.vector.max(top[:, h, :], cand[:, h, :])
                dve.drain()
                nc.vector.tensor_tensor(ex[:], top[:], inner(top[:, :, 0], TOPK), ALU.subtract).then_inc(s_top, 1)
                for h in range(FH):
                    nc.vector.max_index(pos[:, h, :], top[:, h, :], cand[:, h, :])
                dve.drain()
                nc.vector.tensor_copy(posh[:], pos[:])
                dve.wait_ge(s_exp, m + 1)
                nc.vector.tensor_reduce(rs[:], ex[:], AX.X, ALU.add)
                dve.drain()
                nc.vector.reciprocal(rs[:], rs[:]).then_inc(s_rs, 1)
                nc.vector.tensor_tensor(oh[:], posh[:].rearrange("p h (o k) -> p h o k", o=1).broadcast_to([P, FH, CAND, TOPK]),
                                        iotac[:].rearrange("p (o c) k -> p o c k", o=1).broadcast_to([P, FH, CAND, TOPK]),
                                        ALU.is_equal).then_inc(s_oh, 1)

            def experts_of(m):
                dve.wait_ge(s_ohc, m + 1)
                nc.vector.tensor_reduce(ecode[:].rearrange("p (h k) -> p h k", k=TOPK), ohc[:].rearrange("p h c k -> p h k c"),
                                        AX.X, ALU.add).then_inc(s_ec, 1)

            def same(dst, row, n):
                return nc.vector.tensor_tensor(
                    dst.rearrange("p e (a b) -> p e a b", b=16),
                    rtt[:, row:row + 1, :].rearrange("p o (a b) -> p o a b", b=16).broadcast_to([P, n, P // 16, 16]),
                    iota[:, 0:n, :].rearrange("p e (o b) -> p e o b", o=1).broadcast_to([P, n, P // 16, 16]),
                    ALU.is_equal)

            def onehot_low(m, fresh):
                dve.wait_ge(s_rtt, m + 1)
                if not fresh:
                    dve.wait_ge(s_a, m * AG)
                same(vl[:], 1, ELO).then_inc(s_v1, 1)

            def onehot_high(m):
                same(uh[:], 0, EHI).then_inc(s_u1, 1)

            def gate(m, i):
                dve.wait_ge(s_gh, m * HG + HG)
                ghv = gh[i][:].rearrange("p l t -> p t l")
                for j in range(AG):
                    dve.wait_ge(s_a, m * AG + j + 1)
                    nc.vector.scalar_tensor_tensor(ghv[:, j * 16:(j + 1) * 16, :], ps_a[j % 2][:], scl[:, 8:9],
                                                   ghv[:, j * 16:(j + 1) * 16, :], ALU.mult, ALU.mult).then_inc(s_g, 1)

            def finish(m, it, i, fresh):
                dve.wait_ge(s_o, m + 1)
                dve.wait_ge(s_x1[i], it * 16 + 16)
                if not fresh:
                    dve.wait_ge(s_st[i], it * 16)
                nc.vector.scalar_tensor_tensor(y[i][:], ps_o[:, 0:E], scl[:, 9:10], x1[i][:], ALU.mult, ALU.add).then_inc(s_y, 1)

            route(0, True)
            experts_of(0)
            onehot_low(0, True)
            route(1, False)
            onehot_high(0)
            experts_of(1)

            def body(it, first, last):
                for i in range(2):
                    m = it * 2 + i
                    gate(m, i)
                    if i == 1:
                        finish(m - 1, it, 0, first)
                    elif not first:
                        finish(m - 1, it - 1, 1, isinstance(it, int) and it == 1)
                    if not (last and i == 1):
                        onehot_low(m + 1, False)
                    if not last:
                        route(m + 2, False)
                    if not (last and i == 1):
                        onehot_high(m + 1)
                    if not last:
                        experts_of(m + 2)

            passes(dve, body)
            finish(SUBTILES - 1, SUBTILES // 2 - 1, 1, False)


def build(nc, x, wq, wk, wv, wo, wf1, wf2, wg1, wg2, norm_w, fw_q, gamma, beta, keys, down, up,
          c_ident, c_sel, c_red, c_bm, c_iota, c_iotac, out):
    x1_dram = nc.dram_tensor("x1_dram", (TOKENS, E), f32, kind="Internal").ap()
    x2t_dram = nc.dram_tensor("x2t_dram", (SUBTILES, P, 2 * EG, P), f16, kind="Internal").ap()
    with ExitStack() as ctx:
        cacc = ctx.enter_context(nc.sbuf_tensor("cacc", [P, EG, E + 1], f32))
        attention(nc, x, wq, wk, wv, wo, wf1, wf2, wg1, wg2, norm_w, c_ident, c_sel, c_red, c_bm, x1_dram, x2t_dram, cacc)

        def sb(name, shape, dt=f32):
            return ctx.enter_context(nc.sbuf_tensor(name, shape, dt))

        res = (
            sb("m_w", [P, 2, EG, SIMS], f16),
            sb("m_c", [3, SIMS], bf16),
            sb("ones3", [3, P], bf16),
            sb("ident2", [P, P]),
            sb("down_t", [P, 2, EG, ELO, EHI], f16),
            sb("up_s", [P, 2, ELO, E], f16),
            sb("iota", [P, EHI, 16], f16),
            sb("iotac", [P, CAND, TOPK], f16),
            sb("scl", [P, 10]),
        )
        fold(nc, fw_q, gamma, beta, keys, down, up, c_ident, c_iota, c_iotac, cacc, res)
        experts(nc, x1_dram, x2t_dram, out.rearrange("b t e -> (b t) e"), res)


INPUTS = ["L0_attn_x", "L0_attn_Wq", "L0_attn_Wk", "L0_attn_Wv", "L0_attn_Wo", "L0_attn_Wf1", "L0_attn_Wf2", "L0_attn_Wg1",
          "L0_attn_Wg2", "L0_attn_norm_weight", "L0_ffn_w_q", "L0_ffn_bn_gamma", "L0_ffn_bn_beta", "L0_ffn_keys",
          "L0_ffn_down_embed", "L0_ffn_up_embed"]


def constants():
    import numpy as np

    k, m = np.arange(P)[:, None, None], np.arange(P)[None, None, :]
    dv = np.arange(D)[None, :, None]
    row, i = np.arange(3 * QUAD)[:, None, None] % QUAD, np.arange(4)[None, :, None]
    sel = (row // 4 == m // D) & (row % 4 == i)
    red = (k // D == m // D) & (m % D == dv)
    bm = np.arange(P)[:, None] // D == np.arange(P)[None, :] // D
    f = np.float32
    return {
        "c_ident": np.eye(P, dtype=f),
        "c_sel": sel.reshape(3 * QUAD, -1).astype(f),
        "c_red": red.reshape(P, -1).astype(f) * f(D ** -0.5),
        "c_bm": bm.astype(f) * f(1.0 / D),
        "c_iota": np.tile(np.repeat(np.arange(EHI), 16), (P, 1)).astype(f),
        "c_iotac": np.tile(np.repeat(np.arange(CAND), TOPK), (P, 1)).astype(f),
    }


def kernel(**inputs):
    import numpy as np
    import concourse.bacc as bacc
    from concourse.bass_utils import run_bass_kernel_spmd

    nc = bacc.Bacc("TRN2", target_bir_lowering=False, num_devices=1)
    arrays = {f"in_{n}": np.ascontiguousarray(inputs[n]) for n in INPUTS} | constants()
    wv = arrays["in_L0_attn_Wv"].reshape(E, EG, HEADS // EG, 4, 4).transpose(0, 1, 3, 2, 4)
    arrays["in_L0_attn_Wv"] = np.ascontiguousarray(wv.reshape(E, E))
    args = [nc.dram_tensor(n, a.shape, mybir.dt.from_np(a.dtype), kind="ExternalInput").ap() for n, a in arrays.items()]
    args.append(nc.dram_tensor("out_x", (BATCH, SEQ, E), f32, kind="ExternalOutput").ap())
    build(nc, *args)
    r = run_bass_kernel_spmd(nc, [arrays], core_ids=[0])
    return r.results[0]["out_x"]
```

```python
import concourse.bass as bass
from concourse import mybir
from contextlib import ExitStack

BATCH, SEQ, E = 2, 4096, 256
HEADS, D = 16, 16
P = 128
TOKENS = BATCH * SEQ
EG = E // P
TILE = 512
SUB = TILE // P
STEPS = SEQ // TILE
LN_EPS = 1e-5
FH, KD, TOPK, KEYS = 8, 128, 8, 64
QG = 2 * FH
QC = QG * KD
SIMS = QG * KEYS
EHI, ELO = 128, 32
CAND = 20
EXP_AT = 6
TURN_AT = 5
XSCALE = 1024.0
PSCALE = 16384.0
GSCALE = 2.0 ** -24
SIM_STEPS = 14
ROUNDER = 1.5 * 2.0 ** 23
SMALLEST = 2.0 ** -100
SUBTILES = TOKENS // P

f32 = mybir.dt.float32
f16 = mybir.dt.float16
bf16 = mybir.dt.bfloat16
u32 = mybir.dt.uint32
ALU = mybir.AluOpType
ACT = mybir.ActivationFunctionType
AX = mybir.AxisListType

PP_STEPS = 13
QUAD = 32
UNITS = EG * D
NS = 8
NPROD = 4
LAG = 4


def inner(ap, n):
    if len(ap.shape) == 2:
        return ap.rearrange("p (a o) -> p a o", o=1).broadcast_to([ap.shape[0], ap.shape[1], n])
    return ap.rearrange("p a (b o) -> p a b o", o=1).broadcast_to([*ap.shape, n])


def pairs(eng, dst, a, b):
    eng.tensor_tensor(dst[:, :, 0:8], inner(a[:, :, 0], 8), b[:, :, 0:8], ALU.add)
    eng.tensor_tensor(dst[:, :, 8:12], inner(a[:, :, 1], 4), b[:, :, 0:4], ALU.add)
    for r in (2, 3):
        eng.tensor_tensor(dst[:, :, 8 + 2 * r:10 + 2 * r], inner(a[:, :, r], 2), b[:, :, 0:2], ALU.add)
    eng.tensor_tensor(dst[:, :, 16:20], a[:, :, 4:8], inner(b[:, :, 0], 4), ALU.add)


def attention(nc, x, wq, wk, wv, wo, wf1, wf2, wg1, wg2, norm_w, c_ident, c_sel, c_red, c_bm, down, x1_dram, x2t_dram,
              cacc, ident, stage):
    x_v = x.rearrange("b (ts p) e -> b p ts e", p=P)
    x1_v = x1_dram.rearrange("(b ts p) e -> b p ts e", b=BATCH, p=P)
    x2t_v = x2t_dram.rearrange("m p k t -> p m k t")
    with ExitStack() as ctx:
        def sb(name, shape, dt=f32):
            return ctx.enter_context(nc.sbuf_tensor(name, shape, dt))

        def ps(name, shape):
            return ctx.enter_context(nc.psum_tensor(name, shape, f32))

        def sem(name):
            return ctx.enter_context(nc.semaphore(name))

        sel_f = sb("sel_f", [3 * QUAD, 4 * P])
        sel = sb("sel", [3 * QUAD, 4, P], bf16)
        red = sb("red", [P, D, P])
        bm = sb("bm", [P, P])
        w_q = sb("w_q", [P, EG, E])
        w_k = sb("w_k", [P, EG, E])
        w_v = sb("w_v", [P, EG, E])
        w_o = sb("w_o", [P, EG, E])
        w_low = sb("w_low", [P, EG, 48])
        w_up = sb("w_up", [48, E])
        w_all = (w_v, w_low, w_q, w_k)
        w_parts = [sb(f"w_parts{k}", [P, 2, EG, w.shape[2]], f16) for k, w in enumerate(w_all)]
        w_mx = sb("w_mx", [P, 4])
        w_mx4 = sb("w_mx4", [4, 4])
        w_e4 = sb("w_e4", [4, 1], u32)
        w_diag = sb("w_diag", [4, 8])
        ones4 = sb("ones4", [4, P])
        w_scl = sb("w_scl", [P, 8])
        nw = sb("nw", [P, EG])
        eps = sb("eps", [P, 1])
        mhalf = sb("mhalf", [P, SUB])
        x_in = sb("x_in", [P, SUB, E])
        x_res = sb("x_res", [P, SUB, E])
        st = sb("st", [P, SUB, 6])
        mv = sb("mv", [P, SUB, 2])
        veps = sb("veps", [P, SUB])
        rstd = sb("rstd", [P, SUB])
        mr = sb("mr", [P, SUB])
        nmr = sb("nmr", [P, SUB])
        zero = sb("zero", [P, SUB])
        xn = sb("xn", [P, SUB, E])
        xt = sb("xt", [P, 2, EG, TILE], f16)
        low = sb("low", [48, TILE])
        q_s = [sb(f"q_s{b}", [P, EG, TILE]) for b in range(BATCH)]
        k_s = [sb(f"k_s{b}", [P, EG, TILE]) for b in range(BATCH)]
        f_s = [sb(f"f_s{b}", [P, EG, TILE]) for b in range(BATCH)]
        g_s = [sb(f"g_s{b}", [P, EG, TILE]) for b in range(BATCH)]
        v_f = sb("v_f", [P, EG, TILE])
        v_r = sb("v_r", [P, EG, TILE])
        v_p = sb("v_p", [P, 3, EG, TILE], bf16)
        v_s = [sb(f"v_s{b}", [3 * QUAD, 4, EG, TILE], bf16) for b in range(BATCH)]
        kv = sb("kv", [P, 2, TILE])
        state = sb("state", [P, NS, TILE])
        prod = sb("prod", [P, NPROD, TILE])
        carry = [sb(f"carry{b}", [P, UNITS]) for b in range(BATCH)]
        og = sb("og", [P, EG * TILE])
        sq = sb("sq", [P, EG * TILE])
        x1 = sb("x1", [P, SUB, E])
        st2 = sb("st2", [P, SUB, 6])
        mv2 = sb("mv2", [P, SUB, 2])
        veps2 = sb("veps2", [P, SUB])
        rstd2 = sb("rstd2", [P, SUB])
        mr2 = sb("mr2", [P, SUB])
        nmr2 = sb("nmr2", [P, SUB])
        x2 = sb("x2", [P, SUB, E + 1])
        x2t = sb("x2t", [P, SUB, 2 * EG, P], f16)

        pp = [ps(f"pp{i}", [P, TILE]) for i in range(2)]
        vb = [ps(f"vb{i}", [P, TILE]) for i in range(2)]
        o_ps = ps("o_ps", [P, EG, TILE])
        pm = ps("pm", [P, EG, TILE])

        s_wload = sem("s_wload")
        s_const = sem("s_const")
        s_xin = sem("s_xin")
        s_xres = sem("s_xres")
        s_var = sem("s_var")
        s_rstd = sem("s_rstd")
        s_xn = sem("s_xn")
        s_ppfull = sem("s_ppfull")
        s_ppfree = sem("s_ppfree")
        s_vsplit = sem("s_vsplit")
        s_vs = sem("s_vs")
        s_vb = sem("s_vb")
        s_kv = sem("s_kv")
        s_scan = sem("s_scan")
        s_carry = sem("s_carry")
        s_prod = sem("s_prod")
        s_red = sem("s_red")
        s_og = sem("s_og")
        s_sq = sem("s_sq")
        s_ms = sem("s_ms")
        s_rms = sem("s_rms")
        s_ogn = sem("s_ogn")
        s_attn = sem("s_attn")
        s_x1 = sem("s_x1")
        s_var2 = sem("s_var2")
        s_rstd2 = sem("s_rstd2")
        s_x2 = sem("s_x2")
        s_x2tp = sem("s_x2tp")
        s_x2h = sem("s_x2h")
        s_x2t = sem("s_x2t")
        s_cov = sem("s_cov")
        s_cacc = sem("s_cacc")
        s_x1st = sem("s_x1st")
        s_x2st = sem("s_x2st")
        s_step = sem("s_step")
        s_lns = sem("s_lns")
        s_down = sem("s_down")
        s_wm = sem("s_wm")
        s_wh = sem("s_wh")
        s_ws = sem("s_ws")
        s_vr = sem("s_vr")
        s_v2 = sem("s_v2")
        s_xl = sem("s_xl")

        CARRIES = UNITS // 4
        STACKED = 12 * 16

        WLOADS = 13

        def none_before(n):
            return isinstance(n, int) and n == 0

        def passes(eng, body):
            body(0, True, False)
            with eng.Fori(1, STEPS - 1) as it:
                body(it, False, False)
            body(STEPS - 1, False, True)

        block = ctx.enter_context(nc.Block())

        @block.sync
        def _(sp):
            for dst, src in ((ident[:], c_ident), (sel_f[:], c_sel), (red[:].rearrange("p a b -> p (a b)"), c_red),
                             (bm[:], c_bm)):
                sp.dma_start(dst, src).then_inc(s_wload, 16)
            for dst, src in ((w_q, wq), (w_k, wk), (w_v, wv), (w_o, wo)):
                sp.dma_start(dst[:], src.rearrange("(c p) n -> p c n", p=P)).then_inc(s_wload, 16)
            sp.dma_start(nw[:], norm_w.rearrange("(c p) -> p c", p=P), allow_slow_non_contiguous=True).then_inc(s_wload, 16)
            sp.wait_ge(s_const, 1)
            sp.dma_start(w_low[:, :, 0:16], wf1.rearrange("(c p) n -> p c n", p=P)).then_inc(s_wload, 16)
            sp.dma_start(w_low[:, :, 32:48], wg1.rearrange("(c p) n -> p c n", p=P)).then_inc(s_wload, 16)
            sp.dma_start(w_up[0:16, :], wf2).then_inc(s_wload, 16)
            sp.dma_start(w_up[32:48, :], wg2).then_inc(s_wload, 16)

            def load_in(n, it, b):
                if not none_before(n):
                    sp.wait_ge(s_xn, n)
                sp.dma_start(x_in[:], x_v[b, :, bass.ds(it * SUB, SUB), :]).then_inc(s_xin, 16)

            def load_res(n, it, b):
                if not none_before(n):
                    sp.wait_ge(s_x1, n)
                sp.dma_start(x_res[:], x_v[b, :, bass.ds(it * SUB, SUB), :]).then_inc(s_xres, 16)

            def store(n, it, b):
                sp.wait_ge(s_x2t, n + 1)
                sp.dma_start(x2t_v[:, bass.ds(it * SUB + b * (SEQ // P), SUB), :, :], x2t[:]).then_inc(s_x2st, 16)
                sp.dma_start(x1_v[b, :, bass.ts(it, SUB), :], x1[:]).then_inc(s_x1st, 16)

            def stack(n, b):
                if not (isinstance(n, int) and n < 2):
                    sp.wait_ge(s_vb, (n - 1) * UNITS)
                sp.wait_ge(s_vsplit, n + 1)
                for q in range(4):
                    for part in range(3):
                        sp.dma_start(v_s[b][part * QUAD:(part + 1) * QUAD, q],
                                     v_p[q * QUAD:(q + 1) * QUAD, part]).then_inc(s_vs, 16)

            load_in(0, 0, 0)
            load_in(1, 0, 1)
            stack(0, 0)
            sp.dma_start(stage[:], down.rearrange("(p l) c -> p l c", l=ELO)).then_inc(s_down, 16)

            def body(it, first, last):
                n = it * 2
                if not last:
                    load_in(n + 2, it + 1, 0)
                load_res(n, it, 0)
                stack(n + 1, 1)
                if not first:
                    store(n - 1, it - 1, 1)
                if not last:
                    load_in(n + 3, it + 1, 1)
                load_res(n + 1, it, 1)
                if not last:
                    stack(n + 2, 0)
                store(n, it, 0)

            passes(sp, body)
            store(2 * STEPS - 1, STEPS - 1, 1)
            sp.wait_ge(s_x1st, 32 * STEPS)
            sp.wait_ge(s_x2st, 32 * STEPS)
            sp.wait_ge(s_down, 16)

        @block.gpsimd
        def _(pool):
            nc.gpsimd.memset(w_low[:], 0.0).then_inc(s_const, 1)
            nc.gpsimd.memset(mhalf[:], -0.5)
            nc.gpsimd.memset(eps[:], LN_EPS)
            nc.gpsimd.memset(zero[:], 0.0)
            nc.gpsimd.memset(ones4[:], 1.0)
            for b in range(BATCH):
                nc.gpsimd.memset(carry[b][:], 0.0)
            nc.gpsimd.memset(cacc[:], 0.0)
            nc.gpsimd.memset(x2[:, :, E:E + 1], 1.0)
            pool.drain().then_inc(s_const, 1)

            def head_rstd(n):
                pool.wait_ge(s_var, n + 1)
                nc.gpsimd.tensor_tensor(rstd[:], veps[:], mhalf[:], ALU.pow)
                pool.drain()
                nc.gpsimd.tensor_tensor(mr[:], mv[:, :, 0], rstd[:], ALU.mult)
                pool.drain()
                nc.gpsimd.tensor_tensor(nmr[:], zero[:], mr[:], ALU.subtract).then_inc(s_rstd, 1)

            def tail_rstd(n):
                pool.wait_ge(s_var2, n + 1)
                nc.gpsimd.tensor_tensor(rstd2[:], veps2[:], mhalf[:], ALU.pow)
                pool.drain()
                nc.gpsimd.tensor_tensor(mr2[:], mv2[:, :, 0], rstd2[:], ALU.mult)
                pool.drain()
                nc.gpsimd.tensor_tensor(nmr2[:], zero[:], mr2[:], ALU.subtract).then_inc(s_rstd2, 1)

            def rest(n, g):
                pool.wait_ge(s_ppfree, n * PP_STEPS + 3 + g)
                nc.gpsimd.tensor_tensor(v_r[:, g, :], v_f[:, g, :], v_p[:, 0, g, :], ALU.subtract).then_inc(s_vr, 1)

            def third_part(n, g):
                pool.wait_ge(s_v2, n * EG + g + 1)
                i = nc.gpsimd.tensor_tensor(v_p[:, 2, g, :], v_r[:, g, :], v_p[:, 1, g, :], ALU.subtract)
                if g == EG - 1:
                    i.then_inc(s_vsplit, 1)

            def heavy(n, b, tail, head):
                for u in range(UNITS):
                    pool.wait_ge(s_scan, n * UNITS + u + 1)
                    if u >= NPROD or not none_before(n):
                        pool.wait_ge(s_red, n * UNITS + u - NPROD + 1)
                    nc.gpsimd.tensor_tensor(prod[:, u % NPROD, :], state[:, u % NS, :], q_s[b][:, u // D, :],
                                            ALU.mult).then_inc(s_prod, 1)
                    if head and u == 0:
                        head_rstd(n + 1)
                    if head and u in (13, 14):
                        rest(n + 1, u - 13)
                    if head and u in (18, 19):
                        third_part(n + 1, u - 18)
                    if tail and u == 21:
                        tail_rstd(n - 1)

            head_rstd(0)
            for g in range(EG):
                rest(0, g)
            for g in range(EG):
                third_part(0, g)

            def body(it, first, last):
                heavy(it * 2, 0, not first, True)
                heavy(it * 2 + 1, 1, True, not last)

            passes(pool, body)
            tail_rstd(2 * STEPS - 1)

        @block.scalar
        def _(act):
            def evac(n, b, step, out, func, scale=1.0):
                act.wait_ge(s_ppfull, n * PP_STEPS + step + 1)
                nc.scalar.activation(out, pp[(b * PP_STEPS + step) % 2][0:out.shape[0], :], func,
                                     scale=scale).then_inc(s_ppfree, 1)

            def head_norm(n):
                act.wait_ge(s_rstd, n + 1)
                if not none_before(n):
                    act.wait_ge(s_ppfull, (n - 1) * PP_STEPS + 2)
                for s in range(SUB):
                    i = nc.scalar.activation(xn[:, s, :], x_in[:, s, :], ACT.Identity, bias=nmr[:, s:s + 1],
                                             scale=rstd[:, s:s + 1])
                i.then_inc(s_xn, 1)

            def tail_norm(n):
                act.wait_ge(s_rstd2, n + 1)
                if not none_before(n):
                    act.wait_ge(s_cov, n)
                for s in range(SUB):
                    i = nc.scalar.activation(x2[:, s, 0:E], x1[:, s, :], ACT.Identity, bias=nmr2[:, s:s + 1],
                                             scale=rstd2[:, s:s + 1])
                i.then_inc(s_x2, 1)

            def turned(n, b):
                for c in range(EG):
                    evac(n, b, c, xt[:, 0, c, :], ACT.Copy, XSCALE)

            def values(n, b):
                if not none_before(n):
                    act.wait_ge(s_vsplit, n)
                    act.wait_ge(s_vs, n * STACKED)
                for g in range(EG):
                    act.wait_ge(s_ppfull, n * PP_STEPS + 3 + g)
                    bank = pp[(b * PP_STEPS + 2 + g) % 2]
                    nc.scalar.activation(v_f[:, g, :], bank[:], ACT.Copy, scale=w_scl[:, 4:5])
                    nc.scalar.activation(v_p[:, 0, g, :], bank[:], ACT.Copy, scale=w_scl[:, 4:5]).then_inc(s_ppfree, 1)
                evac(n, b, 4, low[:], ACT.Copy, w_scl[0:48, 5:6])

            def second_part(n):
                for g in range(EG):
                    act.wait_ge(s_vr, n * EG + g + 1)
                    nc.scalar.activation(v_p[:, 1, g, :], v_r[:, g, :], ACT.Copy).then_inc(s_v2, 1)

            def query(n, b, g):
                evac(n, b, 5 + g, q_s[b][:, g, :], ACT.Silu, w_scl[:, 6:7])

            def keys(n, b, g):
                evac(n, b, 7 + g, k_s[b][:, g, :], ACT.Silu, w_scl[:, 7:8])

            def gates(n, b):
                for g in range(EG):
                    evac(n, b, 9 + g, f_s[b][:, g, :], ACT.Sigmoid)
                for g in range(EG):
                    evac(n, b, 11 + g, g_s[b][:, g, :], ACT.Sigmoid)

            def tail_sq(n, g):
                act.wait_ge(s_og, n * EG + g + 1)
                ts = slice(g * TILE, (g + 1) * TILE)
                nc.scalar.activation(sq[:, ts], og[:, ts], ACT.Square).then_inc(s_sq, 1)

            def tail_rms(n):
                act.wait_ge(s_ms, n + 1)
                nc.scalar.activation(sq[:], pm[:].rearrange("p c t -> p (c t)"), ACT.Ln, bias=eps[:, 0:1]).then_inc(s_lns, 1)
                act.wait_ge(s_lns, n + 1)
                nc.scalar.activation(sq[:], sq[:], ACT.Exp, scale=-0.5).then_inc(s_rms, 1)

            def tail_x2t(n):
                if not none_before(n):
                    act.wait_ge(s_x2st, n * 16)
                for c in range(EG):
                    act.wait_ge(s_x2tp, n * EG + c + 1)
                    i = nc.scalar.activation(x2t[:, :, c, :], pm[:, c, :].rearrange("p (s t) -> p s t", t=P), ACT.Copy,
                                             scale=XSCALE)
                i.then_inc(s_x2h, 1)

            def during(n, b, tail, head):
                if head:
                    head_norm(n + 1)
                if tail:
                    tail_sq(n - 1, 1)
                if head:
                    turned(n + 1, 1 - b)
                if tail:
                    tail_rms(n - 1)
                if head:
                    values(n + 1, 1 - b)
                    second_part(n + 1)
                    query(n + 1, 1 - b, 0)
                if head:
                    query(n + 1, 1 - b, 1)
                if tail:
                    tail_norm(n - 1)
                tail_sq(n, 0)
                if head:
                    keys(n + 1, 1 - b, 0)
                if tail:
                    tail_x2t(n - 1)
                if head:
                    keys(n + 1, 1 - b, 1)
                    gates(n + 1, 1 - b)

            act.wait_ge(s_const, 2)
            head_norm(0)
            act.wait_ge(s_ws, 1)
            for k, w in enumerate(w_all):
                nc.scalar.activation(w_parts[k][:, 0], w[:], ACT.Copy, scale=w_scl[:, k:k + 1]).then_inc(s_wh, 1)
            turned(0, 0)
            values(0, 0)
            query(0, 0, 0)
            second_part(0)
            query(0, 0, 1)
            keys(0, 0, 0)
            keys(0, 0, 1)
            gates(0, 0)

            def body(it, first, last):
                n = it * 2
                during(n, 0, not first, True)
                during(n + 1, 1, True, not last)

            passes(act, body)
            tail_sq(2 * STEPS - 1, 1)
            tail_rms(2 * STEPS - 1)
            tail_norm(2 * STEPS - 1)
            tail_x2t(2 * STEPS - 1)

        @block.vector
        def _(dve):
            dve.wait_ge(s_const, 2)
            dve.wait_ge(s_wload, 16 * WLOADS)
            nc.vector.tensor_copy(sel[:].rearrange("p a b -> p (a b)"), sel_f[:])
            for c in range(EG):
                nc.vector.tensor_scalar(w_o[:, c, :], w_o[:, c, :], nw[:, c:c + 1], None, ALU.mult)
            for k, w in enumerate(w_all):
                i = nc.vector.tensor_reduce(w_mx[:, k:k + 1], w[:].rearrange("p c n -> p (c n)"), AX.X, ALU.max,
                                            apply_absolute_value=True)
            i.then_inc(s_wm, 1)

            def weight_scales():
                dve.wait_ge(s_wm, 2)
                nc.vector.tensor_reduce(w_mx4[:, 0:1], pp[0][0:4, 0:P], AX.X, ALU.max)
                dve.drain()
                nc.vector.tensor_scalar(w_mx4[:, 1:2], w_mx4[:, 0:1], SMALLEST, None, ALU.max)
                dve.drain()
                nc.vector.tensor_scalar(w_e4[:], w_mx4[:, 1:2].bitcast(u32), 0x7F800000, None, ALU.bitwise_and)
                dve.drain()
                nc.vector.tensor_scalar(w_mx4[:, 2:3].bitcast(u32), w_e4[:], -1.0, float((2 * 127 + 13) << 23),
                                        ALU.mult, ALU.add)
                nc.vector.tensor_scalar(w_mx4[:, 3:4].bitcast(u32), w_e4[:], float(13 << 23), None, ALU.subtract)
                dve.drain()
                nc.vector.tensor_scalar(w_diag[:, 0:4], ident[0:4, 0:4], w_mx4[:, 2:3], None, ALU.mult)
                nc.vector.tensor_scalar(w_diag[:, 4:8], ident[0:4, 0:4], w_mx4[:, 3:4], 1.0 / XSCALE, ALU.mult, ALU.mult)
                dve.drain().then_inc(s_wm, 1)
                dve.wait_ge(s_wm, 4)
                nc.vector.tensor_copy(w_scl[:], pp[1][:, 0:8])
                dve.drain().then_inc(s_ws, 1)
                for k, w in enumerate(w_all):
                    dve.wait_ge(s_wh, k + 1)
                    nc.vector.scalar_tensor_tensor(w_parts[k][:, 1], w[:], w_scl[:, k:k + 1], w_parts[k][:, 0],
                                                   ALU.mult, ALU.subtract)
                dve.drain().then_inc(s_step, 1)

            def head_stats(n, half):
                if half == 0:
                    dve.wait_ge(s_xin, n * 16 + 16)
                for s in (2 * half, 2 * half + 1):
                    nc.vector.bn_stats(st[:, s, :], x_in[:, s, :])

            def head_var(n):
                dve.drain()
                for s in range(SUB):
                    nc.vector.bn_aggr(mv[:, s, :], st[:, s, :])
                dve.drain()
                nc.vector.tensor_scalar(veps[:], mv[:, :, 1], LN_EPS, None, ALU.add).then_inc(s_var, 1)

            def head_low(n, b, c):
                dve.wait_ge(s_ppfree, n * PP_STEPS + c + 1)
                nc.vector.scalar_tensor_tensor(xt[:, 1, c, :], pp[(b * PP_STEPS + c) % 2][:], XSCALE, xt[:, 0, c, :],
                                               ALU.mult, ALU.subtract).then_inc(s_xl, 1)

            def tail_gate(n, b, g):
                dve.wait_ge(s_red, n * UNITS + (g + 1) * D)
                dve.wait_ge(s_ppfree, n * PP_STEPS + PP_STEPS)
                nc.vector.tensor_tensor(og[:, g * TILE:(g + 1) * TILE], o_ps[:, g, :], g_s[b][:, g, :],
                                        ALU.mult).then_inc(s_og, 1)

            def tail_ogn(n, g):
                if g == 0:
                    dve.wait_ge(s_rms, n + 1)
                ts = slice(g * TILE, (g + 1) * TILE)
                nc.vector.tensor_tensor(og[:, ts], og[:, ts], sq[:, ts], ALU.mult).then_inc(s_ogn, 1)

            def tail_x1(n, half):
                if half == 0:
                    dve.wait_ge(s_attn, n + 1)
                    dve.wait_ge(s_xres, n * 16 + 16)
                    if not none_before(n):
                        dve.wait_ge(s_x1st, n * 16)
                ss = slice(2 * half, 2 * half + 2)
                i = nc.vector.tensor_tensor(x1[:, ss, :].rearrange("p s e -> p (s e)"), pm[:, half, :],
                                            x_res[:, ss, :].rearrange("p s e -> p (s e)"), ALU.add)
                if half == 1:
                    i.then_inc(s_x1, 1)

            def tail_stats(n, half):
                dve.drain()
                for s in (2 * half, 2 * half + 1):
                    nc.vector.bn_stats(st2[:, s, :], x1[:, s, :])

            def tail_var(n):
                dve.drain()
                for s in range(SUB):
                    nc.vector.bn_aggr(mv2[:, s, :], st2[:, s, :])
                dve.drain()
                nc.vector.tensor_scalar(veps2[:], mv2[:, :, 1], LN_EPS, None, ALU.add).then_inc(s_var2, 1)

            def tail_low(n, c):
                if c == 0:
                    dve.wait_ge(s_x2h, n + 1)
                i = nc.vector.scalar_tensor_tensor(x2t[:, :, EG + c, :], pm[:, c, :].rearrange("p (s t) -> p s t", t=P), XSCALE,
                                                   x2t[:, :, c, :], ALU.mult, ALU.subtract)
                if c == EG - 1:
                    i.then_inc(s_x2t, 1)

            def tail_cacc(n):
                dve.wait_ge(s_cov, n + 1)
                for c in range(EG):
                    i = nc.vector.tensor_tensor(cacc[:, c, c * P:], pm[:, c, c * P:E + 1], cacc[:, c, c * P:], ALU.add)
                i.then_inc(s_cacc, 1)

            def kv_mult(n, b, u):
                dve.wait_ge(s_vb, n * UNITS + u + 1)
                if u >= 2 or not none_before(n):
                    dve.wait_ge(s_scan, n * UNITS + u - 1)
                nc.vector.tensor_tensor(kv[:, u % 2, :], vb[u % 2][:], k_s[b][:, u // D, :], ALU.mult).then_inc(s_kv, 1)

            def scan(n, b, u):
                dve.wait_ge(s_kv, n * UNITS + u + 1)
                if u >= NS or not none_before(n):
                    dve.wait_ge(s_prod, n * UNITS + u - NS + 1)
                    dve.wait_ge(s_carry, n * CARRIES + (u - NS) // 4 + 1)
                nc.vector.tensor_tensor_scan(state[:, u % NS, :], f_s[b][:, u // D, :], kv[:, u % 2, :],
                                             carry[b][:, u:u + 1], ALU.mult, ALU.add).then_inc(s_scan, 1)

            def save_carry(n, b, j):
                dve.wait_ge(s_scan, n * UNITS + 4 * j + 4)
                u = 4 * j
                nc.vector.tensor_copy(carry[b][:, u:u + 4], state[:, u % NS:u % NS + 4, TILE - 1]).then_inc(s_carry, 1)

            def heavy(n, b, tail, head, cov, stats):
                dve.wait_ge(s_ppfree, n * PP_STEPS + 11)
                kv_mult(n, b, 0)
                for u in range(UNITS):
                    if u + 1 < UNITS:
                        kv_mult(n, b, u + 1)
                    scan(n, b, u)
                    if u % 4 == 0 and u:
                        save_carry(n, b, u // 4 - 1)
                    if head and u == 0:
                        head_var(n + 1)
                    if tail and u == 3:
                        tail_gate(n - 1, 1 - b, 1)
                    if cov and u == 4:
                        tail_cacc(n - 2)
                    if head and u in (5, 6):
                        head_low(n + 1, 1 - b, u - 5)
                    if tail and u in (9, 10):
                        tail_ogn(n - 1, u - 9)
                    if tail and u in (17, 18):
                        tail_x1(n - 1, u - 17)
                    if tail and u in (19, 20):
                        tail_stats(n - 1, u - 19)
                    if tail and u == 21:
                        tail_var(n - 1)
                    if u == 23:
                        tail_gate(n, b, 0)
                    if stats and u in (29, 31):
                        head_stats(n + 2, (u - 29) // 2)
                    if tail and u in (27, 28):
                        tail_low(n - 1, u - 27)
                save_carry(n, b, CARRIES - 1)

            def both(piece, *args):
                piece(*args, 0)
                piece(*args, 1)

            both(head_stats, 0)
            head_var(0)
            weight_scales()
            both(head_low, 0, 0)
            both(head_stats, 1)

            def body(it, first, last):
                heavy(it * 2, 0, not first, True, not first, not last)
                heavy(it * 2 + 1, 1, True, not last, not first, not last)

            passes(dve, body)
            n = 2 * STEPS - 1
            tail_cacc(n - 1)
            tail_gate(n, 1, 1)
            both(tail_ogn, n)
            both(tail_x1, n)
            both(tail_stats, n)
            tail_var(n)
            both(tail_low, n)
            tail_cacc(n)

        @block.tensor
        def _(pe):
            pe.wait_ge(s_wload, 16 * WLOADS)
            pe.wait_ge(s_const, 2)
            pe.wait_ge(s_wm, 1)
            nc.tensor.transpose(pp[0][0:4, 0:P], w_mx[:], ident[:]).then_inc(s_wm, 1)
            pe.wait_ge(s_wm, 3)
            nc.tensor.matmul(pp[1][:, 0:8], ones4[:], w_diag[:], start=True, stop=True).then_inc(s_wm, 1)
            pe.wait_ge(s_ws, 1)

            def pp_bank(n, b, step):
                if step >= 2 or not none_before(n):
                    pe.wait_ge(s_ppfree, n * PP_STEPS + step - 1)
                return pp[(b * PP_STEPS + step) % 2]

            def head(n, b, step, halves=(0, 1)):
                bank = pp_bank(n, b, step) if 0 in halves else pp[(b * PP_STEPS + step) % 2]
                if step < 2:
                    pe.wait_ge(s_xn, n + 1)
                    for s in range(SUB):
                        i = nc.tensor.transpose(bank[:, s * P:(s + 1) * P], xn[:, s, step * P:(step + 1) * P], ident[:])
                elif step < 9:
                    if step == 2 and 0 in halves:
                        pe.wait_ge(s_xl, n * EG + EG)
                        if none_before(n):
                            pe.wait_ge(s_step, 1)
                    k = 0 if step < 4 else 1 if step == 4 else 2 if step < 7 else 3
                    g = step - (2, 4, 5, 7)[k]
                    cols = slice(0, 48) if step == 4 else slice(g * P, (g + 1) * P)
                    for c in halves:
                        for wpart, xpart in ((0, 0), (0, 1), (1, 0)):
                            i = nc.tensor.matmul(bank[0:cols.stop - cols.start, :], w_parts[k][:, wpart, c, cols],
                                                 xt[:, xpart, c, :], start=c == 0 and wpart == xpart,
                                                 stop=c == EG - 1 and wpart == 1)
                else:
                    if step == 9:
                        pe.wait_ge(s_ppfree, n * PP_STEPS + 5)
                    g = (step - 9) % EG
                    r = 0 if step < 11 else 32
                    i = nc.tensor.matmul(bank[:], w_up[r:r + 16, g * P:(g + 1) * P], low[r:r + 16, :], start=True, stop=True)
                if 1 in halves:
                    i.then_inc(s_ppfull, 1)

            def tail_ms(n, g):
                pe.wait_ge(s_sq, n * EG + g + 1)
                if g == 0 and not none_before(n):
                    pe.wait_ge(s_cacc, n)
                i = nc.tensor.matmul(pm[:, g, :], bm[:], sq[:, g * TILE:(g + 1) * TILE], start=True, stop=True)
                if g == EG - 1:
                    i.then_inc(s_ms, 1)

            def tail_wo(n, s):
                if s == 0:
                    pe.wait_ge(s_ogn, n * EG + EG)
                pmv = pm[:].rearrange("p c (s e) -> p (c s) e", e=E)
                for g in range(EG):
                    i = nc.tensor.matmul(pmv[:, s, :], og[:, g * TILE + s * P:g * TILE + (s + 1) * P], w_o[:, g, :],
                                         start=g == 0, stop=g == EG - 1)
                if s == SUB - 1:
                    i.then_inc(s_attn, 1)

            def tail_x2t(n, c):
                if c == 0:
                    pe.wait_ge(s_x2, n + 1)
                for s in range(SUB):
                    i = nc.tensor.transpose(pm[:, c, s * P:(s + 1) * P], x2[:, s, c * P:(c + 1) * P], ident[:])
                i.then_inc(s_x2tp, 1)

            def tail_cov(n, c, half):
                if c == 0 and half == 0:
                    pe.wait_ge(s_x2t, n + 1)
                for s in (2 * half, 2 * half + 1):
                    i = nc.tensor.matmul(pm[:, c, c * P:E + 1], x2[:, s, c * P:(c + 1) * P], x2[:, s, c * P:E + 1],
                                         start=s == 0, stop=s == SUB - 1)
                if c == EG - 1 and half == 1:
                    i.then_inc(s_cov, 1)

            def spread(n, b, u):
                if u >= 2 or not none_before(n):
                    pe.wait_ge(s_kv, n * UNITS + u - 1)
                nc.tensor.matmul(vb[u % 2][:], sel[:, u % 4, :], v_s[b][:, u % D // 4, u // D, :], start=True,
                                 stop=True).then_inc(s_vb, 1)

            def reduce(n, u):
                pe.wait_ge(s_prod, n * UNITS + u + 1)
                if u % D == 0 and not none_before(n):
                    pe.wait_ge(s_og, n * EG - 1 + u // D)
                nc.tensor.matmul(o_ps[:, u // D, :], red[:, u % D, :], prod[:, u % NPROD, :],
                                 start=u % D == 0, stop=u % D == D - 1).then_inc(s_red, 1)

            def heavy(n, b, tail, head_next, cov):
                pe.wait_ge(s_vs, n * STACKED + STACKED)
                for u in range(UNITS):
                    spread(n, b, u)
                    if u >= LAG:
                        reduce(n, u - LAG)
                    elif tail:
                        reduce(n - 1, UNITS - LAG + u)
                    if cov and u < 4:
                        tail_cov(n - 2, u // 2, u % 2)
                    if tail:
                        if u in (6, 7):
                            tail_ms(n - 1, u - 6)
                        if 13 <= u < 13 + SUB:
                            tail_wo(n - 1, u - 13)
                        if u in (25, 26):
                            tail_x2t(n - 1, u - 25)
                    if head_next:
                        if u in (4, 5):
                            head(n + 1, 1 - b, u - 4)
                        if 8 <= u < 12:
                            head(n + 1, 1 - b, 2 + (u - 8) // 2, ((u - 8) % 2,))
                        if u in (12, 17):
                            head(n + 1, 1 - b, 4, ((u - 12) // 5,))
                        if 18 <= u < 25:
                            head(n + 1, 1 - b, 5 + (u - 18) // 2, ((u - 18) % 2,))
                        if u == 27:
                            head(n + 1, 1 - b, 8, (1,))
                        if u >= 28:
                            head(n + 1, 1 - b, 9 + u - 28)

            for step in range(PP_STEPS):
                head(0, 0, step)

            def body(it, first, last):
                heavy(it * 2, 0, not first, True, not first)
                heavy(it * 2 + 1, 1, True, not last, not first)

            passes(pe, body)
            n = 2 * STEPS - 1
            for v in range(UNITS - LAG, UNITS):
                reduce(n, v)
            for c in range(EG):
                for half in range(2):
                    tail_cov(n - 1, c, half)
            for g in range(EG):
                tail_ms(n, g)
            for s in range(SUB):
                tail_wo(n, s)
            for c in range(EG):
                tail_x2t(n, c)
            for c in range(EG):
                for half in range(2):
                    tail_cov(n, c, half)


def fold(nc, fw_q, gamma, beta, keys, up, c_iota, c_iotac, cacc, stage, res):
    m_w, m_c, ones3, ident, down_t, up_s, iota, iotac, scl = res
    with ExitStack() as ctx:
        def sb(name, shape, dt=f32):
            return ctx.enter_context(nc.sbuf_tensor(name, shape, dt))

        def ps(name, shape):
            return ctx.enter_context(nc.psum_tensor(name, shape, f32))

        def sem(name):
            return ctx.enter_context(nc.semaphore(name))

        fq = sb("fq", [P, EG, QC])
        kn = sb("kn", [KEYS, FH, 2, KD])
        kt = sb("kt", [P, QG, KEYS])
        kts = sb("kts", [P, QG, KEYS])
        wt = sb("wt", [P, QG, E])
        yw = sb("yw", [P, 2, 2, E])
        gam = sb("gam", [P, QG])
        bet = sb("bet", [P, QG])
        mcol = sb("mcol", [P, EG])
        mrow = sb("mrow", [1, E])
        cc = sb("cc", [P, EG, E])
        var = sb("var", [P, QG])
        mean = sb("mean", [P, QG])
        mh = sb("mh", [P, QG])
        s_bn = sb("s_bn", [P, QG])
        cst = sb("cst", [P, QG])
        cst3 = sb("cst3", [P, QG, 3])
        mf = sb("mf", [P, EG, SIMS])
        cf = sb("cf", [3, SIMS])
        cr = sb("cr", [3, SIMS])
        c1 = sb("c1", [3, SIMS], bf16)
        c2 = sb("c2", [3, SIMS], bf16)
        c3 = sb("c3", [3, SIMS], bf16)
        io_f = sb("io_f", [P, EHI * 16])
        ioc_f = sb("ioc_f", [P, CAND * TOPK])
        mx = sb("mx", [P, 4])
        mx1 = sb("mx1", [1, 4])
        e1 = sb("e1", [1, 4], u32)
        onesr = sb("onesr", [1, P])

        bank = [ps(f"fb{i}", [P, 512]) for i in range(4)]
        ps_mx = ps("ps_mx", [P, 512])

        s_ld = sem("f_ld")
        s_pe = sem("f_pe")
        s_ev = sem("f_ev")
        s_v = sem("f_v")
        s_pw = sem("f_pw")
        s_up = sem("f_up")
        s_de = sem("f_de")
        s_dh = sem("f_dh")
        s_dl = sem("f_dl")
        s_ea = sem("f_ea")
        s_mm = sem("f_mm")
        s_mf = sem("f_mf")
        s_mx = sem("f_mx")
        s_mt = sem("f_mt")
        s_sc = sem("f_sc")
        s_bc = sem("f_bc")
        s_ds = sem("f_ds")
        s_uh = sem("f_uh")
        s_us = sem("f_us")
        s_mh = sem("f_mh")
        s_ms = sem("f_ms")
        block = ctx.enter_context(nc.Block())

        LOADS = 6
        NKEYT = QG // 8
        NWT = QG // 2
        NDT = EG * ELO // 4
        BY_ACT = NKEYT + NWT
        NUP = 4

        @block.sync
        def _(sp):
            sp.dma_start(fq[:], fw_q.rearrange("(c p) n -> p c n", p=P)).then_inc(s_ld, 16)
            sp.dma_start(kn[:], keys.rearrange("h k p d -> k h p d")).then_inc(s_ld, 16)
            sp.dma_start(gam[:], gamma.rearrange("(g p) -> p g", p=P), allow_slow_non_contiguous=True).then_inc(s_ld, 16)
            sp.dma_start(bet[:], beta.rearrange("(g p) -> p g", p=P), allow_slow_non_contiguous=True).then_inc(s_ld, 16)
            sp.dma_start(io_f[:], c_iota).then_inc(s_ld, 16)
            sp.dma_start(ioc_f[:], c_iotac).then_inc(s_ld, 16)
            sp.wait_ge(s_de, NDT)
            sp.dma_start(stage[:], up.rearrange("(p l) c -> p l c", l=ELO)).then_inc(s_up, 16)

        @block.gpsimd
        def _(pool):
            nc.gpsimd.memset(mh[:], -0.5).then_inc(s_pw, 1)
            pool.wait_ge(s_pw, 1)
            pool.wait_ge(s_v, 3)
            nc.gpsimd.tensor_tensor(s_bn[:], var[:], mh[:], ALU.pow).then_inc(s_pw, 1)

        @block.scalar
        def _(act):
            for j in range(NKEYT):
                act.wait_ge(s_pe, j + 1)
                nc.scalar.activation(kt[:, j * 8:j * 8 + 8, :].rearrange("p a b -> p (a b)"), bank[j % 2][:],
                                     ACT.Copy).then_inc(s_ea, 1)
            for j in range(NWT):
                act.wait_ge(s_pe, NKEYT + j + 1)
                nc.scalar.activation(wt[:, j * 2:j * 2 + 2, :].rearrange("p a b -> p (a b)"), bank[(NKEYT + j) % 2][:],
                                     ACT.Copy).then_inc(s_ea, 1)
            act.wait_ge(s_ds, 1)
            for j in range(NDT):
                act.wait_ge(s_de, j + 1)
                c, l4 = j % EG, j // EG
                nc.scalar.activation(down_t[:, 0, c, l4 * 4:l4 * 4 + 4, :].rearrange("p a b -> p (a b)"),
                                     bank[2 + j % 2][:], ACT.Copy, scale=scl[:, 0:1]).then_inc(s_dh, 1)
            for j in range(4):
                act.wait_ge(s_mm, j + 1)
                c, half = j % EG, j // EG
                nc.scalar.activation(mf[:, c, half * 512:(half + 1) * 512], bank[j][:], ACT.Copy).then_inc(s_mf, 1)
            act.wait_ge(s_us, 1)
            for j in range(NUP):
                if j == 1:
                    act.wait_ge(s_ms, 1)
                    nc.scalar.activation(m_w[:, 0], mf[:], ACT.Copy, scale=scl[:, 2:3]).then_inc(s_mh, 1)
                ls = slice(j * ELO // NUP, (j + 1) * ELO // NUP)
                nc.scalar.activation(up_s[:, 0, ls], stage[:, ls], ACT.Copy, scale=scl[:, 4:5]).then_inc(s_uh, 1)

        @block.tensor
        def _(pe):
            step = [0]

            def take(i):
                i.then_inc(s_pe, 1)
                step[0] += 1

            def free():
                if 2 <= step[0] < BY_ACT + 2:
                    pe.wait_ge(s_ea, step[0] - 1)
                elif step[0] >= 2:
                    pe.wait_ge(s_ev, step[0] - 1 - BY_ACT)
                return bank[step[0] % 2]

            def largest(k):
                pe.wait_ge(s_mx, k + 1)
                nc.tensor.transpose(ps_mx[0:1, 0:P], mx[:, 2:3], ident[:]).then_inc(s_mt, 1)
                pe.wait_ge(s_sc, k + 1)
                nc.tensor.matmul(ps_mx[:, 256:258], onesr[:], mx1[:, 2:4], start=True, stop=True).then_inc(s_bc, 1)

            largest(0)
            pe.wait_ge(s_ld, 16 * LOADS)
            for j in range(NKEYT):
                b = free()
                for i in range(8):
                    g = j * 8 + i
                    last = nc.tensor.transpose(b[:, i * KEYS:(i + 1) * KEYS], kn[:, g % FH, g // FH, :], ident[0:KEYS, 0:KEYS])
                take(last)
            for j in range(NWT):
                b = free()
                for i in range(4):
                    g, c = j * 2 + i // 2, i % 2
                    last = nc.tensor.transpose(b[:, i * P:(i + 1) * P], fq[:, c, g * KD:(g + 1) * KD], ident[:])
                take(last)
            for j in range(NDT):
                c, l4 = j % EG, j // EG
                if j >= 2:
                    pe.wait_ge(s_dl, j - 1)
                for i in range(4):
                    last = nc.tensor.transpose(bank[2 + j % 2][:, i * P:(i + 1) * P],
                                               stage[:, l4 * 4 + i, c * P:(c + 1) * P], ident[:])
                last.then_inc(s_de, 1)
            b = free()
            take(nc.tensor.transpose(b[:, 0:P], cacc[:, 0, P:E], ident[:]))
            pe.wait_ge(s_v, 1)
            b = free()
            for c in range(EG):
                last = nc.tensor.transpose(b[0:1, c * P:(c + 1) * P], mcol[:, c:c + 1], ident[:])
            take(last)
            pe.wait_ge(s_ev, step[0] - BY_ACT)
            b = free()
            for c in range(EG):
                last = nc.tensor.matmul(b[:, c * E:(c + 1) * E], mrow[0:1, c * P:(c + 1) * P], mrow[0:1, :],
                                        start=True, stop=True)
            take(last)
            pe.wait_ge(s_v, 2)
            for j in range(NWT):
                b = free()
                for i in range(2):
                    g = j * 2 + i
                    for c in range(EG):
                        last = nc.tensor.matmul(b[:, i * E:(i + 1) * E], fq[:, c, g * KD:(g + 1) * KD], cc[:, c, :],
                                                start=c == 0, stop=c == EG - 1)
                take(last)
            b = free()
            for g in range(QG):
                for c in range(EG):
                    last = nc.tensor.matmul(b[:, g:g + 1], fq[:, c, g * KD:(g + 1) * KD], mcol[:, c:c + 1],
                                            start=c == 0, stop=c == EG - 1)
            take(last)
            pe.wait_ge(s_v, 4)
            pe.wait_ge(s_ev, step[0] - BY_ACT)
            pe.wait_ge(s_dl, NDT)
            for j in range(4):
                c, half = j % EG, j // EG
                for i in range(8):
                    g = half * 8 + i
                    last = nc.tensor.matmul(bank[j][:, i * KEYS:(i + 1) * KEYS], wt[:, g, c * P:(c + 1) * P], kts[:, g, :],
                                            start=True, stop=True)
                last.then_inc(s_mm, 1)
            largest(1)
            for half in range(2):
                pe.wait_ge(s_mf, half + 1)
                for i in range(8):
                    g = half * 8 + i
                    last = nc.tensor.matmul(bank[half][0:3, i * KEYS:(i + 1) * KEYS], cst3[:, g, :], kt[:, g, :],
                                            start=True, stop=True)
                last.then_inc(s_mm, 1)
            largest(2)

        @block.vector
        def _(dve):
            step = [BY_ACT]

            def full():
                dve.wait_ge(s_pe, step[0] + 1)
                step[0] += 1
                return bank[(step[0] - 1) % 2]

            def magnitude(matrix):
                nc.vector.tensor_reduce(mx[:, 2:3], matrix, AX.X, ALU.max, apply_absolute_value=True).then_inc(s_mx, 1)

            def scale(k, turn):
                dve.wait_ge(s_mt, turn + 1)
                nc.vector.tensor_reduce(mx1[0:1, 0:1], ps_mx[0:1, 0:P], AX.X, ALU.max)
                dve.drain()
                nc.vector.tensor_scalar(mx1[0:1, 1:2], mx1[0:1, 0:1], SMALLEST, None, ALU.max)
                dve.drain()
                nc.vector.tensor_scalar(e1[0:1, 0:1], mx1[0:1, 1:2].bitcast(u32), 0x7F800000, None, ALU.bitwise_and)
                dve.drain()
                nc.vector.tensor_scalar(mx1[0:1, 2:3].bitcast(u32), e1[0:1, 0:1], -1.0, float((2 * 127 + 13) << 23),
                                        ALU.mult, ALU.add)
                nc.vector.tensor_scalar(mx1[0:1, 3:4].bitcast(u32), e1[0:1, 0:1], float(13 << 23), None, ALU.subtract)
                dve.drain().then_inc(s_sc, 1)
                dve.wait_ge(s_bc, turn + 1)
                return nc.vector.tensor_copy(scl[:, 2 * k:2 * k + 2], ps_mx[:, 256:258])

            nc.vector.memset(onesr[:], 1.0)
            magnitude(stage[:].rearrange("p a b -> p (a b)"))
            scale(0, 0).then_inc(s_ds, 1)
            nc.vector.tensor_scalar(mcol[:], cacc[:, :, E], 1.0 / TOKENS, None, ALU.mult).then_inc(s_v, 1)
            dve.wait_ge(s_ld, 16 * LOADS)
            nc.vector.memset(ones3[:], 1.0)
            nc.vector.tensor_copy(iota[:].rearrange("p a b -> p (a b)"), io_f[:])
            nc.vector.tensor_copy(iotac[:].rearrange("p a b -> p (a b)"), ioc_f[:])
            dve.drain()
            for j in range(NDT):
                dve.wait_ge(s_dh, j + 1)
                c, l4 = j % EG, j // EG
                nc.vector.scalar_tensor_tensor(down_t[:, 1, c, l4 * 4:l4 * 4 + 4, :].rearrange("p a b -> p (a b)"),
                                               bank[2 + j % 2][:], scl[:, 0:1],
                                               down_t[:, 0, c, l4 * 4:l4 * 4 + 4, :].rearrange("p a b -> p (a b)"),
                                               ALU.mult, ALU.subtract).then_inc(s_dl, 1)
            nc.vector.tensor_copy(cacc[:, 1, 0:P], full()[:, 0:P]).then_inc(s_ev, 1)
            nc.vector.tensor_copy(mrow[0:1, :], full()[0:1, 0:E]).then_inc(s_ev, 1)
            dve.drain()
            b = full()
            nc.vector.scalar_tensor_tensor(cc[:], cacc[:, :, 0:E], 1.0 / TOKENS,
                                           b[:, 0:EG * E].rearrange("p (c e) -> p c e", e=E),
                                           ALU.mult, ALU.subtract).then_inc(s_ev, 1)
            dve.drain().then_inc(s_v, 1)
            for j in range(NWT):
                if j == 0:
                    dve.wait_ge(s_ea, BY_ACT)
                nc.vector.tensor_tensor(yw[:, j % 2].rearrange("p a b -> p (a b)"), full()[:],
                                        wt[:, j * 2:j * 2 + 2, :].rearrange("p a b -> p (a b)"), ALU.mult).then_inc(s_ev, 1)
                dve.drain()
                nc.vector.tensor_reduce(var[:, j * 2:j * 2 + 2], yw[:, j % 2], AX.X, ALU.add)
            dve.drain()
            nc.vector.tensor_scalar(var[:], var[:], 0.0, LN_EPS, ALU.max, ALU.add).then_inc(s_v, 1)
            nc.vector.tensor_copy(mean[:], full()[:, 0:QG]).then_inc(s_ev, 1)
            dve.wait_ge(s_pw, 2)
            nc.vector.tensor_tensor(s_bn[:], s_bn[:], gam[:], ALU.mult)
            dve.drain()
            nc.vector.tensor_tensor(mean[:], mean[:], s_bn[:], ALU.mult)
            nc.vector.tensor_tensor(kts[:], kt[:], inner(s_bn[:], KEYS), ALU.mult)
            dve.drain()
            nc.vector.tensor_tensor(cst[:], bet[:], mean[:], ALU.subtract)
            dve.drain()
            nc.vector.tensor_copy(cst3[:], inner(cst[:], 3))
            dve.drain().then_inc(s_v, 1)
            dve.wait_ge(s_up, 16)
            magnitude(stage[:].rearrange("p a b -> p (a b)"))
            scale(2, 1).then_inc(s_us, 1)
            dve.wait_ge(s_mf, 4)
            magnitude(mf[:].rearrange("p a b -> p (a b)"))
            for half in range(2):
                dve.wait_ge(s_mm, 4 + half + 1)
                nc.vector.tensor_copy(cf[:, half * 512:(half + 1) * 512], bank[half][0:3, :])
            scale(1, 2).then_inc(s_ms, 1)
            dve.drain()
            nc.vector.tensor_scalar(cf[:], cf[:], scl[0:3, 2:3], XSCALE, ALU.mult, ALU.mult)
            dve.drain()
            nc.vector.tensor_copy(c1[:], cf[:])
            dve.drain()
            nc.vector.tensor_tensor(cr[:], cf[:], c1[:], ALU.subtract)
            dve.drain()
            nc.vector.tensor_copy(c2[:], cr[:])
            dve.drain()
            nc.vector.tensor_tensor(c3[:], cr[:], c2[:], ALU.subtract)
            nc.vector.tensor_scalar(m_c[:], c1[:], ident[0:3, 0:1], None, ALU.mult)
            dve.drain()
            nc.vector.scalar_tensor_tensor(m_c[:], c2[:], ident[0:3, 1:2], m_c[:], ALU.mult, ALU.add)
            dve.drain()
            nc.vector.scalar_tensor_tensor(m_c[:], c3[:], ident[0:3, 2:3], m_c[:], ALU.mult, ALU.add)
            for j in range(NUP):
                if j == 1:
                    dve.wait_ge(s_mh, 1)
                    nc.vector.scalar_tensor_tensor(m_w[:, 1], mf[:], scl[:, 2:3], m_w[:, 0], ALU.mult, ALU.subtract)
                dve.wait_ge(s_uh, j + 1)
                ls = slice(j * ELO // NUP, (j + 1) * ELO // NUP)
                nc.vector.scalar_tensor_tensor(up_s[:, 1, ls], stage[:, ls], scl[:, 4:5], up_s[:, 0, ls],
                                               ALU.mult, ALU.subtract)
            nc.vector.tensor_scalar(scl[:, 6:7], scl[:, 1:2], 1.0 / XSCALE, None, ALU.mult)
            nc.vector.tensor_scalar(scl[:, 7:8], scl[:, 3:4], 1.0 / XSCALE, None, ALU.mult)
            nc.vector.tensor_scalar(scl[:, 8:9], scl[:, 0:1], GSCALE, None, ALU.mult)
            nc.vector.scalar_tensor_tensor(scl[:, 9:10], scl[:, 1:2], 1.0 / (GSCALE * PSCALE), scl[:, 5:6], ALU.mult, ALU.mult)


def experts(nc, x1_dram, x2t_dram, out, stage, res):
    m_w, m_c, ones3, ident, down_t, up_s, iota, iotac, scl = res
    x1_v = x1_dram.rearrange("(m p) e -> p m e", p=P)
    x2t_v = x2t_dram.rearrange("m p k t -> p m k t")
    with ExitStack() as ctx:
        def sb(name, shape, dt=f32):
            return ctx.enter_context(nc.sbuf_tensor(name, shape, dt))

        def ps(name, shape):
            return ctx.enter_context(nc.psum_tensor(name, shape, f32))

        def sem(name):
            return ctx.enter_context(nc.semaphore(name))

        xt = [sb(f"ext{i}", [P, 2, EG, P], f16) for i in range(2)]
        x1 = [sb(f"ex1{i}", [P, E]) for i in range(2)]
        y = [sb(f"ey{i}", [P, E]) for i in range(2)]
        held = sb("held", [P, 1])
        s8 = sb("s8", [P, QG, TOPK])
        i8 = sb("i8", [P, QG, TOPK], u32)
        ix = sb("ix", [P, FH, TOPK])
        iy = sb("iy", [P, FH, TOPK])
        cand = sb("cand", [P, FH, CAND])
        code = sb("code", [P, FH, CAND])
        top = sb("top", [P, FH, TOPK])
        pos = sb("pos", [P, FH, TOPK], u32)
        posh = sb("posh", [P, FH, TOPK], f16)
        oh = sb("oh", [P, FH, CAND, TOPK], f16)
        ohc = sb("ohc", [P, FH, CAND, TOPK])
        ex = sb("ex", [P, FH, TOPK])
        rs = sb("rs", [P, FH])
        held_p = sb("held_p", [P, 1])
        by_elo = sb("by_elo", [P, FH * TOPK])
        pf = sb("pf", [P, FH * TOPK])
        ph = sb("ph", [P, FH * TOPK], f16)
        ecode = sb("ecode", [P, FH * TOPK])
        eh = sb("eh", [P, FH * TOPK])
        el = sb("el", [P, FH * TOPK])
        rt = sb("rt", [P, 3, P])
        rtt = sb("rtt", [P, 3, P], f16)
        uh = sb("uh", [P, EHI, P], f16)
        vl = sb("vl", [P, ELO, P], f16)
        gh = [stage[:].rearrange("p (i a) (b t) -> p i (a b) t", i=2, t=P)[:, i] for i in range(2)]
        gp = sb("gp", [P, 2, ELO, P], f16)

        ps_s = ps("ps_s", [P, SIMS])
        ps_h = [ps(f"ps_h{i}", [P, 512]) for i in range(2)]
        ps_a = [ps(f"ps_a{i}", [P, 16, ELO]) for i in range(2)]
        ps_t = ps("ps_t", [P, 512])
        ps_o = ps("ps_o", [P, 512])

        s_xt = [sem(f"e_xt{i}") for i in range(2)]
        s_x1 = [sem(f"e_x1{i}") for i in range(2)]
        s_st = sem("e_st")
        s_sim = sem("e_sim")
        s_simu = sem("e_simu")
        s_top = sem("e_top")
        s_exp = sem("e_exp")
        s_oh = sem("e_oh")
        s_ohc = sem("e_ohc")
        s_rt = sem("e_rt")
        s_tr = sem("e_tr")
        s_rtt = sem("e_rtt")
        s_v1 = sem("e_v1")
        s_vp = sem("e_vp")
        s_u1 = sem("e_u1")
        s_rs = sem("e_rs")
        s_ec = sem("e_ec")
        s_a = sem("e_a")
        s_g = sem("e_g")
        s_h = sem("e_h")
        s_gh = sem("e_gh")
        s_gp = sem("e_gp")
        s_gl = sem("e_gl")
        s_o = sem("e_o")
        s_y = sem("e_y")
        HG = ELO // 4
        AG = P // 16

        def passes(eng, body):
            body(0, True, False)
            with eng.Fori(1, SUBTILES // 2 - 1) as it:
                body(it, False, False)
            body(SUBTILES // 2 - 1, False, True)

        block = ctx.enter_context(nc.Block())

        @block.sync
        def _(sp):
            def load_xt(m, it, i, fresh):
                if not fresh:
                    sp.wait_ge(s_h, (m - 1) * HG)
                sp.dma_start(xt[i][:].rearrange("p a c t -> p (a c t)"),
                             x2t_v[:, bass.ds(m, 1), :, :].rearrange("p m k t -> p (m k t)")).then_inc(s_xt[i], 16)

            def load_x1(m, it, i, fresh):
                if not fresh:
                    sp.wait_ge(s_y, m - 1)
                sp.dma_start(x1[i][:], x1_v[:, bass.ds(m, 1), :].rearrange("p m e -> p (m e)")).then_inc(s_x1[i], 16)

            def store(m, it, i):
                sp.wait_ge(s_y, m + 1)
                sp.dma_start(out[bass.ts(m, P), :], y[i][:]).then_inc(s_st, 16)

            load_xt(0, 0, 0, True)
            load_xt(1, 0, 1, True)
            load_x1(0, 0, 0, True)
            load_x1(1, 0, 1, True)

            def body(it, first, last):
                for i in range(2):
                    m = it * 2 + i
                    if not last:
                        load_xt(m + 2, it + 1, i, False)
                    if i == 1 or not first:
                        store(m - 1, it - 1 + i, 1 - i)
                        if i == 0 or not last:
                            load_x1(m + 1, it + i, 1 - i, False)

            passes(sp, body)
            store(SUBTILES - 1, SUBTILES // 2 - 1, 1)
            sp.wait_ge(s_st, 16 * SUBTILES)

        @block.gpsimd
        def _(pool):
            def decode(m):
                pool.wait_ge(s_simu, m + 1)
                nc.gpsimd.tensor_tensor(held_p[:], by_elo[:, 0:1], by_elo[:, 0:1], ALU.mult)
                nc.gpsimd.tensor_scalar(ix[:], i8[:, 0:FH, :], float(KEYS), None, ALU.mult)
                nc.gpsimd.tensor_copy(iy[:], i8[:, FH:QG, :])
                pool.drain()
                pairs(nc.gpsimd, code, ix[:], iy[:])
                pool.drain()
                pool.wait_ge(s_oh, m + 1)
                nc.gpsimd.tensor_tensor(ohc[:], oh[:], inner(code[:], TOPK), ALU.mult).then_inc(s_ohc, 1)

            def parts(m, fresh):
                pool.wait_ge(s_rs, m + 1)
                nc.gpsimd.tensor_tensor(pf[:].rearrange("p (h k) -> p h k", k=TOPK), ex[:], inner(rs[:], TOPK), ALU.mult)
                pool.drain()
                nc.gpsimd.tensor_scalar(pf[:], pf[:], PSCALE, None, ALU.mult)
                pool.drain()
                nc.gpsimd.tensor_copy(ph[:], pf[:])
                pool.drain()
                if not fresh:
                    pool.wait_ge(s_tr, m)
                nc.gpsimd.tensor_tensor(rt[:, 2, 64:128], pf[:], ph[:], ALU.subtract)
                nc.gpsimd.tensor_copy(rt[:, 2, 0:64], ph[:])
                pool.wait_ge(s_ec, m + 1)
                nc.gpsimd.tensor_tensor(eh[:], ecode[:], by_elo[:], ALU.mult)
                pool.drain()
                nc.gpsimd.tensor_scalar(eh[:], eh[:], -(ELO - 1) / (2.0 * ELO), ROUNDER, ALU.add, ALU.add)
                pool.drain()
                nc.gpsimd.tensor_scalar(eh[:], eh[:], -ROUNDER, None, ALU.add)
                pool.drain()
                nc.gpsimd.tensor_scalar(el[:], eh[:], float(ELO), None, ALU.mult)
                pool.drain()
                for part in range(2):
                    nc.gpsimd.tensor_copy(rt[:, 0, part * 64:(part + 1) * 64], eh[:])
                    nc.gpsimd.tensor_tensor(rt[:, 1, part * 64:(part + 1) * 64], ecode[:], el[:], ALU.subtract)
                pool.drain().then_inc(s_rt, 1)

            def weigh(m):
                pool.wait_ge(s_v1, m + 1)
                nc.gpsimd.tensor_tensor(vl[:], vl[:], rtt[:, 2:3, :].broadcast_to([P, ELO, P]), ALU.mult).then_inc(s_vp, 1)

            def low(m, i):
                for j in range(AG):
                    pool.wait_ge(s_gp, m * AG + j + 1)
                    ts = slice(j * 16, (j + 1) * 16)
                    nc.gpsimd.tensor_tensor(gp[:, 1, :, ts], gh[i][:, :, ts], gp[:, 0, :, ts], ALU.subtract).then_inc(s_gl, 1)

            nc.gpsimd.memset(by_elo[:], 1.0 / ELO)
            pool.drain()
            decode(0)
            parts(0, True)
            weigh(0)
            decode(1)
            parts(1, False)

            def body(it, first, last):
                for i in range(2):
                    m = it * 2 + i
                    low(m, i)
                    if not (last and i == 1):
                        weigh(m + 1)
                    if not last:
                        decode(m + 2)
                        parts(m + 2, False)

            passes(pool, body)

        @block.scalar
        def _(act):
            def softmax_exp(m):
                act.wait_ge(s_top, m + 1)
                nc.scalar.activation(ex[:], ex[:], ACT.Exp, scale=scl[:, 7:8]).then_inc(s_exp, 1)

            def turn(m):
                act.wait_ge(s_tr, m + 1)
                nc.scalar.activation(rtt[:].rearrange("p a b -> p (a b)"), ps_t[:, 0:3 * P], ACT.Copy).then_inc(s_rtt, 1)

            def gelu(m, i, fresh, lo, hi):
                if lo == 0 and not fresh:
                    act.wait_ge(s_gl, (m - 1) * AG)
                for j in range(lo, hi):
                    act.wait_ge(s_h, m * HG + j + 1)
                    nc.scalar.activation(gh[i][:, 4 * j:4 * j + 4, :].rearrange("p a b -> p (a b)"), ps_h[j % 2][:],
                                         ACT.Gelu_apprx_tanh, scale=scl[:, 6:7]).then_inc(s_gh, 1)

            def high(m, i, fresh, lo, hi):
                if lo == 0 and not fresh:
                    act.wait_ge(s_o, m)
                for j in range(lo, hi):
                    act.wait_ge(s_g, m * AG + j + 1)
                    ts = slice(j * 16, (j + 1) * 16)
                    nc.scalar.activation(gp[:, 0, :, ts], gh[i][:, :, ts], ACT.Copy).then_inc(s_gp, 1)

            gelu(0, 0, True, 0, HG)
            softmax_exp(0)
            turn(0)
            softmax_exp(1)

            def body(it, first, last):
                for i in range(2):
                    m = it * 2 + i
                    high(m, i, first and i == 0, 0, 1)
                    if not (last and i == 1):
                        turn(m + 1)
                    high(m, i, first and i == 0, 1, AG)
                    if not (last and i == 1):
                        gelu(m + 1, 1 - i, first and i == 0, 0, EXP_AT)
                    if not last:
                        softmax_exp(m + 2)
                    if not (last and i == 1):
                        gelu(m + 1, 1 - i, first and i == 0, EXP_AT, HG)

            passes(act, body)

        @block.tensor
        def _(pe):
            def sims(m, it, i, fresh, lo, hi):
                if lo == 0:
                    pe.wait_ge(s_xt[i], it * 16 + 16)
                    if not fresh:
                        pe.wait_ge(s_simu, m)
                for step in range(lo, hi):
                    half, k = step // 7, step % 7
                    cols = slice(half * 512, (half + 1) * 512)
                    if k == 0:
                        last = nc.tensor.matmul(ps_s[:, cols], ones3[:], m_c[:, cols], start=True, stop=False)
                    else:
                        c, (xpart, wpart) = (k - 1) // 3, ((0, 0), (0, 1), (1, 0))[(k - 1) % 3]
                        last = nc.tensor.matmul(ps_s[:, cols], xt[i][:, xpart, c, :], m_w[:, wpart, c, cols], start=False,
                                                stop=k == 6)
                if hi == SIM_STEPS:
                    last.then_inc(s_sim, 1)

            def turn(m):
                pe.wait_ge(s_rt, m + 1)
                for j in range(3):
                    last = nc.tensor.transpose(ps_t[:, j * P:(j + 1) * P], rt[:, j, :], ident[:])
                last.then_inc(s_tr, 1)

            def hidden(m, i):
                for j in range(HG):
                    if not (isinstance(m, int) and m * HG + j < 2):
                        pe.wait_ge(s_gh, m * HG + j - 1)
                    for k in range(4):
                        out_k, l = ps_h[j % 2][:, k * P:(k + 1) * P], 4 * j + k
                        for c in range(EG):
                            nc.tensor.matmul(out_k, down_t[:, 0, c, l, :], xt[i][:, 0, c, :], start=c == 0, stop=False)
                            nc.tensor.matmul(out_k, down_t[:, 0, c, l, :], xt[i][:, 1, c, :], start=False, stop=False)
                            last = nc.tensor.matmul(out_k, down_t[:, 1, c, l, :], xt[i][:, 0, c, :], start=False,
                                                    stop=c == EG - 1)
                    last.then_inc(s_h, 1)

            def weights(m, lo, hi):
                if lo == 0:
                    pe.wait_ge(s_u1, m + 1)
                    pe.wait_ge(s_vp, m + 1)
                for j in range(lo, hi):
                    if not (isinstance(m, int) and m * AG + j < 2):
                        pe.wait_ge(s_g, m * AG + j - 1)
                    for t in range(16):
                        last = nc.tensor.matmul(ps_a[j % 2][:, t, :], uh[:, :, j * 16 + t], vl[:, :, j * 16 + t],
                                                start=True, stop=True)
                    last.then_inc(s_a, 1)

            def combine(m, fresh):
                pe.wait_ge(s_gl, m * AG + AG)
                if not fresh:
                    pe.wait_ge(s_y, m)
                for l in range(ELO):
                    nc.tensor.matmul(ps_o[:, 0:E], gp[:, 0, l, :], up_s[:, 0, l, :], start=l == 0, stop=False)
                    nc.tensor.matmul(ps_o[:, 0:E], gp[:, 0, l, :], up_s[:, 1, l, :], start=False, stop=False)
                    last = nc.tensor.matmul(ps_o[:, 0:E], gp[:, 1, l, :], up_s[:, 0, l, :], start=False, stop=l == ELO - 1)
                last.then_inc(s_o, 1)

            sims(0, 0, 0, True, 0, SIM_STEPS)
            hidden(0, 0)
            sims(1, 0, 1, False, 0, SIM_STEPS)
            turn(0)

            def body(it, first, last):
                for i in range(2):
                    m = it * 2 + i
                    for j in range(AG):
                        weights(m, j, j + 1)
                        if not last:
                            sims(m + 2, it + 1, i, False, j, j + 1)
                        if j == TURN_AT and not (last and i == 1):
                            turn(m + 1)
                    if not last:
                        sims(m + 2, it + 1, i, False, AG, SIM_STEPS)
                    if not (last and i == 1):
                        hidden(m + 1, 1 - i)
                    combine(m, first and i == 0)

            passes(pe, body)

        @block.vector
        def _(dve):
            def route(m, fresh):
                if not fresh:
                    dve.wait_ge(s_rt, m)
                dve.wait_ge(s_sim, m + 1)
                nc.vector.memset(held[:], 0.0)
                for g in range(QG):
                    nc.vector.max(s8[:, g, :], ps_s[:, g * KEYS:(g + 1) * KEYS])
                dve.drain()
                pairs(nc.vector, cand, s8[:, 0:FH, :], s8[:, FH:QG, :])
                for g in range(QG):
                    last = nc.vector.max_index(i8[:, g, :], s8[:, g, :], ps_s[:, g * KEYS:(g + 1) * KEYS])
                last.then_inc(s_simu, 1)
                dve.drain()
                for h in range(FH):
                    nc.vector.max(top[:, h, :], cand[:, h, :])
                dve.drain()
                nc.vector.tensor_tensor(ex[:], top[:], inner(top[:, :, 0], TOPK), ALU.subtract).then_inc(s_top, 1)
                for h in range(FH):
                    nc.vector.max_index(pos[:, h, :], top[:, h, :], cand[:, h, :])
                dve.drain()
                nc.vector.tensor_copy(posh[:], pos[:])
                dve.drain()
                nc.vector.tensor_tensor(oh[:], posh[:].rearrange("p h (o k) -> p h o k", o=1).broadcast_to([P, FH, CAND, TOPK]),
                                        iotac[:].rearrange("p (o c) k -> p o c k", o=1).broadcast_to([P, FH, CAND, TOPK]),
                                        ALU.is_equal).then_inc(s_oh, 1)
                dve.wait_ge(s_exp, m + 1)
                nc.vector.tensor_reduce(rs[:], ex[:], AX.X, ALU.add)
                dve.drain()
                nc.vector.reciprocal(rs[:], rs[:]).then_inc(s_rs, 1)

            def experts_of(m):
                dve.wait_ge(s_ohc, m + 1)
                nc.vector.tensor_reduce(ecode[:].rearrange("p (h k) -> p h k", k=TOPK), ohc[:].rearrange("p h c k -> p h k c"),
                                        AX.X, ALU.add).then_inc(s_ec, 1)

            def same(dst, row, n):
                return nc.vector.tensor_tensor(
                    dst.rearrange("p e (a b) -> p e a b", b=16),
                    rtt[:, row:row + 1, :].rearrange("p o (a b) -> p o a b", b=16).broadcast_to([P, n, P // 16, 16]),
                    iota[:, 0:n, :].rearrange("p e (o b) -> p e o b", o=1).broadcast_to([P, n, P // 16, 16]),
                    ALU.is_equal)

            def onehot_low(m, fresh):
                dve.wait_ge(s_rtt, m + 1)
                if not fresh:
                    dve.wait_ge(s_a, m * AG)
                same(vl[:], 1, ELO).then_inc(s_v1, 1)

            def onehot_high(m):
                same(uh[:], 0, EHI).then_inc(s_u1, 1)

            def gate(m, i):
                dve.wait_ge(s_gh, m * HG + HG)
                ghv = gh[i].rearrange("p l t -> p t l")
                for j in range(AG):
                    dve.wait_ge(s_a, m * AG + j + 1)
                    nc.vector.scalar_tensor_tensor(ghv[:, j * 16:(j + 1) * 16, :], ps_a[j % 2][:], scl[:, 8:9],
                                                   ghv[:, j * 16:(j + 1) * 16, :], ALU.mult, ALU.mult).then_inc(s_g, 1)

            def finish(m, it, i, fresh):
                dve.wait_ge(s_o, m + 1)
                dve.wait_ge(s_x1[i], it * 16 + 16)
                if not fresh:
                    dve.wait_ge(s_st, m * 16)
                nc.vector.scalar_tensor_tensor(y[i][:], ps_o[:, 0:E], scl[:, 9:10], x1[i][:], ALU.mult, ALU.add).then_inc(s_y, 1)

            route(0, True)
            experts_of(0)
            onehot_low(0, True)
            route(1, False)
            onehot_high(0)
            experts_of(1)

            def body(it, first, last):
                for i in range(2):
                    m = it * 2 + i
                    gate(m, i)
                    if i == 1:
                        finish(m - 1, it, 0, first)
                    elif not first:
                        finish(m - 1, it - 1, 1, False)
                    if not (last and i == 1):
                        onehot_low(m + 1, False)
                    if not last:
                        route(m + 2, False)
                    if not (last and i == 1):
                        onehot_high(m + 1)
                    if not last:
                        experts_of(m + 2)

            passes(dve, body)
            finish(SUBTILES - 1, SUBTILES // 2 - 1, 1, False)


def build(nc, x, wq, wk, wv, wo, wf1, wf2, wg1, wg2, norm_w, fw_q, gamma, beta, keys, down, up,
          c_ident, c_sel, c_red, c_bm, c_iota, c_iotac, out):
    x1_dram = nc.dram_tensor("x1_dram", (TOKENS, E), f32, kind="Internal").ap()
    x2t_dram = nc.dram_tensor("x2t_dram", (SUBTILES, P, 2 * EG, P), f16, kind="Internal").ap()
    with ExitStack() as ctx:
        cacc = ctx.enter_context(nc.sbuf_tensor("cacc", [P, EG, E + 1], f32))
        ident = ctx.enter_context(nc.sbuf_tensor("ident", [P, P], f32))
        stage = ctx.enter_context(nc.sbuf_tensor("stage", [P, ELO, E], f32))
        attention(nc, x, wq, wk, wv, wo, wf1, wf2, wg1, wg2, norm_w, c_ident, c_sel, c_red, c_bm, down, x1_dram, x2t_dram,
                  cacc, ident, stage)

        def sb(name, shape, dt=f32):
            return ctx.enter_context(nc.sbuf_tensor(name, shape, dt))

        res = (
            sb("m_w", [P, 2, EG, SIMS], f16),
            sb("m_c", [3, SIMS], bf16),
            sb("ones3", [3, P], bf16),
            ident,
            sb("down_t", [P, 2, EG, ELO, EHI], f16),
            sb("up_s", [P, 2, ELO, E], f16),
            sb("iota", [P, EHI, 16], f16),
            sb("iotac", [P, CAND, TOPK], f16),
            sb("scl", [P, 10]),
        )
        fold(nc, fw_q, gamma, beta, keys, up, c_iota, c_iotac, cacc, stage, res)
        experts(nc, x1_dram, x2t_dram, out.rearrange("b t e -> (b t) e"), stage, res)


INPUTS = ["L0_attn_x", "L0_attn_Wq", "L0_attn_Wk", "L0_attn_Wv", "L0_attn_Wo", "L0_attn_Wf1", "L0_attn_Wf2", "L0_attn_Wg1",
          "L0_attn_Wg2", "L0_attn_norm_weight", "L0_ffn_w_q", "L0_ffn_bn_gamma", "L0_ffn_bn_beta", "L0_ffn_keys",
          "L0_ffn_down_embed", "L0_ffn_up_embed"]


def constants():
    import numpy as np

    k, m = np.arange(P)[:, None, None], np.arange(P)[None, None, :]
    dv = np.arange(D)[None, :, None]
    row, i = np.arange(3 * QUAD)[:, None, None] % QUAD, np.arange(4)[None, :, None]
    sel = (row // 4 == m // D) & (row % 4 == i)
    red = (k // D == m // D) & (m % D == dv)
    bm = np.arange(P)[:, None] // D == np.arange(P)[None, :] // D
    f = np.float32
    return {
        "c_ident": np.eye(P, dtype=f),
        "c_sel": sel.reshape(3 * QUAD, -1).astype(f),
        "c_red": red.reshape(P, -1).astype(f) * f(D ** -0.5),
        "c_bm": bm.astype(f) * f(1.0 / D),
        "c_iota": np.tile(np.repeat(np.arange(EHI), 16), (P, 1)).astype(f),
        "c_iotac": np.tile(np.repeat(np.arange(CAND), TOPK), (P, 1)).astype(f),
    }


def kernel(**inputs):
    import numpy as np
    import concourse.bacc as bacc
    from concourse.bass_utils import run_bass_kernel_spmd

    nc = bacc.Bacc("TRN2", target_bir_lowering=False, num_devices=1)
    arrays = {f"in_{n}": np.ascontiguousarray(inputs[n]) for n in INPUTS} | constants()
    wv = arrays["in_L0_attn_Wv"].reshape(E, EG, HEADS // EG, 4, 4).transpose(0, 1, 3, 2, 4)
    arrays["in_L0_attn_Wv"] = np.ascontiguousarray(wv.reshape(E, E))
    args = [nc.dram_tensor(n, a.shape, mybir.dt.from_np(a.dtype), kind="ExternalInput").ap() for n, a in arrays.items()]
    args.append(nc.dram_tensor("out_x", (BATCH, SEQ, E), f32, kind="ExternalOutput").ap())
    build(nc, *args)
    r = run_bass_kernel_spmd(nc, [arrays], core_ids=[0])
    return r.results[0]["out_x"]
```
